# Optimizing a Trainium2 kernel written in Bass

```python
import numpy as np
import jax
import jax.numpy as jnp

def _softmax(x, axis=-1):
    return jax.nn.softmax(x, axis=axis)

def _gelu(x):
    return jax.nn.gelu(x, approximate=True)

def _silu(x):
    return jax.nn.silu(x)

def _sigmoid(x):
    return jax.nn.sigmoid(x)

def _layernorm(x, axis=-1, eps=1e-05):
    m = jnp.mean(x, axis=axis, keepdims=True)
    v = jnp.var(x, axis=axis, keepdims=True)
    return (x - m) / jnp.sqrt(v + eps)

def _scatter_add(tgt, idx, src, axis=0):
    return tgt.at[idx].add(src)

def _segment_sum(src, seg, n):
    return jax.ops.segment_sum(src, seg, n)
kernel_name = 'mk_gps_d1_gnn_r8_3eda02'

def setup_inputs(seed: int=0):
    np.random.seed(seed)
    _w = jnp.asarray

    def _rec_inputs():
        import jax
        import jax.numpy as jnp
        _gk = jax.random.key(seed)
        x = -0.0003713 + 1 * jax.random.normal(jax.random.fold_in(_gk, 1), (6250, 256), jnp.float32)
        src = jax.random.randint(jax.random.fold_in(_gk, 2), (200000,), 0, 6250, jnp.int32)
        dst = jax.random.randint(jax.random.fold_in(_gk, 3), (200000,), 0, 6250, jnp.int32)
        _o = jnp.argsort(dst, stable=True)
        src = src[_o]
        dst = dst[_o]
        return (x, src, dst)
    x, src, dst = _rec_inputs()

    def _L0_gnn_setup():
        import jax, jax.numpy as jnp
        import numpy as np
        N = 6250
        E = 100000
        H = 8
        C = 32
        HS = H * C
        NEG_SLOPE = 0.2
        EPS = 1e-16
        key = jax.random.key(seed)
        ks = jax.random.split(key, 6)
        x = jax.random.normal(ks[0], (N, HS), dtype=jnp.float32)
        edge_index = jax.random.randint(ks[1], (2, E), 0, N, dtype=jnp.int64)
        W = jax.random.normal(ks[2], (HS, HS), dtype=jnp.float32) * (1.0 / np.sqrt(HS))
        att_src = jax.random.normal(ks[3], (H, C), dtype=jnp.float32) * (1.0 / np.sqrt(C))
        att_dst = jax.random.normal(ks[4], (H, C), dtype=jnp.float32) * (1.0 / np.sqrt(C))
        bias = jax.random.normal(ks[5], (HS,), dtype=jnp.float32) * 0.02
        return {'x': x, 'edge_index': edge_index, 'W': W, 'att_src': att_src, 'att_dst': att_dst, 'bias': bias}
    _L0_gnn_all = _L0_gnn_setup()
    _L0_gnn_in = {k: v for k, v in _L0_gnn_all.items() if k in ('W', 'att_src', 'att_dst', 'bias')}
    del _L0_gnn_all

    def _L0_mix_setup():
        import jax, jax.numpy as jnp
        import numpy as np
        A, Bc, Cc = (0.5, 1.0, 1.0)
        H = 8
        EPS = 1e-12

        def _normalize(t):
            n = jnp.linalg.norm(t, axis=-1, keepdims=True)
            return t / jnp.maximum(n, EPS)
        key = jax.random.key(seed)
        ks = jax.random.split(key, 5)
        B, N, C = (8, 256, 256)
        D = C // H
        x = jax.random.normal(ks[0], (B, N, C), dtype=jnp.float32)
        Wqkv = jax.random.normal(ks[1], (3 * H * D, C), dtype=jnp.float32) * 0.02
        bqkv = jnp.zeros((3 * H * D,), dtype=jnp.float32)
        Wproj = jax.random.normal(ks[2], (C, H * D), dtype=jnp.float32) * 0.02
        bproj = jnp.zeros((C,), dtype=jnp.float32)
        temperature = jnp.ones((1, H, 1, 1), dtype=jnp.float32)
        return {'x': x, 'Wqkv': Wqkv, 'bqkv': bqkv, 'Wproj': Wproj, 'bproj': bproj, 'temperature': temperature}
    _L0_mix_all = _L0_mix_setup()
    _L0_mix_in = {k: v for k, v in _L0_mix_all.items() if k in ('Wqkv', 'bqkv', 'Wproj', 'bproj', 'temperature')}
    del _L0_mix_all

    def _L0_ffn_setup():
        import jax, jax.numpy as jnp
        import numpy as np
        B, S, H, F, E, K = (8, 512, 256, 512, 16, 2)
        EPS = 1e-05
        key = jax.random.key(seed)
        ks = jax.random.split(key, 9)
        sc = 0.02
        return {'x': jax.random.normal(ks[0], (B, S, H), dtype=jnp.float32), 'gate_w': jax.random.normal(ks[1], (H, E), dtype=jnp.float32) * sc, 'gate_b': jnp.zeros((E,), dtype=jnp.float32), 'w1': jax.random.normal(ks[2], (E, H, F), dtype=jnp.float32) * sc, 'b1': jnp.zeros((E, F), dtype=jnp.float32), 'w2': jax.random.normal(ks[3], (E, F, H), dtype=jnp.float32) * sc, 'b2': jnp.zeros((E, H), dtype=jnp.float32), 'gamma': jnp.ones((H,), dtype=jnp.float32), 'beta': jnp.zeros((H,), dtype=jnp.float32)}
    _L0_ffn_all = _L0_ffn_setup()
    _L0_ffn_in = {k: v for k, v in _L0_ffn_all.items() if k in ('gate_w', 'gate_b', 'w1', 'b1', 'w2', 'b2', 'gamma', 'beta')}
    del _L0_ffn_all
    return {'x': x, 'src': src, 'dst': dst, 'L0_gnn_W': _L0_gnn_in['W'], 'L0_gnn_att_src': _L0_gnn_in['att_src'], 'L0_gnn_att_dst': _L0_gnn_in['att_dst'], 'L0_gnn_bias': _L0_gnn_in['bias'], 'L0_mix_Wqkv': _L0_mix_in['Wqkv'], 'L0_mix_bqkv': _L0_mix_in['bqkv'], 'L0_mix_Wproj': _L0_mix_in['Wproj'], 'L0_mix_bproj': _L0_mix_in['bproj'], 'L0_mix_temperature': _L0_mix_in['temperature'], 'L0_ffn_gate_w': _L0_ffn_in['gate_w'], 'L0_ffn_gate_b': _L0_ffn_in['gate_b'], 'L0_ffn_w1': _L0_ffn_in['w1'], 'L0_ffn_b1': _L0_ffn_in['b1'], 'L0_ffn_w2': _L0_ffn_in['w2'], 'L0_ffn_b2': _L0_ffn_in['b2'], 'L0_ffn_gamma': _L0_ffn_in['gamma'], 'L0_ffn_beta': _L0_ffn_in['beta']}

def reference(x, src, dst, L0_gnn_W, L0_gnn_att_src, L0_gnn_att_dst, L0_gnn_bias, L0_mix_Wqkv, L0_mix_bqkv, L0_mix_Wproj, L0_mix_bproj, L0_mix_temperature, L0_ffn_gate_w, L0_ffn_gate_b, L0_ffn_w1, L0_ffn_b1, L0_ffn_w2, L0_ffn_b2, L0_ffn_gamma, L0_ffn_beta):
    import jax
    import jax.numpy as jnp

    def _L0_gnn_ref(x, edge_index, W, att_src, att_dst, bias):
        import jax, jax.numpy as jnp
        import numpy as np
        N = 6250
        E = 100000
        H = 8
        C = 32
        HS = H * C
        NEG_SLOPE = 0.2
        EPS = 1e-16
        src, dst = (edge_index[0], edge_index[1])
        xw = (x @ W).reshape(N, H, C)
        a_src = jnp.einsum('nhc,hc->nh', xw, att_src)
        a_dst = jnp.einsum('nhc,hc->nh', xw, att_dst)
        e = a_src[src] + a_dst[dst]
        e = jax.nn.leaky_relu(e, NEG_SLOPE)
        m = jax.ops.segment_max(e, dst, num_segments=N)
        m = jnp.where(jnp.isfinite(m), m, 0.0)
        ex = jnp.exp(e - m[dst])
        denom = jax.ops.segment_sum(ex, dst, num_segments=N)
        alpha = ex / (denom[dst] + EPS)
        msg = xw[src] * alpha[:, :, None]
        out = jax.ops.segment_sum(msg, dst, num_segments=N)
        out = out.reshape(N, HS) + bias
        return jax.nn.relu(out)

    def _L0_mix_ref(x, Wqkv, bqkv, Wproj, bproj, temperature):
        import jax, jax.numpy as jnp
        import numpy as np
        A, Bc, Cc = (0.5, 1.0, 1.0)
        H = 8
        EPS = 1e-12

        def _normalize(t):
            n = jnp.linalg.norm(t, axis=-1, keepdims=True)
            return t / jnp.maximum(n, EPS)
        B, N, C = x.shape
        D = C // H
        scale = float(D) ** 0.25
        qkv = (x @ Wqkv.T + bqkv).reshape(B, N, 3, H, D)
        qkv = jnp.transpose(qkv, (2, 0, 3, 1, 4))
        q, k, v = (qkv[0], qkv[1], qkv[2])
        q = q * scale
        v1 = jnp.concatenate([jnp.ones((B, H, N, 1), dtype=v.dtype), v], axis=-1)
        qn = _normalize(q) * (scale * temperature)
        kn = _normalize(k) * scale
        vN = v1 / N
        kv_mod = jnp.einsum('bhni,bhnj,bhne->bhije', kn, kn, vN)
        kv = jnp.einsum('bhnd,bhne->bhde', kn, vN)
        vsum = jnp.sum(vN, axis=-2)[:, :, None, :]
        y = A * jnp.einsum('bhni,bhnj,bhije->bhne', qn, qn, kv_mod) + scale ** 2 * Bc * jnp.einsum('bhnd,bhde->bhne', qn, kv) + scale ** 4 * Cc * vsum
        y_norm, y = (y[..., :1], y[..., 1:])
        y = y / y_norm
        out = jnp.transpose(y, (0, 2, 1, 3)).reshape(B, N, H * D)
        return out @ Wproj.T + bproj

    def _L0_ffn_ref(x, gate_w, gate_b, w1, b1, w2, b2, gamma, beta):
        import jax, jax.numpy as jnp
        import numpy as np
        B, S, H, F, E, K = (8, 512, 256, 512, 16, 2)
        EPS = 1e-05
        gate_logits = x @ gate_w + gate_b
        topk_vals, topk_idx = jax.lax.top_k(gate_logits, K)
        topk_w = jax.nn.softmax(topk_vals, axis=-1)
        h = jax.nn.relu(jnp.einsum('bsh,ehf->bsef', x, w1) + b1)
        expert_out = jnp.einsum('bsef,efh->bseh', h, w2) + b2
        sel = jnp.take_along_axis(expert_out, topk_idx[:, :, :, None], axis=2)
        moe = jnp.sum(topk_w[..., None] * sel, axis=2)
        y = x + moe
        mu = jnp.mean(y, axis=-1, keepdims=True)
        var = jnp.var(y, axis=-1, keepdims=True)
        return (y - mu) / jnp.sqrt(var + EPS) * gamma + beta
    edge_index = jnp.stack([src, dst])
    xn = _layernorm(x, axis=-1)
    x = x + _L0_gnn_ref(xn, edge_index, L0_gnn_W, L0_gnn_att_src, L0_gnn_att_dst, L0_gnn_bias) + _L0_mix_ref(xn[None], L0_mix_Wqkv, L0_mix_bqkv, L0_mix_Wproj, L0_mix_bproj, L0_mix_temperature)[0]
    x = x + _L0_ffn_ref(_layernorm(x, axis=-1)[None], L0_ffn_gate_w, L0_ffn_gate_b, L0_ffn_w1, L0_ffn_b1, L0_ffn_w2, L0_ffn_b2, L0_ffn_gamma, L0_ffn_beta)[0]
    return x

_drawn_inputs = setup_inputs


def setup_inputs(seed=0):
    import zlib

    import numpy as np

    out = dict(_drawn_inputs(seed))
    spreads = {'L0_mix_bqkv': (0.0, 0.1),
     'L0_mix_bproj': (0.0, 0.1),
     'L0_mix_temperature': (1.0, 0.6),
     'L0_ffn_gate_b': (0.0, 0.1),
     'L0_ffn_b1': (0.0, 0.714),
     'L0_ffn_b2': (0.0, 0.1),
     'L0_ffn_gamma': (1.0, 0.2),
     'L0_ffn_beta': (0.0, 0.1)}
    factors = {'L0_gnn_bias': 3.544, 'L0_mix_Wqkv': 22.76}
    for name, (base, spread) in spreads.items():
        noise = np.random.default_rng([zlib.crc32(name.encode()), seed]).standard_normal(out[name].shape)
        drawn = base * np.exp(spread * noise) if base else spread * noise
        out[name] = jnp.asarray(drawn.astype(out[name].dtype))
    for name, factor in factors.items():
        out[name] = (out[name] * factor).astype(out[name].dtype)
    return out
```

```python
from contextlib import ExitStack

import concourse.bass as bass
from concourse import mybir

F32 = mybir.dt.float32
I32 = mybir.dt.int32
U32 = mybir.dt.uint32
ALU = mybir.AluOpType
ACT = mybir.ActivationFunctionType
AXX = mybir.AxisListType.X
RMAX = bass.bass_isa.ReduceOp.max

P = 128
N = 6250
E = 200000
D = 256
H = 8
C = D // H
T = 50
NFULL = N // P
NREST = N - NFULL * P
BLOCKS = -(-N // P)
TILES_PER_CHUNK = 4
CHUNK = TILES_PER_CHUNK * P
CHUNKS = -(-E // CHUNK)
STEPS = CHUNKS + BLOCKS
ROW = D + H
V1 = C + 1
DIAGS = C // 2 + 1
FEAT = 2 * (DIAGS + 1) * C
FCH = FEAT // P
NEXP, FF = 16, 512
SLOT_TILES = 114
LN_EPS = 1e-5
NORM_EPS = 1e-12
TINY = 1e-37
A_COEF, B_COEF, C_COEF = 0.5, 1.0, 1.0
SCALE = float(C) ** 0.25
SLOPE = 0.2
PAD_DST = 1 << 20
assert STEPS % 2 == 0


def wait(eng, sem, value):
    if isinstance(value, int) and value <= 0:
        return
    eng.wait_ge(sem, value)


def pairs(eng, count, body):
    body(0, 0)
    body(1, 1)
    with eng.Fori(1, count // 2) as i:
        body(i * 2, 0)
        body(i * 2 + 1, 1)


def moments(dve, mv, st):
    m, v = mv[:, :, 0], mv[:, :, 1]
    dve.tensor_tensor(m, st[:, :, 1], st[:, :, 4], ALU.subtract)
    dve.tensor_tensor(st[:, :, 0], st[:, :, 2], st[:, :, 5], ALU.add)
    dve.drain()
    dve.tensor_tensor(v, m, m, ALU.mult)
    dve.drain()
    dve.tensor_scalar(v, v, 0.25, None, ALU.mult)
    dve.tensor_tensor(m, st[:, :, 1], st[:, :, 4], ALU.add)
    dve.drain()
    dve.scalar_tensor_tensor(out=v, in0=st[:, :, 0], scalar=1.0 / D, in1=v, op0=ALU.mult, op1=ALU.add)
    dve.tensor_scalar(m, m, 0.5, None, ALU.mult)
    dve.drain()


def bcast_rows(ap, n):
    return ap.unsqueeze(0).broadcast_to([P, n])


def gps_layer(nc, x, src, dst, gnn_W, att_src, att_dst, gnn_bias, Wqkv, bqkv, Wproj, bproj, temperature,
              gate_w, gate_b, w1, b1, w2, b2, gamma, beta, out):
    top = ExitStack()

    def sb(name, shape, dt=F32, ctx=None):
        return (ctx or top).enter_context(nc.sbuf_tensor(name, shape, dt))

    def ps(name, shape, ctx):
        return ctx.enter_context(nc.psum_tensor(name, shape, F32))

    def sem(name, ctx=None):
        return (ctx or top).enter_context(nc.semaphore(name))

    with top:
        node_rows = nc.dram_tensor("node_rows", (T * P, ROW), F32).ap()
        qn_dram = nc.dram_tensor("qn_dram", (T * P, D), F32).ap()
        src_pad = nc.dram_tensor("src_pad", (CHUNKS, CHUNK), I32).ap()
        dst_pad = nc.dram_tensor("dst_pad", (CHUNKS, CHUNK), I32).ap()
        slot_x = nc.dram_tensor("slot_x", (SLOT_TILES * P, D), F32).ap()
        slot_y = nc.dram_tensor("slot_y", (SLOT_TILES * P, D), F32).ap()
        b1_cols = nc.dram_tensor("b1_cols", (NEXP, P, FF // P), F32).ap()

        resid = sb("resid", [P, T, D])
        ident = sb("ident", [P, P])
        iota_row = sb("iota_row", [P, P])
        iota_col = sb("iota_col", [P, 1])
        ones = sb("ones", [P, P])
        valid = sb("valid", [P, T])
        adm = sb("adm", [P, T, 2 * H])
        loc_wide = sb("loc_wide", [P, 2 * D + 8])

        early = ExitStack()
        w_cat = sb("w_cat", [P, 2, 2 * D + 2 * D + 2 * H], ctx=early)
        wp_t = sb("wp_t", [P, 2, D], ctx=early)
        b_qkv = sb("b_qkv", [P, 3 * D], ctx=early)
        b_proj = sb("b_proj", [P, D], ctx=early)
        b_gnn = sb("b_gnn", [P, D], ctx=early)
        ss_scale = sb("ss_scale", [P, 2 * H], ctx=early)
        nrm_scale = sb("nrm_scale", [P, 2 * H], ctx=early)
        mv = sb("mv", [P, T, 2], ctx=early)
        rstd = sb("rstd", [P, T], ctx=early)
        nmr = sb("nmr", [P, T], ctx=early)
        a_s = sb("a_s", [P, T, H], ctx=early)
        mix_w = sb("mix_w", [P, 4, 8 * V1 + 2 * V1], ctx=early)
        vsum_w = sb("vsum_w", [1, H * V1], ctx=early)
        W_Q = D + 2 * H

        with ExitStack() as c:
            raw = sb("raw", [P, 6, D], ctx=c)
            raw_w = sb("raw_w", [P, 2, D], ctx=c)
            raw_p = sb("raw_p", [P, 2, D], ctx=c)
            gw_t = sb("gw_t", [P, 2, D], ctx=c)
            att_bd = sb("att_bd", [P, 2, 2 * H], ctx=c)
            zrow = sb("zrow", [P, D], ctx=c)
            temp_b = sb("temp_b", [P, H], ctx=c)
            pad_i = sb("pad_i", [P, CHUNKS * CHUNK - E], I32, ctx=c)
            pad_s = sb("pad_s", [P, CHUNKS * CHUNK - E], I32, ctx=c)
            iota_i = sb("iota_i", [P, P], I32, ctx=c)
            iota_ci = sb("iota_ci", [P, 1], I32, ctx=c)
            b1_raw = sb("b1_raw", [NEXP * FF // P, P], ctx=c)
            b1_t = sb("b1_t", [P, NEXP * FF // P], ctx=c)
            st6 = sb("st6", [P, T, 6], ctx=c)
            pt = [ps(f"s1_pt{i}", [P, 512], c) for i in range(2)]
            pw = ps("s1_pw", [P, 512], c)
            x_zeroed = sem("x_zeroed", c)
            x_in = sem("x_in", c)
            x_rest_in = sem("x_rest_in", c)
            w_in = sem("w_in", c)
            b_in = sem("b_in", c)
            att_zeroed = sem("att_zeroed", c)
            att_in = sem("att_in", c)
            pads_set = sem("pads_set", c)
            scratch_out = sem("scratch_out", c)
            ident_ready = sem("ident_ready", c)
            turned = sem("turned", c)
            copied = sem("copied", c)
            b1_out = sem("b1_out", c)
            watt_ready = sem("watt_ready", c)
            iotas = sem("iotas", c)
            var_ready = sem("var_ready", c)
            std_ready = sem("std_ready", c)
            block = c.enter_context(nc.Block())

            turns = []
            for kc in range(2):
                for m in range(6):
                    turns.append((raw[:, m, kc * P:(kc + 1) * P],
                                  w_cat[:, kc, W_Q + m * P:W_Q + (m + 1) * P]))
                for m in range(2):
                    turns.append((raw_p[:, m, kc * P:(kc + 1) * P], wp_t[:, kc, m * P:(m + 1) * P]))
                    turns.append((raw_w[:, m, kc * P:(kc + 1) * P], gw_t[:, kc, m * P:(m + 1) * P]))

            @block.sync
            def _(sp):
                sp.wait_ge(x_zeroed, 1)
                for q in range(4):
                    n = NFULL // 4
                    sp.dma_start(resid[:, q * n:(q + 1) * n, :],
                                 x[q * n * P:(q + 1) * n * P, :].rearrange("(t p) f -> p t f", p=P)).then_inc(x_in, 16)
                sp.dma_start(resid[0:NREST, NFULL, :], x[NFULL * P:N, :]).then_inc(x_rest_in, 16)
                sp.dma_start(raw[:], Wqkv.rearrange("(m p) k -> p m k", p=P)).then_inc(w_in, 16)
                sp.dma_start(raw_w[:], gnn_W.rearrange("(m p) k -> p m k", p=P)).then_inc(w_in, 16)
                sp.dma_start(raw_p[:], Wproj.rearrange("(m p) k -> p m k", p=P)).then_inc(w_in, 16)
                sp.dma_start(b1_raw[:], b1.rearrange("e (c p) -> (e c) p", p=P)).then_inc(w_in, 16)
                sp.dma_start(w_cat[:, :, 0:D], gnn_W.rearrange("(c k) n -> k c n", k=P)).then_inc(w_in, 16)
                sp.wait_ge(att_zeroed, 1)
                for h in range(H):
                    p0 = (h % 4) * C
                    for k, a in enumerate((att_src, att_dst)):
                        sp.dma_start(att_bd[p0:p0 + C, h // 4, k * H + h:k * H + h + 1],
                                     a[h:h + 1, :].rearrange("a c -> c a")).then_inc(att_in, 16)
                sp.wait_ge(pads_set, 3)
                full = E // CHUNK
                rest = E - full * CHUNK
                for lst, pad, pads in ((src, src_pad, pad_s), (dst, dst_pad, pad_i)):
                    sp.dma_start(pad[0:full, :], lst[0:full * CHUNK].rearrange("(a b) -> a b", b=CHUNK)).then_inc(scratch_out, 16)
                    sp.dma_start(pad[full:full + 1, 0:rest], lst[full * CHUNK:E].unsqueeze(0)).then_inc(scratch_out, 16)
                    sp.dma_start(pad[full:full + 1, rest:CHUNK], pads[0:1, :]).then_inc(scratch_out, 16)
                sp.dma_start(slot_x.rearrange("(t p) f -> p t f", p=P),
                             zrow[:].unsqueeze(1).broadcast_to([P, SLOT_TILES, D])).then_inc(scratch_out, 16)
                sp.wait_ge(scratch_out, 7 * 16)
                sp.wait_ge(copied, len(turns) + 1)
                sp.dma_start(b1_cols.rearrange("e p c -> p e c"), b1_t[:].rearrange("p (e c) -> p e c", e=NEXP)).then_inc(b1_out, 16)
                sp.wait_ge(b1_out, 16)

            @block.gpsimd
            def _(pool):
                pool.memset(ident[:], 0.0)
                pool.memset(ones[:], 1.0)
                pool.memset(valid[:], 1.0)
                pool.iota(iota_i[:], [[1, P]], base=0, channel_multiplier=0)
                pool.iota(iota_ci[:], [[1, 1]], base=0, channel_multiplier=1).then_inc(iotas, 1)
                pool.drain()
                pool.affine_select(out=ident[:], in_=ident[:], compare_op=ALU.not_equal, fill=1.0, base=0,
                                   pattern=[[-1, P]], channel_multiplier=1).then_inc(ident_ready, 1)
                pool.affine_select(out=valid[:], in_=valid[:], compare_op=ALU.is_ge, fill=0.0, base=N - 1,
                                   pattern=[[-P, T]], channel_multiplier=-1)
                for ap, vec, n in ((b_qkv, bqkv, 3 * D), (b_proj, bproj, D), (b_gnn, gnn_bias, D)):
                    pool.dma_start(ap[:], bcast_rows(vec, n)).then_inc(b_in, 16)
                pool.dma_start(temp_b[:], bcast_rows(temperature.rearrange("a h b c -> (a h b c)"), H)).then_inc(b_in, 16)

            @block.vector
            def _(dve):
                dve.memset(resid[:, NFULL:T, :], 0.0).then_inc(x_zeroed, 1)
                dve.memset(att_bd[:], 0.0).then_inc(att_zeroed, 1)
                dve.memset(pad_s[:], 0).then_inc(pads_set, 1)
                dve.memset(pad_i[:], PAD_DST).then_inc(pads_set, 1)
                dve.memset(zrow[:], 0.0).then_inc(pads_set, 1)
                dve.memset(ss_scale[:, 0:H], SCALE * SCALE)
                dve.memset(ss_scale[:, H:2 * H], 1.0)
                dve.memset(nrm_scale[:, H:2 * H], SCALE)
                dve.wait_ge(iotas, 1)
                dve.tensor_copy(iota_row[:], iota_i[:])
                dve.tensor_copy(iota_col[:], iota_ci[:])
                dve.wait_ge(b_in, 4 * 16)
                dve.tensor_scalar(nrm_scale[:, 0:H], temp_b[:], SCALE * SCALE, None, ALU.mult)
                dve.wait_ge(x_in, 64)
                dve.wait_ge(x_rest_in, 16)
                with dve.Fori(0, T) as t:
                    dve.bn_stats(st6[:, bass.ds(t, 1), :], resid[:, bass.ds(t, 1), :])
                dve.drain()
                moments(dve, mv, st6)
                dve.tensor_scalar(rstd[:], mv[:, :, 1], LN_EPS, None, ALU.add).then_inc(var_ready, 1)
                dve.wait_ge(std_ready, 1)
                dve.reciprocal(rstd[:], rstd[:])
                dve.drain()
                dve.scalar_tensor_tensor(out=nmr[:], in0=mv[:, :, 0], scalar=-1.0, in1=rstd[:], op0=ALU.mult, op1=ALU.mult)

            @block.tensor
            def _(pe):
                pe.wait_ge(ident_ready, 1)
                pe.wait_ge(w_in, 5 * 16)
                for n, (a, _) in enumerate(turns):
                    if n >= 2:
                        pe.wait_ge(copied, n - 1)
                    pe.transpose(pt[n % 2][:, 0:P], a, ident[:]).then_inc(turned, 1)
                n = len(turns)
                pe.wait_ge(copied, n - 1)
                pe.transpose(pt[n % 2][:, 0:NEXP * FF // P], b1_raw[:], ident[0:NEXP * FF // P, 0:NEXP * FF // P]).then_inc(turned, 1)
                pe.wait_ge(copied, n)
                pe.wait_ge(att_in, 2 * H * 16)
                for m in range(2):
                    for kc in range(2):
                        mm = pe.matmul(pw[:, m * 2 * H:(m + 1) * 2 * H], gw_t[:, kc, m * P:(m + 1) * P], att_bd[:, kc, :],
                                       start=(kc == 0), stop=(kc == 1))
                mm.then_inc(watt_ready, 1)

            @block.scalar
            def _(act):
                for n, (_, b) in enumerate(turns):
                    act.wait_ge(turned, n + 1)
                    act.copy(b, pt[n % 2][:, 0:P]).then_inc(copied, 1)
                n = len(turns)
                act.wait_ge(turned, n + 1)
                act.copy(b1_t[:], pt[n % 2][:, 0:NEXP * FF // P]).then_inc(copied, 1)
                act.wait_ge(var_ready, 1)
                act.sqrt(rstd[:], rstd[:]).then_inc(std_ready, 1)
                act.wait_ge(watt_ready, 1)
                act.copy(w_cat[:, :, D:D + 2 * H], pw[:, 0:4 * H].rearrange("p (m a) -> p m a", m=2))

        def products(dve, feat, dbl, g, done):
            base = dbl[:, 2 * g, 0:1]
            whole = [base.ap[0][0], P]
            nd = DIAGS - 1
            dve.tensor_tensor(
                feat[:, 0:2 * nd * C].rearrange("p (h d i) -> p h d i", h=2, d=nd),
                bass.AP(base.tensor, base.offset, [whole, [2 * C, 2], [0, nd], [1, C]]),
                bass.AP(base.tensor, base.offset, [whole, [2 * C, 2], [1, nd], [1, C]]), ALU.mult)
            tail = feat[:, 2 * nd * C:FEAT].rearrange("p (h a i) -> p h a i", h=2, a=2)
            dve.tensor_tensor(tail[:, :, 0, :], dbl[:, 2 * g:2 * g + 2, 0:C], dbl[:, 2 * g:2 * g + 2, nd:nd + C], ALU.mult)
            dve.tensor_copy(tail[:, :, 1, :], dbl[:, 2 * g:2 * g + 2, 0:C]).then_inc(done, 1)

        with ExitStack() as c:
            xn = [sb(f"xn{i}", [P, D], ctx=c) for i in range(2)]
            xt = [sb(f"xt{i}", [P, 2, P], ctx=c) for i in range(2)]
            row = [sb(f"row{i}", [P, ROW], ctx=c) for i in range(2)]
            qk = sb("qk", [P, 2 * D], ctx=c)
            sq = sb("sq", [P, 2 * D], ctx=c)
            nrm = sb("nrm", [P, 2 * H], ctx=c)
            vtmp = sb("vtmp", [P, D], ctx=c)
            v1 = [sb(f"v1{i}", [P, H, V1], ctx=c) for i in range(2)]
            qst = [sb(f"qst{i}", [P, D], ctx=c) for i in range(2)]
            kk = sb("kk", [P, H, 2 * C], ctx=c)
            feat = [sb(f"kfeat{i}", [P, FEAT], ctx=c) for i in range(2)]
            zeros = sb("zeros", [P, 512], ctx=c)
            vmask = sb("vmask", [P, T], ctx=c)
            p_t = ps("p_t", [P, 512], c)
            p_row = ps("p_row", [P, 512], c)
            p_qk = ps("p_qk", [P, 512], c)
            p_v = ps("p_v", [P, 512], c)
            p_kv = [ps(f"p_kv{i}", [P, 512], c) for i in range(3)]
            p_vsum = ps("p_vsum", [P, 512], c)
            zeroed = sem("zeroed", c)
            xn_ready = sem("xn_ready", c)
            xt_in_psum = sem("xt_in_psum", c)
            xt_ready = sem("xt_ready", c)
            projected = sem("projected", c)
            row_ready = sem("row_ready", c)
            qkv_taken = sem("qkv_taken", c)
            v1_ready = sem("v1_ready", c)
            squares_ready = sem("squares_ready", c)
            norms_ready = sem("norms_ready", c)
            q_ready = sem("q_ready", c)
            feat_ready = sem("feat_ready", c)
            feat_used = sem("feat_used", c)
            row_out = [sem(f"row_out{i}", c) for i in range(2)]
            q_out = [sem(f"q_out{i}", c) for i in range(2)]
            block = c.enter_context(nc.Block())

            def kv_place(g, m):
                if m < 8:
                    at = g * 8 + m
                    return p_kv[at // 15][:, (at % 15) * V1:(at % 15 + 1) * V1]
                return p_kv[2][:, 2 * V1 + g * 2 * V1:2 * V1 + (g + 1) * 2 * V1]

            @block.scalar
            def _(act):
                def take_row(t, s):
                    act.wait_ge(projected, t + 1)
                    wait(act, row_out[s], (t - s) * 8)
                    act.copy(row[s][:], p_row[:, 0:ROW])
                    act.copy(a_s[:, bass.ds(t, 1), :], p_row[:, D:D + H].unsqueeze(1))
                    act.copy(adm[:, bass.ds(t, 1), 0:H], p_row[:, ROW:ROW + H].unsqueeze(1)).then_inc(row_ready, 1)

                def body(t, s):
                    wait(act, xt_in_psum, t - 1)
                    act.activation(xn[s][:], resid[:, bass.ds(t, 1), :].rearrange("p a f -> p (a f)"), ACT.Identity,
                                   bias=nmr[:, bass.ds(t, 1)], scale=rstd[:, bass.ds(t, 1)]).then_inc(xn_ready, 1)
                    if not (isinstance(t, int) and t == 0):
                        take_row(t - 1, 1 - s)
                    act.wait_ge(xt_in_psum, t + 1)
                    wait(act, projected, t - 1)
                    act.copy(xt[s][:], p_t[:, 0:D].rearrange("p (a b) -> p a b", a=2)).then_inc(xt_ready, 1)
                    if not (isinstance(t, int) and t == 0):
                        root(t - 1)

                def root(t):
                    act.wait_ge(squares_ready, t + 1)
                    act.sqrt(nrm[:], nrm[:]).then_inc(norms_ready, 1)

                pairs(act, T, body)
                take_row(T - 1, 1)
                root(T - 1)

            @block.tensor
            def _(pe):
                pe.wait_ge(zeroed, 1)
                for bank in p_kv + [p_vsum]:
                    pe.matmul(bank[:], zeros[:, 0:P], zeros[:], start=True, stop=False, skip_group_check=True)

                def kv_sums(t, s):
                    for g in range(4):
                        pe.wait_ge(feat_ready, t * 4 + (g + 1))
                        if g == 0:
                            pe.wait_ge(v1_ready, t + 1)
                            pe.matmul(p_vsum[0:1, 0:H * V1], ones[:, 0:1], v1[s][:].rearrange("p h e -> p (h e)"),
                                      start=False, stop=False, skip_group_check=True)
                        for m in range(FCH):
                            h = 2 * g + m // 4
                            rhs = v1[s][:, h, :] if m < 8 else v1[s][:, 2 * g:2 * g + 2, :].rearrange("p h e -> p (h e)")
                            mm = pe.matmul(kv_place(g, m), feat[g % 2][:, m * P:(m + 1) * P], rhs,
                                           start=False, stop=False, skip_group_check=True)
                        mm.then_inc(feat_used, 1)

                def body(t, s):
                    pe.wait_ge(xn_ready, t + 1)
                    wait(pe, xt_ready, t)
                    pe.transpose(p_t[:, 0:P], xn[s][:, 0:P], ident[:])
                    pe.transpose(p_t[:, P:D], xn[s][:, P:D], ident[:]).then_inc(xt_in_psum, 1)
                    if not (isinstance(t, int) and t == 0):
                        kv_sums(t - 1, 1 - s)
                    pe.wait_ge(xt_ready, t + 1)
                    wait(pe, row_ready, t)
                    wait(pe, qkv_taken, t)
                    for bank, lo, hi in ((p_row, 0, W_Q), (p_qk, W_Q, W_Q + 2 * D), (p_v, W_Q + 2 * D, W_Q + 3 * D)):
                        for kc in range(2):
                            mm = pe.matmul(bank[:, 0:hi - lo], xt[s][:, kc, :], w_cat[:, kc, lo:hi], start=(kc == 0), stop=(kc == 1))
                    mm.then_inc(projected, 1)

                pairs(pe, T, body)
                kv_sums(T - 1, 1)

            @block.vector
            def _(dve):
                dve.memset(zeros[:], 0.0).then_inc(zeroed, 1)
                dve.tensor_scalar(vmask[:], valid[:], 1.0 / N, None, ALU.mult)
                dve.drain()

                def body(t, s):
                    dve.wait_ge(projected, t + 1)
                    dve.tensor_tensor(qk[:], p_qk[:], b_qkv[:, 0:2 * D], ALU.add)
                    dve.tensor_tensor(vtmp[:], p_v[:, 0:D], b_qkv[:, 2 * D:3 * D], ALU.add).then_inc(qkv_taken, 1)
                    dve.drain()
                    dve.tensor_tensor(sq[:], qk[:], qk[:], ALU.mult)
                    dve.drain()
                    dve.tensor_reduce(nrm[:], sq[:].rearrange("p (h e) -> p h e", e=C), AXX, ALU.add)
                    dve.drain()
                    dve.tensor_tensor(nrm[:], nrm[:], ss_scale[:], ALU.mult).then_inc(squares_ready, 1)
                    wait(dve, feat_used, t * 4 - 4)
                    dve.tensor_scalar(v1[s][:, :, 1:V1], vtmp[:].rearrange("p (h e) -> p h e", h=H), vmask[:, bass.ds(t, 1)], None, ALU.mult)
                    dve.tensor_copy(v1[s][:, :, 0:1], vmask[:, bass.ds(t, 1)].unsqueeze(1).broadcast_to([P, H, 1])).then_inc(v1_ready, 1)
                    dve.wait_ge(norms_ready, t + 1)
                    dve.tensor_scalar(nrm[:], nrm[:], NORM_EPS, None, ALU.max)
                    dve.drain()
                    dve.reciprocal(nrm[:], nrm[:])
                    dve.drain()
                    dve.tensor_tensor(nrm[:], nrm[:], nrm_scale[:], ALU.mult)
                    dve.drain()
                    k3 = qk[:, D:2 * D].rearrange("p (h e) -> p h e", h=H)
                    kn = nrm[:, H:2 * H].unsqueeze(2).broadcast_to([P, H, C])
                    dve.tensor_tensor(kk[:, :, 0:C], k3, kn, ALU.mult)
                    dve.tensor_tensor(kk[:, :, C:2 * C], k3, kn, ALU.mult)
                    wait(dve, q_out[s], (t - s) * 8)
                    dve.tensor_tensor(qst[s][:].rearrange("p (h e) -> p h e", h=H), qk[:, 0:D].rearrange("p (h e) -> p h e", h=H),
                                      nrm[:, 0:H].unsqueeze(2).broadcast_to([P, H, C]), ALU.mult).then_inc(q_ready, 1)
                    dve.drain()
                    for g in range(4):
                        wait(dve, feat_used, t * 4 + (g - 1))
                        products(dve, feat[g % 2], kk, g, feat_ready)

                pairs(dve, T, body)
                dve.wait_ge(feat_used, 4 * T)
                dve.memset(mix_w[:, :, 8 * V1:10 * V1], 0.0)
                dve.drain()
                for g in range(4):
                    for m in range(8):
                        o = mix_w[:, g, m * V1:(m + 1) * V1]
                        k = kv_place(g, m)
                        if m % 4 == 0:
                            dve.tensor_scalar(o[0:C], k[0:C], A_COEF, None, ALU.mult)
                            dve.tensor_scalar(o[C:2 * C], k[C:2 * C], 2 * A_COEF, None, ALU.mult)
                            dve.tensor_scalar(o[2 * C:P], k[2 * C:P], 2 * A_COEF, None, ALU.mult)
                        else:
                            dve.tensor_scalar(o, k, 2 * A_COEF, None, ALU.mult)
                    for hh in range(2):
                        for a, coef in enumerate((A_COEF, SCALE ** 2 * B_COEF)):
                            p0 = hh * 2 * C + a * C
                            dve.tensor_scalar(mix_w[p0:p0 + C, g, (8 + hh) * V1:(9 + hh) * V1],
                                              kv_place(g, 8)[p0:p0 + C, hh * V1:(hh + 1) * V1], coef, None, ALU.mult)
                dve.tensor_scalar(vsum_w[:], p_vsum[0:1, 0:H * V1], SCALE ** 4 * C_COEF, None, ALU.mult)

            @block.sync
            def _(sp):
                def body(t, s):
                    sp.wait_ge(row_ready, t + 1)
                    sp.dma_start(node_rows[bass.ts(t, P), :], row[s][:]).then_inc(row_out[s], 16)
                    sp.wait_ge(q_ready, t + 1)
                    sp.dma_start(qn_dram[bass.ts(t, P), :], qst[s][:]).then_inc(q_out[s], 16)

                pairs(sp, T, body)
                for s in range(2):
                    sp.wait_ge(row_out[s], T // 2 * 16)
                    sp.wait_ge(q_out[s], T // 2 * 16)

        with ExitStack() as c:
            qs = [sb(f"qs{i}", [P, D], ctx=c) for i in range(2)]
            qq = [sb(f"qq{i}", [P, H, 2 * C], ctx=c) for i in range(2)]
            feat = [sb(f"qfeat{i}", [P, FEAT], ctx=c) for i in range(2)]
            feat_t = [sb(f"qfeat_t{i}", [P, FEAT], ctx=c) for i in range(2)]
            ry = sb("ry", [P, H], ctx=c)
            yn = sb("yn", [P, D], ctx=c)
            yt = sb("yt", [P, D], ctx=c)
            p_ft = [ps(f"p_ft{i}", [P, 1536], c) for i in range(2)]
            p_y = ps("p_y", [P, 512], c)
            p_o = ps("p_o", [P, 512], c)
            q_in = [sem(f"q_in{i}", c) for i in range(2)]
            q_doubled = sem("q_doubled", c)
            feat_ready = sem("qfeat_ready", c)
            feat_turned = sem("feat_turned", c)
            feat_t_ready = sem("feat_t_ready", c)
            feat_t_used = sem("feat_t_used", c)
            y_taken = sem("y_taken", c)
            yt_in_psum = sem("yt_in_psum", c)
            yt_ready = sem("yt_ready", c)
            mix_ready = sem("mix_ready", c)
            mix_added = sem("mix_added", c)
            block = c.enter_context(nc.Block())

            @block.sync
            def _(sp):
                def body(t, s):
                    wait(sp, q_doubled, t - 1)
                    sp.dma_start(qs[s][:], qn_dram[bass.ts(t, P), :]).then_inc(q_in[s], 16)
                pairs(sp, T, body)

            @block.vector
            def _(dve):
                def finish(t):
                    dve.wait_ge(feat_t_used, t * 4 + 4)
                    y3 = p_y[:, 0:H * V1].rearrange("p (h e) -> p h e", h=H)
                    dve.reciprocal(ry[:], y3[:, :, 0])
                    dve.drain()
                    wait(dve, yt_in_psum, t)
                    dve.tensor_tensor(yn[:].rearrange("p (h e) -> p h e", h=H), y3[:, :, 1:V1],
                                      ry[:].unsqueeze(2).broadcast_to([P, H, C]), ALU.mult).then_inc(y_taken, 1)

                def add(t):
                    r = resid[:, bass.ds(t, 1), :].rearrange("p a f -> p (a f)")
                    dve.wait_ge(mix_ready, t + 1)
                    dve.tensor_tensor(r, r, p_o[:, D:2 * D], ALU.add).then_inc(mix_added, 1)
                    dve.drain()
                    dve.tensor_tensor(r, r, b_proj[:], ALU.add)

                def body(t, s):
                    dve.wait_ge(q_in[s], (t - s) * 8 + 16)
                    wait(dve, feat_ready, t * 4 - 4)
                    dve.tensor_copy(qq[s][:, :, 0:C], qs[s][:].rearrange("p (h e) -> p h e", h=H))
                    dve.tensor_copy(qq[s][:, :, C:2 * C], qs[s][:].rearrange("p (h e) -> p h e", h=H)).then_inc(q_doubled, 1)
                    dve.drain()
                    for g in range(4):
                        wait(dve, feat_turned, t * 4 + (g - 1))
                        products(dve, feat[g % 2], qq[s], g, feat_ready)
                        if g == 1 and not (isinstance(t, int) and t == 0):
                            finish(t - 1)
                        if g == 3 and not (isinstance(t, int) and t == 0):
                            add(t - 1)

                pairs(dve, T, body)
                finish(T - 1)
                add(T - 1)

            @block.scalar
            def _(act):
                def project(t):
                    act.wait_ge(yt_in_psum, t + 1)
                    wait(act, mix_ready, t)
                    act.copy(yt[:], p_o[:, 0:D]).then_inc(yt_ready, 1)

                def body(t, s):
                    for g in range(4):
                        act.wait_ge(feat_turned, t * 4 + (g + 1))
                        wait(act, feat_t_used, t * 4 + (g - 1))
                        act.copy(feat_t[g % 2][:], p_ft[g % 2][:, 0:FEAT]).then_inc(feat_t_ready, 1)
                        if g == 2 and not (isinstance(t, int) and t == 0):
                            project(t - 1)

                pairs(act, T, body)
                project(T - 1)

            @block.tensor
            def _(pe):
                def turn(t, g):
                    pe.wait_ge(feat_ready, t * 4 + (g + 1))
                    wait(pe, feat_t_ready, t * 4 + (g - 1))
                    for m in range(FCH):
                        mm = pe.transpose(p_ft[g % 2][:, m * P:(m + 1) * P], feat[g % 2][:, m * P:(m + 1) * P], ident[:])
                    mm.then_inc(feat_turned, 1)

                def sums(t, g):
                    if g == 0:
                        wait(pe, y_taken, t)
                        pe.matmul(p_y[:, 0:H * V1], ones[0:1, :], vsum_w[:], start=True, stop=False, skip_group_check=True)
                    pe.wait_ge(feat_t_ready, t * 4 + (g + 1))
                    for m in range(FCH):
                        h = 2 * g + m // 4
                        o = p_y[:, h * V1:(h + 1) * V1] if m < 8 else p_y[:, 2 * g * V1:(2 * g + 2) * V1]
                        w = mix_w[:, g, m * V1:(m + 1) * V1] if m < 8 else mix_w[:, g, 8 * V1:10 * V1]
                        mm = pe.matmul(o, feat_t[g % 2][:, m * P:(m + 1) * P], w, start=False, stop=(g == 3 and m == 8),
                                       skip_group_check=True)
                    mm.then_inc(feat_t_used, 1)

                def turn_y(t):
                    pe.wait_ge(y_taken, t + 1)
                    wait(pe, mix_added, t)
                    for k in range(2):
                        mm = pe.transpose(p_o[:, k * P:(k + 1) * P], yn[:, k * P:(k + 1) * P], ident[:])
                    mm.then_inc(yt_in_psum, 1)

                def project(t):
                    pe.wait_ge(yt_ready, t + 1)
                    for k in range(2):
                        mm = pe.matmul(p_o[:, D:2 * D], yt[:, k * P:(k + 1) * P], wp_t[:, k, :], start=(k == 0), stop=(k == 1))
                    mm.then_inc(mix_ready, 1)

                def body(t, s):
                    for g in range(4):
                        turn(t, g)
                        if g == 0:
                            if not (isinstance(t, int) and t == 0):
                                sums(t - 1, 3)
                        else:
                            sums(t, g - 1)
                        if not (isinstance(t, int) and t == 0):
                            if g == 2:
                                turn_y(t - 1)
                            if g == 3:
                                project(t - 1)

                def body_first(t, s):
                    body(t, s)

                pairs(pe, T, body_first)
                sums(T - 1, 3)
                turn_y(T - 1)
                project(T - 1)

        G4 = 4
        SP_ = G4 * P
        acc = sb("acc", [P, T, ROW], ctx=early)
        src_t = sb("src_t", [P, SP_, TILES_PER_CHUNK], I32, ctx=early)
        dst_t = sb("dst_t", [P, SP_, TILES_PER_CHUNK], ctx=early)
        blk_row = sb("blk_row", [1, SP_], I32, ctx=early)
        with ExitStack() as c:
            fd = sb("fd", [1, CHUNKS], I32, ctx=c)
            fdf = sb("fdf", [1, CHUNKS], ctx=c)
            ci = sb("ci", [1, CHUNKS], I32, ctx=c)
            cf = sb("cf", [1, CHUNKS], ctx=c)
            scol = sb("scol", [P, G4], ctx=c)
            cmp = sb("cmp", [P, G4, CHUNKS], ctx=c)
            ccol = sb("ccol", [P, G4], ctx=c)
            bcol = sb("bcol", [P, G4], ctx=c)
            b128 = sb("b128", [P, G4], ctx=c)
            cidx = sb("cidx", [P, G4], I32, ctx=c)
            s_rows = [sb(f"s_rows{i}", [P, CHUNK], I32, ctx=c) for i in range(G4)]
            d_rows = [sb(f"d_rows{i}", [P, CHUNK], I32, ctx=c) for i in range(G4)]
            s_f = sb("s_f", [P, CHUNK], ctx=c)
            d_f = sb("d_f", [P, CHUNK], ctx=c)
            gmax = sb("gmax", [P, H], ctx=c)
            gmax_all = sb("gmax_all", [P, H], ctx=c)
            shift = sb("shift", [P, T, H], ctx=c)
            p_g = ps("p_g", [P, 512], c)
            p_b = ps("p_b", [P, 512], c)
            p_s = ps("p_s", [P, 512], c)
            p_d = ps("p_d", [P, 512], c)
            first_in = sem("first_in", c)
            chunk_nr = sem("chunk_nr", c)
            g_ready = sem("g_ready", c)
            g_spread = sem("g_spread", c)
            b_ready = sem("b_ready", c)
            b_turned = sem("b_turned", c)
            rows_in = [sem(f"rows_in{i}", c) for i in range(G4)]
            rows_ready = sem("rows_ready", c)
            rows_turned = sem("rows_turned", c)
            lists_ready = sem("lists_ready", c)
            gmax_part = sem("gmax_part", c)
            gmax_ready = sem("gmax_ready", c)
            block = c.enter_context(nc.Block())

            @block.sync
            def _(sp):
                sp.dma_start(fd[:], dst_pad[:, 0:1].rearrange("c a -> a c"), allow_slow_non_contiguous=True).then_inc(first_in, 16)

            @block.gpsimd
            def _(pool):
                pool.iota(ci[:], [[1, CHUNKS]], base=0, channel_multiplier=0).then_inc(chunk_nr, 1)
                pool.wait_ge(gmax_part, 1)
                pool.partition_all_reduce(gmax_all[:], gmax[:], P, RMAX).then_inc(gmax_ready, 1)
                pool.wait_ge(b_ready, 1)
                for g in range(G4):
                    pool.indirect_dma_start(s_rows[g][:], None, src_pad, bass.IndirectOffsetOnAxis(ap=cidx[:, g:g + 1], axis=0)).then_inc(rows_in[g], 16)
                    pool.indirect_dma_start(d_rows[g][:], None, dst_pad, bass.IndirectOffsetOnAxis(ap=cidx[:, g:g + 1], axis=0)).then_inc(rows_in[g], 16)

            @block.vector
            def _(dve):
                dve.tensor_reduce(gmax[:], a_s[:].rearrange("p t h -> p h t"), AXX, ALU.max).then_inc(gmax_part, 1)
                dve.wait_ge(first_in, 16)
                dve.wait_ge(chunk_nr, 1)
                dve.tensor_scalar(fd[:], fd[:], P.bit_length() - 1, None, ALU.arith_shift_right)
                dve.tensor_copy(cf[:], ci[:])
                for g in range(G4):
                    dve.tensor_scalar(scol[:, g:g + 1], iota_col[:], float(g * P), None, ALU.add)
                dve.drain()
                dve.tensor_copy(fdf[:], fd[:])
                dve.drain()
                dve.tensor_tensor(fdf[:], fdf[:], cf[:], ALU.add).then_inc(g_ready, 1)
                dve.wait_ge(g_spread, 1)
                for g in range(G4):
                    dve.tensor_scalar(cmp[:, g, 1:CHUNKS], p_g[:, 1:CHUNKS], scol[:, g:g + 1], None, ALU.is_le)
                dve.drain()
                dve.tensor_reduce(ccol[:], cmp[:, :, 1:CHUNKS], AXX, ALU.add)
                dve.drain()
                dve.tensor_copy(cidx[:], ccol[:])
                dve.tensor_tensor(bcol[:], scol[:], ccol[:], ALU.subtract)
                dve.drain()
                dve.tensor_scalar(b128[:], bcol[:], float(P), None, ALU.mult).then_inc(b_ready, 1)
                dve.wait_ge(gmax_ready, 1)
                dve.tensor_tensor(shift[:], adm[:, :, 0:H], gmax_all[:].unsqueeze(1).broadcast_to([P, T, H]), ALU.add)
                dve.memset(acc[:], 0.0)
                dve.drain()
                dve.scalar_tensor_tensor(out=adm[:, :, H:2 * H], in0=shift[:], scalar=SLOPE, in1=shift[:], op0=ALU.mult, op1=ALU.max)
                dve.wait_ge(b_turned, 1)
                dve.tensor_copy(blk_row[:], p_b[0:1, :])
                for g in range(G4):
                    dve.wait_ge(rows_in[g], 32)
                    wait(dve, rows_turned, g)
                    dve.tensor_copy(s_f[:], s_rows[g][:])
                    dve.tensor_copy(d_f[:], d_rows[g][:])
                    dve.drain()
                    dve.tensor_scalar(d_f[:], d_f[:], b128[:, g:g + 1], None, ALU.subtract).then_inc(rows_ready, 1)
                    dve.wait_ge(rows_turned, g + 1)
                    dve.tensor_copy(src_t[:, g * P:(g + 1) * P, :].rearrange("p s u -> p u s"), p_s[:].rearrange("p (u s) -> p u s", u=4))
                    dve.tensor_copy(dst_t[:, g * P:(g + 1) * P, :].rearrange("p s u -> p u s"), p_d[:].rearrange("p (u s) -> p u s", u=4)).then_inc(lists_ready, 1)

            @block.tensor
            def _(pe):
                pe.wait_ge(g_ready, 1)
                pe.matmul(p_g[:, 0:CHUNKS], ones[0:1, :], fdf[:], start=True, stop=True).then_inc(g_spread, 1)
                pe.wait_ge(b_ready, 1)
                for g in range(G4):
                    mm = pe.matmul(p_b[0:1, g * P:(g + 1) * P], bcol[:, g:g + 1], ident[:], start=True, stop=True)
                mm.then_inc(b_turned, 1)
                for g in range(G4):
                    pe.wait_ge(rows_ready, g + 1)
                    wait(pe, lists_ready, g)
                    for bank, f in ((p_s, s_f), (p_d, d_f)):
                        for u in range(TILES_PER_CHUNK):
                            mm = pe.transpose(bank[:, u * P:(u + 1) * P], f[:, u * P:(u + 1) * P], ident[:])
                    mm.then_inc(rows_turned, 1)

        TC = TILES_PER_CHUNK
        with ExitStack() as c:
            idx = [sb(f"idx{i}", [P, TC], I32, ctx=c) for i in range(2)]
            msg = [sb(f"msg{i}", [P, TC, ROW], ctx=c) for i in range(2)]
            sel = [sb(f"sel{i}", [P, TC, P], ctx=c) for i in range(2)]
            sel_t = [sb(f"sel_t{i}", [P, TC * P], ctx=c) for i in range(2)]
            lg = [sb(f"lg{i}", [P, TC, H], ctx=c) for i in range(2)]
            p_st = [ps(f"p_st{i}", [P, 512], c) for i in range(2)]
            p_e = [ps(f"p_e{i}", [P, 512], c) for i in range(2)]
            p_m = [ps(f"p_m{i}", [P, 512], c) for i in range(2)]
            idx_ready = sem("idx_ready", c)
            gather_opened = sem("gather_opened", c)
            gathered = [sem(f"gathered{i}", c) for i in range(2)]
            sel_ready = sem("sel_ready", c)
            sel_turned = sem("sel_turned", c)
            sel_t_ready = sem("sel_t_ready", c)
            dst_spread = sem("dst_spread", c)
            logit_ready = sem("logit_ready", c)
            weight_ready = sem("weight_ready", c)
            msg_ready = sem("msg_ready", c)
            msg_summed = sem("msg_summed", c)
            acc_added = sem("acc_added", c)
            block = c.enter_context(nc.Block())

            @block.gpsimd
            def _(pool):
                def body(s, j):
                    pool.wait_ge(idx_ready, s + 1)
                    wait(pool, msg_summed, s - 1)
                    pool.sem_inc(gather_opened, 1)
                    for u in range(TC):
                        pool.indirect_dma_start(msg[j][:, u, :], None, node_rows,
                                                bass.IndirectOffsetOnAxis(ap=idx[j][:, u:u + 1], axis=0)).then_inc(gathered[j], 16)
                pairs(pool, STEPS, body)

            @block.scalar
            def _(act):
                def index(s, j):
                    if not (isinstance(s, int) and s < 2):
                        act.wait_ge(gathered[j], (s - j) * (8 * TC))
                    act.copy(idx[j][:], src_t[:, bass.ds(s, 1), :].rearrange("p s u -> p (s u)")).then_inc(idx_ready, 1)

                def body(s, j):
                    index(s, j)
                    act.wait_ge(sel_turned, s + 1)
                    wait(act, dst_spread, s - 1)
                    act.copy(sel_t[j][:], p_st[j][:]).then_inc(sel_t_ready, 1)
                    act.wait_ge(logit_ready, s + 1)
                    act.activation(msg[j][:, :, D:ROW], lg[j][:], ACT.Exp).then_inc(weight_ready, 1)

                pairs(act, STEPS, body)

            @block.vector
            def _(dve):
                def select(s, j):
                    wait(dve, msg_summed, s - 1)
                    dve.tensor_tensor(sel[j][:], dst_t[:, bass.ds(s, 1), :].rearrange("p s u -> p (s u)").unsqueeze(2).broadcast_to([P, TC, P]),
                                      iota_row[:].unsqueeze(1).broadcast_to([P, TC, P]), ALU.is_equal).then_inc(sel_ready, 1)

                def accumulate(s, j):
                    b = dve.value_load(blk_row[0:1, bass.ds(s, 1)], min_val=0, max_val=T - 1)
                    a = acc[:, bass.ds(b, 1), :].rearrange("p a f -> p (a f)")
                    dve.wait_ge(msg_summed, s + 1)
                    dve.tensor_tensor(a, a, p_m[j][:, 0:ROW], ALU.add).then_inc(acc_added, 1)

                def body(s, j):
                    select(s, j)
                    dve.wait_ge(gathered[j], (s - j) * (8 * TC) + 16 * TC)
                    dve.wait_ge(dst_spread, s + 1)
                    pe3 = p_e[j][:, 0:TC * 2 * H].rearrange("p (u a) -> p u a", u=TC)
                    dve.tensor_tensor(lg[j][:], msg[j][:, :, D:ROW], pe3[:, :, 0:H], ALU.add)
                    dve.drain()
                    dve.scalar_tensor_tensor(out=lg[j][:], in0=lg[j][:], scalar=SLOPE, in1=lg[j][:], op0=ALU.mult, op1=ALU.max)
                    dve.drain()
                    dve.tensor_tensor(lg[j][:], lg[j][:], pe3[:, :, H:2 * H], ALU.subtract).then_inc(logit_ready, 1)
                    if not (isinstance(s, int) and s == 0):
                        accumulate(s - 1, 1 - j)
                    dve.wait_ge(weight_ready, s + 1)
                    m4 = msg[j][:, :, 0:D].rearrange("p u (h e) -> p u h e", h=H)
                    dve.tensor_tensor(m4, m4, msg[j][:, :, D:ROW].unsqueeze(3).broadcast_to([P, TC, H, C]), ALU.mult).then_inc(msg_ready, 1)

                pairs(dve, STEPS, body)
                accumulate(STEPS - 1, 1)
                dve.drain()

            @block.tensor
            def _(pe):
                def aggregate(s, j):
                    pe.wait_ge(msg_ready, s + 1)
                    wait(pe, acc_added, s - 1)
                    for u in range(TC):
                        mm = pe.matmul(p_m[j][:, 0:ROW], sel[j][:, u, :], msg[j][:, u, :], start=(u == 0), stop=(u == TC - 1))
                    mm.then_inc(msg_summed, 1)

                def body(s, j):
                    pe.wait_ge(sel_ready, s + 1)
                    wait(pe, sel_t_ready, s - 1)
                    for u in range(TC):
                        mm = pe.transpose(p_st[j][:, u * P:(u + 1) * P], sel[j][:, u, :], ident[:])
                    mm.then_inc(sel_turned, 1)
                    b = pe.value_load(blk_row[0:1, bass.ds(s, 1)], min_val=0, max_val=T - 1)
                    pe.wait_ge(sel_t_ready, s + 1)
                    wait(pe, logit_ready, s - 1)
                    for u in range(TC):
                        mm = pe.matmul(p_e[j][:, u * 2 * H:(u + 1) * 2 * H], sel_t[j][:, u * P:(u + 1) * P],
                                       adm[:, bass.ds(b, 1), :].rearrange("p a f -> p (a f)"), start=True, stop=True)
                    mm.then_inc(dst_spread, 1)
                    aggregate(s, j)

                pairs(pe, STEPS, body)

        with ExitStack() as c:
            block = c.enter_context(nc.Block())

            @block.vector
            def _(dve):
                w = acc[:, :, D:ROW]
                dve.tensor_scalar(w, w, TINY, None, ALU.max)
                dve.drain()
                dve.reciprocal(w, w)
                dve.drain()
                with dve.Fori(0, T) as t:
                    a = acc[:, bass.ds(t, 1), 0:D].rearrange("p a f -> p (a f)")
                    a3 = a.rearrange("p (h e) -> p h e", h=H)
                    r = resid[:, bass.ds(t, 1), :].rearrange("p a f -> p (a f)")
                    dve.tensor_tensor(a3, a3, acc[:, bass.ds(t, 1), D:ROW].rearrange("p a h -> p (a h)").unsqueeze(2).broadcast_to([P, H, C]), ALU.mult)
                    dve.drain()
                    dve.tensor_tensor(a, a, b_gnn[:], ALU.add)
                    dve.drain()
                    dve.scalar_tensor_tensor(out=r, in0=a, scalar=0.0, in1=r, op0=ALU.max, op1=ALU.add)
                dve.drain()
        early.close()

        late = ExitStack()
        xl = sb("xl", [P, T, D], ctx=late)
        top_w = sb("top_w", [P, T, 2], ctx=late)
        places = sb("places", [P, 2, T], I32, ctx=late)
        exp_row = sb("exp_row", [1, P], I32, ctx=late)
        g_b = sb("g_b", [P, D], ctx=late)
        be_b = sb("be_b", [P, D], ctx=late)
        with ExitStack() as c:
            gw = sb("gw", [P, 2, NEXP], ctx=c)
            gb = sb("gb", [P, NEXP], ctx=c)
            st = sb("m_st", [P, T, 6], ctx=c)
            ag = sb("m_ag", [P, T, 2], ctx=c)
            rs = sb("m_rs", [P, T], ctx=c)
            var_ready = sem("m_var_ready", c)
            std_ready = sem("m_std_ready", c)
            xt = [sb(f"m_xt{i}", [P, D], ctx=c) for i in range(2)]
            lgt = sb("m_lg", [P, NEXP], ctx=c)
            m8 = sb("m8", [P, 8], ctx=c)
            i8 = sb("i8", [P, 8], U32, ctx=c)
            top8 = sb("top8", [P, T, 8], ctx=c)
            idx8 = sb("idx8", [P, T, 8], U32, ctx=c)
            idf = sb("idf", [P, T, 2], ctx=c)
            oh = [sb(f"oh{i}", [P, T, NEXP], ctx=c) for i in range(2)]
            cnt = sb("cnt", [P, T, NEXP], ctx=c)
            tri = sb("tri", [P, P], ctx=c)
            pos = sb("pos", [P, T, NEXP], ctx=c)
            tot = sb("tot", [P, T, NEXP], ctx=c)
            toe = sb("toe", [P, NEXP, T], ctx=c)
            keep = sb("keep", [P, NEXP, T], ctx=c)
            run = sb("run", [P, NEXP, T], ctx=c)
            ti = sb("ti", [P, NEXP], I32, ctx=c)
            tf = sb("tf", [P, NEXP], ctx=c)
            zf = sb("zf", [P, NEXP], ctx=c)
            base = sb("base", [P, NEXP], ctx=c)
            placef = sb("placef", [P, 2, T], ctx=c)
            ecmp = sb("ecmp", [P, NEXP], ctx=c)
            ecol = sb("ecol", [P, 1], ctx=c)
            p_x = [ps(f"m_px{i}", [P, 512], c) for i in range(2)]
            p_l = [ps(f"m_pl{i}", [P, 512], c) for i in range(2)]
            p_w = [ps(f"m_pw{i}", [P, 512], c) for i in range(2)]
            p_t2 = [ps(f"m_pt{i}", [P, 512], c) for i in range(2)]
            w_in = sem("m_w_in", c)
            xl_ready = sem("xl_ready", c)
            x_turned = sem("x_turned", c)
            xt_ready = sem("m_xt_ready", c)
            logits = sem("logits", c)
            logits_taken = sem("logits_taken", c)
            tops = sem("tops", c)
            exps = sem("exps", c)
            cnt_ready = sem("cnt_ready", c)
            ranked = sem("ranked", c)
            tri_ready = sem("tri_ready", c)
            places_ready = sem("places_ready", c)
            sent = sem("sent", c)
            ecol_ready = sem("ecol_ready", c)
            erow_in_psum = sem("erow_in_psum", c)
            block = c.enter_context(nc.Block())
            HALF = T * NEXP // 2

            @block.sync
            def _(sp):
                sp.dma_start(gw[:], gate_w.rearrange("(c k) e -> k c e", k=P)).then_inc(w_in, 16)
                sp.dma_start(gb[:], bcast_rows(gate_b, NEXP)).then_inc(w_in, 16)
                sp.dma_start(g_b[:], bcast_rows(gamma, D)).then_inc(w_in, 16)
                sp.dma_start(be_b[:], bcast_rows(beta, D)).then_inc(w_in, 16)

            @block.vector
            def _(dve):
                def norm(t, s):
                    r = resid[:, bass.ds(t, 1), :].rearrange("p a f -> p (a f)")
                    dve.tensor_scalar(xl[:, bass.ds(t, 1), :].rearrange("p a f -> p (a f)"), r, ag[:, bass.ds(t, 1), 0:1].rearrange("p a b -> p (a b)"),
                                      rs[:, bass.ds(t, 1)], ALU.subtract, ALU.mult).then_inc(xl_ready, 1)

                def best(t, s):
                    dve.drain()
                    dve.wait_ge(logits, t + 1)
                    dve.tensor_tensor(lgt[:], p_l[s][:, 0:NEXP], gb[:], ALU.add).then_inc(logits_taken, 1)
                    dve.drain()
                    dve.max(m8[:], lgt[:])
                    dve.drain()
                    dve.max_index(i8[:], m8[:], lgt[:])
                    dve.tensor_copy(top8[:, bass.ds(t, 1), :], m8[:].unsqueeze(1))
                    dve.drain()
                    dve.tensor_copy(idx8[:, bass.ds(t, 1), :], i8[:].unsqueeze(1))

                def body(t, s):
                    norm(t, s)
                    if not (isinstance(t, int) and t == 0):
                        best(t - 1, 1 - s)

                dve.wait_ge(w_in, 64)
                with dve.Fori(0, T) as t:
                    dve.bn_stats(st[:, bass.ds(t, 1), :], resid[:, bass.ds(t, 1), :])
                dve.drain()
                moments(dve, ag, st)
                dve.tensor_scalar(rs[:], ag[:, :, 1], LN_EPS, None, ALU.add).then_inc(var_ready, 1)
                dve.wait_ge(std_ready, 1)
                dve.reciprocal(rs[:], rs[:])
                dve.drain()
                pairs(dve, T, body)
                best(T - 1, 1)
                dve.drain()
                dve.tensor_tensor(top_w[:, :, 1:2], top8[:, :, 1:2], top8[:, :, 0:1], ALU.subtract).then_inc(tops, 1)
                dve.tensor_copy(idf[:], idx8[:, :, 0:2])
                dve.drain()
                for k in range(2):
                    dve.tensor_tensor(oh[k][:], idf[:, :, k:k + 1].broadcast_to([P, T, NEXP]),
                                      iota_row[:, 0:NEXP].unsqueeze(1).broadcast_to([P, T, NEXP]), ALU.is_equal)
                dve.drain()
                dve.tensor_tensor(cnt[:], oh[0][:], oh[1][:], ALU.add)
                dve.drain()
                dve.tensor_tensor(cnt[:], cnt[:], valid[:].unsqueeze(2).broadcast_to([P, T, NEXP]), ALU.mult).then_inc(cnt_ready, 1)
                dve.wait_ge(exps, 1)
                dve.tensor_scalar(top_w[:, :, 0:1], top_w[:, :, 1:2], 1.0, None, ALU.add)
                dve.drain()
                dve.reciprocal(top_w[:, :, 0:1], top_w[:, :, 0:1])
                dve.drain()
                dve.tensor_tensor(top_w[:, :, 1:2], top_w[:, :, 1:2], top_w[:, :, 0:1], ALU.mult)
                dve.memset(keep[:], 1.0)
                dve.memset(zf[:], 0.0)
                dve.drain()
                dve.memset(keep[:, :, 0:1], 0.0)
                dve.wait_ge(ranked, 1)
                for k in range(2):
                    dve.tensor_copy(toe[:, :, k * (T // 2):(k + 1) * (T // 2)].rearrange("p e t -> p t e"),
                                    p_t2[k][:, 0:HALF].rearrange("p (t e) -> p t e", e=NEXP))
                dve.drain()
                dve.tensor_tensor_scan(run[:].rearrange("p e t -> p (e t)"), keep[:].rearrange("p e t -> p (e t)"),
                                       toe[:].rearrange("p e t -> p (e t)"), 0.0, ALU.mult, ALU.add)
                dve.drain()
                dve.tensor_scalar(tf[:], run[:, :, T - 1], float(P - 1), None, ALU.add)
                dve.drain()
                dve.tensor_copy(ti[:], tf[:])
                dve.drain()
                dve.tensor_scalar(ti[:], ti[:], P.bit_length() - 1, None, ALU.arith_shift_right)
                dve.drain()
                dve.tensor_copy(tf[:], ti[:])
                dve.drain()
                dve.tensor_tensor_scan(base[:], tf[:], zf[:], 0.0, ALU.add, ALU.add)
                dve.drain()
                dve.tensor_tensor(base[:], base[:], tf[:], ALU.subtract)
                dve.tensor_tensor(run[:], run[:], toe[:], ALU.subtract)
                dve.drain()
                dve.tensor_scalar(ecmp[:], base[:], iota_col[:], None, ALU.is_le)
                dve.scalar_tensor_tensor(out=pos[:], in0=base[:].unsqueeze(1).broadcast_to([P, T, NEXP]), scalar=float(P),
                                         in1=run[:].rearrange("p e t -> p t e"), op0=ALU.mult, op1=ALU.add)
                dve.drain()
                dve.tensor_reduce(ecol[:], ecmp[:, 1:NEXP], AXX, ALU.add).then_inc(ecol_ready, 1)
                for k in range(2):
                    half = pos[:, k * (T // 2):(k + 1) * (T // 2), :].rearrange("p t e -> p (t e)")
                    dve.tensor_tensor(half, half, p_w[k][:, 0:HALF], ALU.add)
                dve.drain()
                for k in range(2):
                    dve.tensor_tensor(oh[k][:], oh[k][:], pos[:], ALU.mult)
                dve.drain()
                for k in range(2):
                    dve.tensor_reduce(placef[:, k, :], oh[k][:], AXX, ALU.add)
                dve.drain()
                dve.tensor_copy(places[:], placef[:]).then_inc(places_ready, 1)
                dve.wait_ge(erow_in_psum, 1)
                dve.tensor_copy(exp_row[:], p_l[0][0:1, 0:P])

            @block.scalar
            def _(act):
                def body(t, s):
                    act.wait_ge(x_turned, t + 1)
                    wait(act, logits, t - 1)
                    act.copy(xt[s][:], p_x[s][:, 0:D]).then_inc(xt_ready, 1)
                act.wait_ge(var_ready, 1)
                act.sqrt(rs[:], rs[:]).then_inc(std_ready, 1)
                pairs(act, T, body)
                act.wait_ge(tops, 1)
                act.activation(top_w[:, :, 1:2], top_w[:, :, 1:2], ACT.Exp).then_inc(exps, 1)

            @block.tensor
            def _(pe):
                def gate(t, s):
                    pe.wait_ge(xt_ready, t + 1)
                    wait(pe, logits_taken, t - 1)
                    for k in range(2):
                        mm = pe.matmul(p_l[s][:, 0:NEXP], xt[s][:, k * P:(k + 1) * P], gw[:, k, :], start=(k == 0), stop=(k == 1))
                    mm.then_inc(logits, 1)

                def body(t, s):
                    pe.wait_ge(xl_ready, t + 1)
                    wait(pe, xt_ready, t - 1)
                    for k in range(2):
                        mm = pe.transpose(p_x[s][:, k * P:(k + 1) * P], xl[:, t, k * P:(k + 1) * P], ident[:])
                    mm.then_inc(x_turned, 1)
                    gate(t, s)

                for t in range(T):
                    body(t, t % 2)
                pe.wait_ge(cnt_ready, 1)
                pe.wait_ge(tri_ready, 1)
                for k in range(2):
                    half = cnt[:, k * (T // 2):(k + 1) * (T // 2), :].rearrange("p t e -> p (t e)")
                    pe.matmul(p_w[k][:, 0:HALF], tri[:], half, start=True, stop=True)
                    mm = pe.matmul(p_t2[k][:, 0:HALF], ones[:], half, start=True, stop=True)
                mm.then_inc(ranked, 1)
                pe.wait_ge(ecol_ready, 1)
                pe.wait_ge(logits_taken, T)
                pe.matmul(p_l[0][0:1, 0:P], ecol[:], ident[:], start=True, stop=True).then_inc(erow_in_psum, 1)

            @block.gpsimd
            def _(pool):
                pool.affine_select(out=tri[:], in_=ones[:], compare_op=ALU.is_ge, fill=0.0, base=-1,
                                   pattern=[[1, P]], channel_multiplier=-1).then_inc(tri_ready, 1)
                pool.wait_ge(places_ready, 1)
                for t in range(BLOCKS):
                    n = P if t < NFULL else NREST
                    for k in range(2):
                        pool.indirect_dma_start(slot_x, bass.IndirectOffsetOnAxis(ap=places[0:n, k, t:t + 1], axis=0),
                                                xl[0:n, t, :], None).then_inc(sent, 16)
                pool.wait_ge(sent, 2 * BLOCKS * 16)

        with ExitStack() as c:
            KF = FF // P
            wa = [sb(f"wa{i}", [P, 2, FF], ctx=c) for i in range(2)]
            wb = [sb(f"wb{i}", [P, KF, D], ctx=c) for i in range(2)]
            ba = [sb(f"ba{i}", [P, KF], ctx=c) for i in range(2)]
            bb = [sb(f"bb{i}", [P, D], ctx=c) for i in range(2)]
            xs = [sb(f"xs{i}", [P, D], ctx=c) for i in range(2)]
            xst = [sb(f"xst{i}", [P, D], ctx=c) for i in range(2)]
            ht = [sb(f"ht{i}", [P, FF], ctx=c) for i in range(2)]
            ysb = [sb(f"ysb{i}", [P, D], ctx=c) for i in range(2)]
            p_x = [ps(f"e_px{i}", [P, 512], c) for i in range(2)]
            p_h = [ps(f"e_ph{i}", [P, 512], c) for i in range(2)]
            p_y = [ps(f"e_py{i}", [P, 512], c) for i in range(2)]
            x_in = [sem(f"e_x_in{i}", c) for i in range(2)]
            w_in = [sem(f"e_w_in{i}", c) for i in range(2)]
            x_turned = sem("e_x_turned", c)
            xt_ready = sem("e_xt_ready", c)
            hidden = sem("hidden", c)
            ht_ready = sem("ht_ready", c)
            y_in_psum = sem("y_in_psum", c)
            y_ready = sem("y_ready", c)
            y_out = [sem(f"y_out{i}", c) for i in range(2)]
            block = c.enter_context(nc.Block())
            w1v = w1.rearrange("e (c k) f -> k e c f", k=P)
            w2v = w2.rearrange("e (c k) f -> k e c f", k=P)

            @block.sync
            def _(sp):
                def body(t, s):
                    e = sp.value_load(exp_row[0:1, bass.ds(t, 1)], min_val=0, max_val=NEXP - 1)
                    wait(sp, x_turned, t - 1)
                    sp.dma_start(xs[s][:], slot_x[bass.ts(t, P), :]).then_inc(x_in[s], 16)
                    wait(sp, hidden, t - 1)
                    sp.dma_start(wa[s][:], w1v[:, bass.ds(e, 1), :, :].rearrange("k a c f -> k (a c) f")).then_inc(w_in[s], 16)
                    wait(sp, y_ready, t - 1)
                    sp.dma_start(ba[s][:], b1_cols[bass.ds(e, 1), :, :].rearrange("a p c -> p (a c)")).then_inc(w_in[s], 16)
                    sp.dma_start(wb[s][:], w2v[:, bass.ds(e, 1), :, :].rearrange("k a c f -> k (a c) f")).then_inc(w_in[s], 16)
                    sp.dma_start(bb[s][:], b2[bass.ds(e, 1), :].broadcast_to([P, D])).then_inc(w_in[s], 16)
                pairs(sp, SLOT_TILES, body)

            @block.tensor
            def _(pe):
                def second(t, s):
                    pe.wait_ge(ht_ready, t + 1)
                    wait(pe, y_ready, t - 1)
                    for k in range(KF):
                        mm = pe.matmul(p_y[s][:, 0:D], ht[s][:, k * P:(k + 1) * P], wb[s][:, k, :], start=(k == 0), stop=(k == KF - 1))
                    mm.then_inc(y_in_psum, 1)

                def body(t, s):
                    pe.wait_ge(x_in[s], (t - s) * 8 + 16)
                    wait(pe, xt_ready, t - 1)
                    for k in range(2):
                        mm = pe.transpose(p_x[s][:, k * P:(k + 1) * P], xs[s][:, k * P:(k + 1) * P], ident[:])
                    mm.then_inc(x_turned, 1)
                    if not (isinstance(t, int) and t == 0):
                        second(t - 1, 1 - s)
                    pe.wait_ge(w_in[s], (t - s) * 32 + 64)
                    pe.wait_ge(xt_ready, t + 1)
                    wait(pe, ht_ready, t - 1)
                    for m in range(KF):
                        for k in range(2):
                            mm = pe.matmul(p_h[s][:, m * P:(m + 1) * P], wa[s][:, k, m * P:(m + 1) * P], xst[s][:, k * P:(k + 1) * P],
                                           start=(k == 0), stop=(k == 1))
                    mm.then_inc(hidden, 1)
                pairs(pe, SLOT_TILES, body)
                second(SLOT_TILES - 1, 1)

            @block.scalar
            def _(act):
                def body(t, s):
                    act.wait_ge(x_turned, t + 1)
                    wait(act, hidden, t - 1)
                    act.copy(xst[s][:], p_x[s][:, 0:D]).then_inc(xt_ready, 1)
                    act.wait_ge(hidden, t + 1)
                    act.wait_ge(w_in[s], (t - s) * 32 + 64)
                    wait(act, y_in_psum, t - 1)
                    for m in range(KF):
                        a = act.activation(ht[s][:, m * P:(m + 1) * P], p_h[s][:, m * P:(m + 1) * P], ACT.Relu, bias=ba[s][:, m:m + 1])
                    a.then_inc(ht_ready, 1)
                pairs(act, SLOT_TILES, body)

            @block.vector
            def _(dve):
                def body(t, s):
                    dve.wait_ge(y_in_psum, t + 1)
                    dve.wait_ge(w_in[s], (t - s) * 32 + 64)
                    wait(dve, y_out[s], (t - s) * 8)
                    dve.tensor_tensor(ysb[s][:], p_y[s][:, 0:D], bb[s][:], ALU.add).then_inc(y_ready, 1)
                pairs(dve, SLOT_TILES, body)

            @block.gpsimd
            def _(pool):
                def body(t, s):
                    pool.wait_ge(y_ready, t + 1)
                    pool.dma_start(slot_y[bass.ts(t, P), :], ysb[s][:]).then_inc(y_out[s], 16)
                pairs(pool, SLOT_TILES, body)
                for s in range(2):
                    pool.wait_ge(y_out[s], SLOT_TILES // 2 * 16)

        with ExitStack() as c:
            R = 4
            ya = [sb(f"ya{i}", [P, 2, D], ctx=c) for i in range(R)]
            st = [sb(f"f_st{i}", [P, 6], ctx=c) for i in range(R)]
            ag = [sb(f"f_ag{i}", [P, 2], ctx=c) for i in range(R)]
            rs = [sb(f"f_rs{i}", [P, 1], ctx=c) for i in range(R)]
            y_in = [sem(f"f_y_in{i}", c) for i in range(R)]
            ready = sem("f_ready", c)
            ya_used = sem("ya_used", c)
            var_ready = sem("f_var_ready", c)
            std_ready = sem("f_std_ready", c)
            stored = sem("stored", c)
            block = c.enter_context(nc.Block())

            @block.gpsimd
            def _(pool):
                for t in range(BLOCKS):
                    n = P if t < NFULL else NREST
                    wait(pool, ya_used, t - R + 1)
                    for k in range(2):
                        pool.indirect_dma_start(ya[t % R][0:n, k, :], None, slot_y,
                                                bass.IndirectOffsetOnAxis(ap=places[0:n, k, t:t + 1], axis=0)).then_inc(y_in[t % R], 16)

            @block.scalar
            def _(act):
                for t in range(BLOCKS):
                    n = P if t < NFULL else NREST
                    act.wait_ge(var_ready, t + 1)
                    act.sqrt(rs[t % R][0:n], rs[t % R][0:n]).then_inc(std_ready, 1)

            @block.vector
            def _(dve):
                def combine(t):
                    n = P if t < NFULL else NREST
                    s = t % R
                    y = xl[0:n, t, :]
                    dve.wait_ge(y_in[s], (t // R + 1) * 32)
                    for k in range(2):
                        dve.scalar_tensor_tensor(out=y, in0=ya[s][0:n, k, :], scalar=top_w[0:n, t, k:k + 1], in1=y, op0=ALU.mult, op1=ALU.add)
                        dve.drain()
                    dve.bn_stats(st[s][0:n], y).then_inc(ya_used, 1)
                    dve.tensor_tensor(resid[0:n, t, :], resid[0:n, t, :], be_b[0:n], ALU.add)
                    dve.drain()
                    dve.bn_aggr(ag[s][0:n], st[s][0:n])
                    dve.drain()
                    dve.tensor_scalar(rs[s][0:n], ag[s][0:n, 1:2], LN_EPS, None, ALU.add).then_inc(var_ready, 1)

                def finish(t):
                    n = P if t < NFULL else NREST
                    s = t % R
                    y = xl[0:n, t, :]
                    dve.wait_ge(std_ready, t + 1)
                    dve.reciprocal(rs[s][0:n], rs[s][0:n])
                    dve.drain()
                    dve.tensor_scalar(y, y, ag[s][0:n, 0:1], rs[s][0:n], ALU.subtract, ALU.mult)
                    dve.drain()
                    dve.tensor_tensor(y, y, g_b[0:n], ALU.mult)
                    dve.drain()
                    dve.tensor_tensor(y, y, resid[0:n, t, :], ALU.add).then_inc(ready, 1)

                for t in range(BLOCKS):
                    combine(t)
                    if t:
                        finish(t - 1)
                finish(BLOCKS - 1)

            @block.sync
            def _(sp):
                for t in range(BLOCKS):
                    n = P if t < NFULL else NREST
                    sp.wait_ge(ready, t + 1)
                    sp.dma_start(out[t * P:t * P + n, :], xl[0:n, t, :]).then_inc(stored, 16)
                sp.wait_ge(stored, BLOCKS * 16)
        late.close()


_INS = ['x', 'src', 'dst', 'L0_gnn_W', 'L0_gnn_att_src', 'L0_gnn_att_dst', 'L0_gnn_bias', 'L0_mix_Wqkv',
        'L0_mix_bqkv', 'L0_mix_Wproj', 'L0_mix_bproj', 'L0_mix_temperature', 'L0_ffn_gate_w', 'L0_ffn_gate_b',
        'L0_ffn_w1', 'L0_ffn_b1', 'L0_ffn_w2', 'L0_ffn_b2', 'L0_ffn_gamma', 'L0_ffn_beta']
_OUTS = [((N, D), 'float32')]


def kernel(**inputs):
    import numpy as _np
    import concourse.bacc as _bacc
    from concourse import mybir as _mybir
    from concourse.bass_utils import run_bass_kernel_spmd as _run

    nc = _bacc.Bacc("TRN2", target_bir_lowering=False, num_devices=1)
    arrays, args = {}, []
    for name in _INS:
        a = _np.ascontiguousarray(inputs[name])
        arrays[f"in_{name}_dram"] = a
        args.append(nc.dram_tensor(f"in_{name}_dram", a.shape, _mybir.dt.from_np(a.dtype), kind="ExternalInput").ap())
    for i, (shape, dtype) in enumerate(_OUTS):
        args.append(nc.dram_tensor(f"out_{i}_dram", shape, _mybir.dt.from_np(_np.dtype(dtype)), kind="ExternalOutput").ap())
    gps_layer(nc, *args)
    r = _run(nc, [arrays], core_ids=[0])
    return r.results[0]["out_0_dram"]
```

```python
from contextlib import ExitStack

import concourse.bass as bass
from concourse import mybir

F32 = mybir.dt.float32
BF16 = mybir.dt.bfloat16
I32 = mybir.dt.int32
U32 = mybir.dt.uint32
ALU = mybir.AluOpType
ACT = mybir.ActivationFunctionType
AXX = mybir.AxisListType.X
RMAX = bass.bass_isa.ReduceOp.max

P = 128
N = 6250
E = 200000
D = 256
H = 8
C = D // H
T = 50
NFULL = N // P
NREST = N - NFULL * P
BLOCKS = -(-N // P)
TILES_PER_CHUNK = 4
CHUNK = TILES_PER_CHUNK * P
CHUNKS = -(-E // CHUNK)
STEPS = CHUNKS + BLOCKS
ROW = D + H
V1 = C + 1
DIAGS = C // 2 + 1
FEAT = (DIAGS - 1) * C
FCH = FEAT // P
UNITS = H + 1
WRAP = C + DIAGS - 1
NEXP, FF = 16, 512
SLOT_TILES = 114
LN_EPS = 1e-5
NORM_EPS = 1e-12
TINY = 1e-37
A_COEF, B_COEF, C_COEF = 0.5, 1.0, 1.0
SCALE = float(C) ** 0.25
SLOPE = 0.2
PAD_DST = 1 << 20
R = 4
OCT = 8
assert STEPS % OCT == 0 and STEPS // OCT > T + 1 and OCT % R == 0


def wait(eng, sem, value):
    if isinstance(value, int) and value <= 0:
        return
    eng.wait_ge(sem, value)


def pairs(eng, count, body):
    body(0, 0)
    body(1, 1)
    with eng.Fori(1, count // 2) as i:
        body(i * 2, 0)
        body(i * 2 + 1, 1)


def ring(eng, count, slots, body):
    for j in range(slots):
        body(j, j)
    with eng.Fori(1, count // slots) as i:
        for j in range(slots):
            body(i * slots + j, j)


def moments(dve, mv, st):
    m, v = mv[:, :, 0], mv[:, :, 1]
    dve.tensor_tensor(m, st[:, :, 1], st[:, :, 4], ALU.subtract)
    dve.tensor_tensor(st[:, :, 0], st[:, :, 2], st[:, :, 5], ALU.add)
    dve.drain()
    dve.tensor_tensor(v, m, m, ALU.mult)
    dve.drain()
    dve.tensor_scalar(v, v, 0.25, None, ALU.mult)
    dve.tensor_tensor(m, st[:, :, 1], st[:, :, 4], ALU.add)
    dve.drain()
    dve.scalar_tensor_tensor(out=v, in0=st[:, :, 0], scalar=1.0 / D, in1=v, op0=ALU.mult, op1=ALU.add)
    dve.tensor_scalar(m, m, 0.5, None, ALU.mult)
    dve.drain()


def bcast_rows(ap, n):
    return ap.unsqueeze(0).broadcast_to([P, n])


def gps_layer(nc, x, src, dst, gnn_W, att_src, att_dst, gnn_bias, Wqkv, bqkv, Wproj, bproj, temperature,
              gate_w, gate_b, w1, b1, w2, b2, gamma, beta, out):
    top = ExitStack()

    def sb(name, shape, dt=F32, ctx=None):
        return (ctx or top).enter_context(nc.sbuf_tensor(name, shape, dt))

    def ps(name, shape, ctx):
        return ctx.enter_context(nc.psum_tensor(name, shape, F32))

    def sem(name, ctx=None):
        return (ctx or top).enter_context(nc.semaphore(name))

    with top:
        node_rows = nc.dram_tensor("node_rows", (T * P, ROW), F32).ap()
        qn_dram = nc.dram_tensor("qn_dram", (T * P, D), F32).ap()
        src_pad = nc.dram_tensor("src_pad", (CHUNKS, CHUNK), I32).ap()
        dst_pad = nc.dram_tensor("dst_pad", (CHUNKS, CHUNK), I32).ap()
        slot_x = nc.dram_tensor("slot_x", (SLOT_TILES * P, D), F32).ap()
        slot_y = nc.dram_tensor("slot_y", (SLOT_TILES * P, D), F32).ap()
        gram_dram = nc.dram_tensor("gram_dram", (H, C, 2 * C), F32).ap()
        sums_dram = nc.dram_tensor("sums_dram", (1, 2 * D), F32).ap()
        b1_cols = nc.dram_tensor("b1_cols", (NEXP, P, FF // P), F32).ap()

        resid = sb("resid", [P, T, D])
        ident = sb("ident", [P, P])
        iota_row = sb("iota_row", [P, P])
        iota_col = sb("iota_col", [P, 1])
        ones = sb("ones", [P, P])
        valid = sb("valid", [P, T])
        iota_bf = sb("iota_bf", [P, P], BF16)
        ident_bf = sb("ident_bf", [P, P], BF16)
        adm = sb("adm", [P, T, 2 * H])
        adm_parts = sb("adm_parts", [P, T, 3, 2 * H], BF16)

        early = ExitStack()
        w_cat = sb("w_cat", [P, 2, 2 * D + 2 * D + 2 * H], ctx=early)
        wp_t = sb("wp_t", [P, 2, D], ctx=early)
        b_qkv = sb("b_qkv", [P, 3 * D], ctx=early)
        b_proj = sb("b_proj", [P, D], ctx=early)
        b_gnn = sb("b_gnn", [P, D], ctx=early)
        ss_scale = sb("ss_scale", [P, 2 * H], ctx=early)
        nrm_scale = sb("nrm_scale", [P, 2 * H], ctx=early)
        mv = sb("mv", [P, T, 2], ctx=early)
        rstd = sb("rstd", [P, T], ctx=early)
        nmr = sb("nmr", [P, T], ctx=early)
        a_s = sb("a_s", [P, T, H], ctx=early)
        mix_w = sb("mix_w", [P, H, FCH, V1], ctx=early)
        mix_tail = sb("mix_tail", [P, H // 2, 2 * V1], ctx=early)
        vsum_w = sb("vsum_w", [1, H * V1], ctx=early)
        W_Q = D + 2 * H

        with ExitStack() as c:
            raw = sb("raw", [P, 6, D], ctx=c)
            raw_w = sb("raw_w", [P, 2, D], ctx=c)
            raw_p = sb("raw_p", [P, 2, D], ctx=c)
            gw_t = sb("gw_t", [P, 2, D], ctx=c)
            att_bd = sb("att_bd", [P, 2, 2 * H], ctx=c)
            zrow = sb("zrow", [P, D], ctx=c)
            temp_b = sb("temp_b", [P, H], ctx=c)
            pad_i = sb("pad_i", [P, CHUNKS * CHUNK - E], I32, ctx=c)
            pad_s = sb("pad_s", [P, CHUNKS * CHUNK - E], I32, ctx=c)
            iota_i = sb("iota_i", [P, P], I32, ctx=c)
            iota_ci = sb("iota_ci", [P, 1], I32, ctx=c)
            b1_raw = sb("b1_raw", [NEXP * FF // P, P], ctx=c)
            b1_t = sb("b1_t", [P, NEXP * FF // P], ctx=c)
            st6 = sb("st6", [P, T, 6], ctx=c)
            pt = [ps(f"s1_pt{i}", [P, 512], c) for i in range(2)]
            pw = ps("s1_pw", [P, 512], c)
            x_zeroed = sem("x_zeroed", c)
            x_in = sem("x_in", c)
            x_rest_in = sem("x_rest_in", c)
            w_in = sem("w_in", c)
            b_in = sem("b_in", c)
            att_zeroed = sem("att_zeroed", c)
            att_in = sem("att_in", c)
            pads_set = sem("pads_set", c)
            scratch_out = sem("scratch_out", c)
            ident_ready = sem("ident_ready", c)
            turned = sem("turned", c)
            copied = sem("copied", c)
            b1_out = sem("b1_out", c)
            watt_ready = sem("watt_ready", c)
            iotas = sem("iotas", c)
            var_ready = sem("var_ready", c)
            std_ready = sem("std_ready", c)
            block = c.enter_context(nc.Block())

            turns = []
            for kc in range(2):
                for m in range(6):
                    turns.append((raw[:, m, kc * P:(kc + 1) * P],
                                  w_cat[:, kc, W_Q + m * P:W_Q + (m + 1) * P]))
                for m in range(2):
                    turns.append((raw_p[:, m, kc * P:(kc + 1) * P], wp_t[:, kc, m * P:(m + 1) * P]))
                    turns.append((raw_w[:, m, kc * P:(kc + 1) * P], gw_t[:, kc, m * P:(m + 1) * P]))

            @block.sync
            def _(sp):
                sp.wait_ge(x_zeroed, 1)
                for q in range(4):
                    n = NFULL // 4
                    sp.dma_start(resid[:, q * n:(q + 1) * n, :],
                                 x[q * n * P:(q + 1) * n * P, :].rearrange("(t p) f -> p t f", p=P)).then_inc(x_in, 16)
                sp.dma_start(resid[0:NREST, NFULL, :], x[NFULL * P:N, :]).then_inc(x_rest_in, 16)
                sp.dma_start(raw[:], Wqkv.rearrange("(m p) k -> p m k", p=P)).then_inc(w_in, 16)
                sp.dma_start(raw_w[:], gnn_W.rearrange("(m p) k -> p m k", p=P)).then_inc(w_in, 16)
                sp.dma_start(raw_p[:], Wproj.rearrange("(m p) k -> p m k", p=P)).then_inc(w_in, 16)
                sp.dma_start(b1_raw[:], b1.rearrange("e (c p) -> (e c) p", p=P)).then_inc(w_in, 16)
                sp.dma_start(w_cat[:, :, 0:D], gnn_W.rearrange("(c k) n -> k c n", k=P)).then_inc(w_in, 16)
                sp.wait_ge(att_zeroed, 1)
                for h in range(H):
                    p0 = (h % 4) * C
                    for k, a in enumerate((att_src, att_dst)):
                        sp.dma_start(att_bd[p0:p0 + C, h // 4, k * H + h:k * H + h + 1],
                                     a[h:h + 1, :].rearrange("a c -> c a")).then_inc(att_in, 16)
                sp.wait_ge(pads_set, 3)
                full = E // CHUNK
                rest = E - full * CHUNK
                for lst, pad, pads in ((src, src_pad, pad_s), (dst, dst_pad, pad_i)):
                    sp.dma_start(pad[0:full, :], lst[0:full * CHUNK].rearrange("(a b) -> a b", b=CHUNK)).then_inc(scratch_out, 16)
                    sp.dma_start(pad[full:full + 1, 0:rest], lst[full * CHUNK:E].unsqueeze(0)).then_inc(scratch_out, 16)
                    sp.dma_start(pad[full:full + 1, rest:CHUNK], pads[0:1, :]).then_inc(scratch_out, 16)
                sp.dma_start(slot_x.rearrange("(t p) f -> p t f", p=P),
                             zrow[:].unsqueeze(1).broadcast_to([P, SLOT_TILES, D])).then_inc(scratch_out, 16)
                sp.wait_ge(scratch_out, 7 * 16)
                sp.wait_ge(copied, len(turns) + 1)
                sp.dma_start(b1_cols.rearrange("e p c -> p e c"), b1_t[:].rearrange("p (e c) -> p e c", e=NEXP)).then_inc(b1_out, 16)
                sp.wait_ge(b1_out, 16)

            @block.gpsimd
            def _(pool):
                pool.memset(ident[:], 0.0)
                pool.memset(ones[:], 1.0)
                pool.memset(valid[:], 1.0)
                pool.iota(iota_i[:], [[1, P]], base=0, channel_multiplier=0)
                pool.iota(iota_ci[:], [[1, 1]], base=0, channel_multiplier=1).then_inc(iotas, 1)
                pool.drain()
                pool.affine_select(out=ident[:], in_=ident[:], compare_op=ALU.not_equal, fill=1.0, base=0,
                                   pattern=[[-1, P]], channel_multiplier=1).then_inc(ident_ready, 1)
                pool.affine_select(out=valid[:], in_=valid[:], compare_op=ALU.is_ge, fill=0.0, base=N - 1,
                                   pattern=[[-P, T]], channel_multiplier=-1)
                for ap, vec, n in ((b_qkv, bqkv, 3 * D), (b_proj, bproj, D), (b_gnn, gnn_bias, D)):
                    pool.dma_start(ap[:], bcast_rows(vec, n)).then_inc(b_in, 16)
                pool.dma_start(temp_b[:], bcast_rows(temperature.rearrange("a h b c -> (a h b c)"), H)).then_inc(b_in, 16)

            @block.vector
            def _(dve):
                dve.memset(resid[:, NFULL:T, :], 0.0).then_inc(x_zeroed, 1)
                dve.memset(att_bd[:], 0.0).then_inc(att_zeroed, 1)
                dve.memset(pad_s[:], 0).then_inc(pads_set, 1)
                dve.memset(pad_i[:], PAD_DST).then_inc(pads_set, 1)
                dve.memset(zrow[:], 0.0).then_inc(pads_set, 1)
                dve.memset(ss_scale[:, 0:H], SCALE * SCALE)
                dve.memset(ss_scale[:, H:2 * H], 1.0)
                dve.memset(nrm_scale[:, H:2 * H], SCALE)
                dve.wait_ge(iotas, 1)
                dve.tensor_copy(iota_row[:], iota_i[:])
                dve.tensor_copy(iota_bf[:], iota_i[:])
                dve.tensor_copy(iota_col[:], iota_ci[:])
                dve.wait_ge(ident_ready, 1)
                dve.tensor_copy(ident_bf[:], ident[:])
                dve.wait_ge(b_in, 4 * 16)
                dve.tensor_scalar(nrm_scale[:, 0:H], temp_b[:], SCALE * SCALE, None, ALU.mult)
                dve.wait_ge(x_in, 64)
                dve.wait_ge(x_rest_in, 16)
                with dve.Fori(0, T) as t:
                    dve.bn_stats(st6[:, bass.ds(t, 1), :], resid[:, bass.ds(t, 1), :])
                dve.drain()
                moments(dve, mv, st6)
                dve.tensor_scalar(rstd[:], mv[:, :, 1], LN_EPS, None, ALU.add).then_inc(var_ready, 1)
                dve.wait_ge(std_ready, 1)
                dve.reciprocal(rstd[:], rstd[:])
                dve.drain()
                dve.scalar_tensor_tensor(out=nmr[:], in0=mv[:, :, 0], scalar=-1.0, in1=rstd[:], op0=ALU.mult, op1=ALU.mult)

            @block.tensor
            def _(pe):
                pe.wait_ge(ident_ready, 1)
                pe.wait_ge(w_in, 5 * 16)
                for n, (a, _) in enumerate(turns):
                    if n >= 2:
                        pe.wait_ge(copied, n - 1)
                    pe.transpose(pt[n % 2][:, 0:P], a, ident[:]).then_inc(turned, 1)
                n = len(turns)
                pe.wait_ge(copied, n - 1)
                pe.transpose(pt[n % 2][:, 0:NEXP * FF // P], b1_raw[:], ident[0:NEXP * FF // P, 0:NEXP * FF // P]).then_inc(turned, 1)
                pe.wait_ge(copied, n)
                pe.wait_ge(att_in, 2 * H * 16)
                for m in range(2):
                    for kc in range(2):
                        mm = pe.matmul(pw[:, m * 2 * H:(m + 1) * 2 * H], gw_t[:, kc, m * P:(m + 1) * P], att_bd[:, kc, :],
                                       start=(kc == 0), stop=(kc == 1))
                mm.then_inc(watt_ready, 1)

            @block.scalar
            def _(act):
                for n, (_, b) in enumerate(turns):
                    act.wait_ge(turned, n + 1)
                    act.copy(b, pt[n % 2][:, 0:P]).then_inc(copied, 1)
                n = len(turns)
                act.wait_ge(turned, n + 1)
                act.copy(b1_t[:], pt[n % 2][:, 0:NEXP * FF // P]).then_inc(copied, 1)
                act.wait_ge(var_ready, 1)
                act.sqrt(rstd[:], rstd[:]).then_inc(std_ready, 1)
                act.wait_ge(watt_ready, 1)
                act.copy(w_cat[:, :, D:D + 2 * H], pw[:, 0:4 * H].rearrange("p (m a) -> p m a", m=2))

        def products(dve, feat, wrapped, u, done):
            if u < H:
                base = wrapped[:, u, 0:1]
                whole = [base.ap[0][0], P]
                dve.tensor_tensor(feat[:].rearrange("p (d i) -> p d i", i=C),
                                  bass.AP(base.tensor, base.offset, [whole, [0, DIAGS - 1], [1, C]]),
                                  bass.AP(base.tensor, base.offset, [whole, [1, DIAGS - 1], [1, C]]), ALU.mult).then_inc(done, 1)
            else:
                tail = feat[:].rearrange("p (h a i) -> p h a i", h=H, a=2)
                dve.tensor_tensor(tail[:, :, 0, :], wrapped[:, :, 0:C], wrapped[:, :, DIAGS - 1:WRAP], ALU.mult)
                dve.tensor_copy(tail[:, :, 1, :], wrapped[:, :, 0:C]).then_inc(done, 1)

        with ExitStack() as c:
            xn = [sb(f"xn{i}", [P, D], ctx=c) for i in range(2)]
            xt = [sb(f"xt{i}", [P, 2, P], ctx=c) for i in range(2)]
            row = [sb(f"row{i}", [P, ROW], ctx=c) for i in range(2)]
            qk = sb("qk", [P, 2 * D], ctx=c)
            sq = sb("sq", [P, 2 * D], ctx=c)
            nrm = sb("nrm", [P, 2 * H], ctx=c)
            qst = [sb(f"qst{i}", [P, D], ctx=c) for i in range(2)]
            kv = [sb(f"kv{i}", [P, 2 * D], ctx=c) for i in range(2)]
            km = [sb(f"km{i}", [P, D], ctx=c) for i in range(2)]
            vm = [sb(f"vm{i}", [P, D], ctx=c) for i in range(2)]
            vcol = [sb(f"vcol{i}", [P, 1], ctx=c) for i in range(2)]
            kk = [sb(f"kk{i}", [P, H, WRAP], ctx=c) for i in range(2)]
            feat = [sb(f"kfeat{i}", [P, FEAT], ctx=c) for i in range(3)]
            zeros = sb("zeros", [P, 512], ctx=c)
            vmask = sb("vmask", [P, T], ctx=c)
            main_sb = [sb(f"main_sb{i}", [P, FEAT], ctx=c) for i in range(2)]
            tg_sb = sb("tg_sb", [P, 3 * P], ctx=c)
            sum_sb = sb("sum_sb", [1, 2 * D], ctx=c)
            gcol = sb("gcol", [P, H, FCH], ctx=c)
            gtail = sb("gtail", [P, H // 2], ctx=c)
            coef = sb("coef", [P, FCH], ctx=c)
            p_t = ps("p_t", [P, 512], c)
            p_row = ps("p_row", [P, 512], c)
            p_qk = ps("p_qk", [P, 512], c)
            p_main = [ps(f"p_main{i}", [P, 512], c) for i in range(2)]
            p_tg = ps("p_tg", [P, 512], c)
            p_sum = ps("p_sum", [P, 512], c)
            p_v = ps("p_v", [P, 512], c)
            TAILW = 2 * C
            zeroed = sem("zeroed", c)
            xn_ready = sem("xn_ready", c)
            xt_in_psum = sem("xt_in_psum", c)
            xt_ready = sem("xt_ready", c)
            projected = sem("projected", c)
            row_ready = sem("row_ready", c)
            qkv_taken = sem("qkv_taken", c)
            kv_ready = sem("kv_ready", c)
            squares_ready = sem("squares_ready", c)
            norms_ready = sem("norms_ready", c)
            q_ready = sem("q_ready", c)
            feat_ready = sem("feat_ready", c)
            feat_used = sem("feat_used", c)
            row_out = [sem(f"row_out{i}", c) for i in range(2)]
            q_out = [sem(f"q_out{i}", c) for i in range(2)]
            sums_ready = sem("sums_ready", c)
            sums_out = sem("sums_out", c)
            gcol_in = sem("gcol_in", c)
            main_turned = sem("main_turned", c)
            block = c.enter_context(nc.Block())

            @block.scalar
            def _(act):
                def take_row(t, s):
                    act.wait_ge(projected, t + 1)
                    wait(act, row_out[s], (t - s) * 8)
                    act.copy(row[s][:], p_row[:, 0:ROW])
                    act.copy(a_s[:, bass.ds(t, 1), :], p_row[:, D:D + H].unsqueeze(1))
                    act.copy(adm[:, bass.ds(t, 1), 0:H], p_row[:, ROW:ROW + H].unsqueeze(1)).then_inc(row_ready, 1)

                def root(t):
                    act.wait_ge(squares_ready, t + 1)
                    act.sqrt(nrm[:], nrm[:]).then_inc(norms_ready, 1)

                def body(t, s):
                    wait(act, xt_in_psum, t - 1)
                    act.activation(xn[s][:], resid[:, bass.ds(t, 1), :].rearrange("p a f -> p (a f)"), ACT.Identity,
                                   bias=nmr[:, bass.ds(t, 1)], scale=rstd[:, bass.ds(t, 1)]).then_inc(xn_ready, 1)
                    if not (isinstance(t, int) and t == 0):
                        take_row(t - 1, 1 - s)
                    act.wait_ge(xt_in_psum, t + 1)
                    wait(act, projected, t - 1)
                    act.copy(xt[s][:], p_t[:, 0:D].rearrange("p (a b) -> p a b", a=2)).then_inc(xt_ready, 1)
                    if not (isinstance(t, int) and t == 0):
                        root(t - 1)

                pairs(act, T, body)
                take_row(T - 1, 1)
                root(T - 1)
                act.wait_ge(feat_used, T * UNITS)
                act.copy(main_sb[0][:], p_main[0][:])
                act.copy(main_sb[1][:], p_main[1][:])
                act.copy(tg_sb[:], p_tg[:, 0:3 * P])
                act.copy(sum_sb[:], p_sum[0:1, :]).then_inc(sums_ready, 1)

            @block.tensor
            def _(pe):
                pe.wait_ge(zeroed, 1)
                for bank in p_main + [p_tg, p_sum]:
                    pe.matmul(bank[:], zeros[:, 0:P], zeros[:], start=True, stop=False, skip_group_check=True)

                def add_sum(o, w, x):
                    return pe.matmul(o, w, x, start=False, stop=False, skip_group_check=True)

                def kv_sums(t, s):
                    pe.wait_ge(kv_ready, t + 1)
                    add_sum(p_sum[0:1, :], vcol[s][:], kv[s][:])
                    for g in range(2):
                        add_sum(p_tg[:, (1 + g) * P:(2 + g) * P], km[s][:, g * P:(g + 1) * P], kv[s][:, g * P:(g + 1) * P])
                    for u in range(UNITS):
                        pe.wait_ge(feat_ready, t * UNITS + (u + 1))
                        if u < H:
                            j = u % 4
                            mm = add_sum(p_main[u // 4][j * C:(j + 1) * C, :], vm[s][:, u * C:(u + 1) * C], feat[u % 3][:])
                        else:
                            for h in range(H):
                                j, g = h % 4, h // 4
                                mm = add_sum(p_tg[j * C:(j + 1) * C, g * TAILW:(g + 1) * TAILW], vm[s][:, h * C:(h + 1) * C],
                                             feat[u % 3][:, h * TAILW:(h + 1) * TAILW])
                        mm.then_inc(feat_used, 1)

                def body(t, s):
                    pe.wait_ge(xn_ready, t + 1)
                    wait(pe, xt_ready, t)
                    pe.transpose(p_t[:, 0:P], xn[s][:, 0:P], ident[:])
                    pe.transpose(p_t[:, P:D], xn[s][:, P:D], ident[:]).then_inc(xt_in_psum, 1)
                    if not (isinstance(t, int) and t == 0):
                        kv_sums(t - 1, 1 - s)
                    pe.wait_ge(xt_ready, t + 1)
                    wait(pe, row_ready, t)
                    wait(pe, qkv_taken, t)
                    for o, lo, hi in ((p_row[:, 0:W_Q], 0, W_Q), (p_qk[:], W_Q, W_Q + 2 * D), (p_v[:, 0:D], W_Q + 2 * D, W_Q + 3 * D)):
                        for kc in range(2):
                            mm = pe.matmul(o, xt[s][:, kc, :], w_cat[:, kc, lo:hi], start=(kc == 0), stop=(kc == 1))
                    mm.then_inc(projected, 1)

                pairs(pe, T, body)
                kv_sums(T - 1, 1)
                pe.wait_ge(sums_ready, 1)
                for g, bank in enumerate((p_row, p_qk)):
                    for m in range(FCH):
                        pe.transpose(bank[:, m * P:(m + 1) * P], main_sb[g][:, m * P:(m + 1) * P], ident[:])
                pe.transpose(p_v[:, 0:P], tg_sb[:, 0:P], ident[:]).then_inc(main_turned, 1)

            @block.vector
            def _(dve):
                dve.memset(zeros[:], 0.0).then_inc(zeroed, 1)
                dve.tensor_scalar(vmask[:], valid[:], 1.0 / N, None, ALU.mult)
                dve.memset(mix_tail[:], 0.0)
                dve.memset(vsum_w[:], SCALE ** 4 * C_COEF)
                dve.memset(coef[:], 2 * A_COEF)
                dve.drain()
                dve.memset(coef[0:C, 0:1], A_COEF)
                dve.drain()

                def body(t, s):
                    dve.wait_ge(projected, t + 1)
                    dve.tensor_tensor(qk[:], p_qk[:], b_qkv[:, 0:2 * D], ALU.add)
                    wait(dve, feat_used, t * UNITS - UNITS)
                    dve.tensor_tensor(kv[s][:, D:2 * D], p_v[:, 0:D], b_qkv[:, 2 * D:3 * D], ALU.add).then_inc(qkv_taken, 1)
                    dve.drain()
                    dve.tensor_tensor(sq[:], qk[:], qk[:], ALU.mult)
                    dve.drain()
                    dve.tensor_reduce(nrm[:], sq[:].rearrange("p (h e) -> p h e", e=C), AXX, ALU.add)
                    dve.drain()
                    dve.tensor_tensor(nrm[:], nrm[:], ss_scale[:], ALU.mult).then_inc(squares_ready, 1)
                    dve.tensor_scalar(vm[s][:], kv[s][:, D:2 * D], vmask[:, bass.ds(t, 1)], None, ALU.mult)
                    dve.tensor_copy(vcol[s][:], vmask[:, bass.ds(t, 1)])
                    dve.wait_ge(norms_ready, t + 1)
                    dve.tensor_scalar(nrm[:], nrm[:], NORM_EPS, None, ALU.max)
                    dve.drain()
                    dve.reciprocal(nrm[:], nrm[:])
                    dve.drain()
                    dve.tensor_tensor(nrm[:], nrm[:], nrm_scale[:], ALU.mult)
                    dve.drain()
                    k3 = qk[:, D:2 * D].rearrange("p (h e) -> p h e", h=H)
                    kn = nrm[:, H:2 * H].unsqueeze(2).broadcast_to([P, H, C])
                    dve.tensor_tensor(kk[s][:, :, 0:C], k3, kn, ALU.mult)
                    dve.drain()
                    dve.tensor_copy(kk[s][:, :, C:WRAP], kk[s][:, :, 0:WRAP - C])
                    dve.tensor_copy(kv[s][:, 0:D].rearrange("p (h e) -> p h e", h=H), kk[s][:, :, 0:C])
                    dve.tensor_scalar(km[s][:].rearrange("p (h e) -> p h e", h=H), kk[s][:, :, 0:C], vmask[:, bass.ds(t, 1)], None, ALU.mult).then_inc(kv_ready, 1)
                    dve.drain()
                    for u in range(UNITS):
                        wait(dve, feat_used, t * UNITS + (u - 2))
                        products(dve, feat[u % 3], kk[s], u, feat_ready)
                    wait(dve, q_out[s], (t - s) * 8)
                    dve.tensor_tensor(qst[s][:].rearrange("p (h e) -> p h e", h=H), qk[:, 0:D].rearrange("p (h e) -> p h e", h=H),
                                      nrm[:, 0:H].unsqueeze(2).broadcast_to([P, H, C]), ALU.mult).then_inc(q_ready, 1)
                    dve.drain()

                pairs(dve, T, body)
                dve.wait_ge(sums_ready, 1)
                dve.tensor_scalar(vsum_w[:].rearrange("p (h e) -> p h e", h=H)[:, :, 1:V1],
                                  sum_sb[:, D:2 * D].rearrange("p (h e) -> p h e", h=H), SCALE ** 4 * C_COEF, None, ALU.mult)
                dve.wait_ge(main_turned, 1)
                for g, bank in enumerate((p_row, p_qk)):
                    for m in range(FCH):
                        dve.tensor_scalar(mix_w[:, 4 * g:4 * g + 4, m, 1:V1], bank[:, m * P:(m + 1) * P].rearrange("p (j e) -> p j e", j=4),
                                          coef[:, m:m + 1], None, ALU.mult)
                tails = (A_COEF, SCALE ** 2 * B_COEF)
                for h in range(H):
                    for a, k in enumerate(tails):
                        p0, q0 = (h % 2) * TAILW + a * C, (h // 4) * TAILW + a * C
                        dve.tensor_scalar(mix_tail[p0:p0 + C, h // 2, (h % 2) * V1 + 1:(h % 2 + 1) * V1],
                                          p_v[q0:q0 + C, (h % 4) * C:(h % 4 + 1) * C], k, None, ALU.mult)
                dve.wait_ge(gcol_in, (4 + 4 * FCH) * 16)
                dve.tensor_tensor(mix_w[:, :, :, 0], gcol[:], coef[:].unsqueeze(1).broadcast_to([P, H, FCH]), ALU.mult)
                for hh in range(2):
                    for a, k in enumerate(tails):
                        p0 = hh * TAILW + a * C
                        dve.tensor_scalar(mix_tail[p0:p0 + C, :, hh * V1], gtail[p0:p0 + C, :], k, None, ALU.mult)

            @block.sync
            def _(sp):
                def body(t, s):
                    sp.wait_ge(row_ready, t + 1)
                    sp.dma_start(node_rows[bass.ts(t, P), :], row[s][:]).then_inc(row_out[s], 16)
                    sp.wait_ge(q_ready, t + 1)
                    sp.dma_start(qn_dram[bass.ts(t, P), :], qst[s][:]).then_inc(q_out[s], 16)

                pairs(sp, T, body)
                for s in range(2):
                    sp.wait_ge(row_out[s], T // 2 * 16)
                    sp.wait_ge(q_out[s], T // 2 * 16)
                sp.wait_ge(sums_ready, 1)
                for h in range(H):
                    j, g = h % 4, h // 4
                    blk = tg_sb[j * C:(j + 1) * C, (1 + g) * P + j * C:(1 + g) * P + (j + 1) * C]
                    for half in range(2):
                        sp.dma_start(gram_dram[h, :, half * C:(half + 1) * C], blk).then_inc(sums_out, 16)
                sp.dma_start(sums_dram, sum_sb[:]).then_inc(sums_out, 16)
                sp.wait_ge(sums_out, (2 * H + 1) * 16)
                gt, st = gram_dram.tensor, sums_dram.tensor
                HW = C * 2 * C
                for dd in range(4):
                    for m in range(FCH):
                        sp.dma_start(gcol[dd * C:(dd + 1) * C, :, m], bass.AP(gt, dd + 4 * m, [[2 * C + 1, C], [HW, H]]),
                                     allow_slow_non_contiguous=True).then_inc(gcol_in, 16)
                for hh in range(2):
                    sp.dma_start(gtail[hh * TAILW:hh * TAILW + C, :], bass.AP(gt, hh * HW + DIAGS - 1, [[2 * C + 1, C], [2 * HW, H // 2]]),
                                 allow_slow_non_contiguous=True).then_inc(gcol_in, 16)
                    sp.dma_start(gtail[hh * TAILW + C:(hh + 1) * TAILW, :], bass.AP(st, hh * C, [[1, C], [2 * C, H // 2]]),
                                 allow_slow_non_contiguous=True).then_inc(gcol_in, 16)

        G4 = 4
        SP_ = G4 * P
        acc = sb("acc", [P, T, ROW], ctx=early)
        src_t = sb("src_t", [P, SP_, TILES_PER_CHUNK], I32, ctx=early)
        dst_t = sb("dst_t", [P, SP_, TILES_PER_CHUNK], ctx=early)
        blk_row = sb("blk_row", [1, SP_], I32, ctx=early)
        with ExitStack() as c:
            fd = sb("fd", [1, CHUNKS], I32, ctx=c)
            fdf = sb("fdf", [1, CHUNKS], ctx=c)
            ci = sb("ci", [1, CHUNKS], I32, ctx=c)
            cf = sb("cf", [1, CHUNKS], ctx=c)
            scol = sb("scol", [P, G4], ctx=c)
            cmp = sb("cmp", [P, G4, CHUNKS], ctx=c)
            ccol = sb("ccol", [P, G4], ctx=c)
            bcol = sb("bcol", [P, G4], ctx=c)
            b128 = sb("b128", [P, G4], ctx=c)
            cidx = sb("cidx", [P, G4], I32, ctx=c)
            s_rows = [sb(f"s_rows{i}", [P, CHUNK], I32, ctx=c) for i in range(G4)]
            d_rows = [sb(f"d_rows{i}", [P, CHUNK], I32, ctx=c) for i in range(G4)]
            s_f = sb("s_f", [P, CHUNK], ctx=c)
            d_f = sb("d_f", [P, CHUNK], ctx=c)
            gmax = sb("gmax", [P, H], ctx=c)
            gmax_all = sb("gmax_all", [P, H], ctx=c)
            shift = sb("shift", [P, T, H], ctx=c)
            p_g = ps("p_g", [P, 512], c)
            p_b = ps("p_b", [P, 512], c)
            p_s = ps("p_s", [P, 512], c)
            p_d = ps("p_d", [P, 512], c)
            first_in = sem("first_in", c)
            chunk_nr = sem("chunk_nr", c)
            g_ready = sem("g_ready", c)
            g_spread = sem("g_spread", c)
            b_ready = sem("b_ready", c)
            b_turned = sem("b_turned", c)
            rows_in = [sem(f"rows_in{i}", c) for i in range(G4)]
            rows_ready = sem("rows_ready", c)
            rows_turned = sem("rows_turned", c)
            lists_ready = sem("lists_ready", c)
            gmax_part = sem("gmax_part", c)
            gmax_ready = sem("gmax_ready", c)
            block = c.enter_context(nc.Block())

            @block.sync
            def _(sp):
                sp.dma_start(fd[:], dst_pad[:, 0:1].rearrange("c a -> a c"), allow_slow_non_contiguous=True).then_inc(first_in, 16)

            @block.gpsimd
            def _(pool):
                pool.iota(ci[:], [[1, CHUNKS]], base=0, channel_multiplier=0).then_inc(chunk_nr, 1)
                pool.wait_ge(gmax_part, 1)
                pool.partition_all_reduce(gmax_all[:], gmax[:], P, RMAX).then_inc(gmax_ready, 1)
                pool.wait_ge(b_ready, 1)
                for g in range(G4):
                    pool.indirect_dma_start(s_rows[g][:], None, src_pad, bass.IndirectOffsetOnAxis(ap=cidx[:, g:g + 1], axis=0)).then_inc(rows_in[g], 16)
                    pool.indirect_dma_start(d_rows[g][:], None, dst_pad, bass.IndirectOffsetOnAxis(ap=cidx[:, g:g + 1], axis=0)).then_inc(rows_in[g], 16)

            @block.vector
            def _(dve):
                dve.tensor_reduce(gmax[:], a_s[:].rearrange("p t h -> p h t"), AXX, ALU.max).then_inc(gmax_part, 1)
                dve.wait_ge(first_in, 16)
                dve.wait_ge(chunk_nr, 1)
                dve.tensor_scalar(fd[:], fd[:], P.bit_length() - 1, None, ALU.arith_shift_right)
                dve.tensor_copy(cf[:], ci[:])
                for g in range(G4):
                    dve.tensor_scalar(scol[:, g:g + 1], iota_col[:], float(g * P), None, ALU.add)
                dve.drain()
                dve.tensor_copy(fdf[:], fd[:])
                dve.drain()
                dve.tensor_tensor(fdf[:], fdf[:], cf[:], ALU.add).then_inc(g_ready, 1)
                dve.wait_ge(g_spread, 1)
                for g in range(G4):
                    dve.tensor_scalar(cmp[:, g, 1:CHUNKS], p_g[:, 1:CHUNKS], scol[:, g:g + 1], None, ALU.is_le)
                dve.drain()
                dve.tensor_reduce(ccol[:], cmp[:, :, 1:CHUNKS], AXX, ALU.add)
                dve.drain()
                dve.tensor_copy(cidx[:], ccol[:])
                dve.tensor_tensor(bcol[:], scol[:], ccol[:], ALU.subtract)
                dve.drain()
                dve.tensor_scalar(b128[:], bcol[:], float(P), None, ALU.mult).then_inc(b_ready, 1)
                dve.wait_ge(gmax_ready, 1)
                dve.tensor_tensor(shift[:], adm[:, :, 0:H], gmax_all[:].unsqueeze(1).broadcast_to([P, T, H]), ALU.add)
                dve.memset(acc[:], 0.0)
                dve.drain()
                dve.scalar_tensor_tensor(out=adm[:, :, H:2 * H], in0=shift[:], scalar=SLOPE, in1=shift[:], op0=ALU.mult, op1=ALU.max)
                dve.drain()
                for part in range(3):
                    dve.tensor_copy(adm_parts[:, :, part, :], adm[:])
                    dve.drain()
                    if part < 2:
                        dve.tensor_tensor(adm[:], adm[:], adm_parts[:, :, part, :], ALU.subtract)
                        dve.drain()
                dve.wait_ge(b_turned, 1)
                dve.tensor_scalar(blk_row[:], p_b[0:1, :], float(T - 1), None, ALU.min)
                for g in range(G4):
                    dve.wait_ge(rows_in[g], 32)
                    wait(dve, rows_turned, g)
                    dve.tensor_copy(s_f[:], s_rows[g][:])
                    dve.tensor_copy(d_f[:], d_rows[g][:])
                    dve.drain()
                    dve.tensor_scalar(d_f[:], d_f[:], b128[:, g:g + 1], None, ALU.subtract).then_inc(rows_ready, 1)
                    dve.wait_ge(rows_turned, g + 1)
                    dve.tensor_copy(src_t[:, g * P:(g + 1) * P, :].rearrange("p s u -> p u s"), p_s[:].rearrange("p (u s) -> p u s", u=4))
                    dve.tensor_copy(dst_t[:, g * P:(g + 1) * P, :].rearrange("p s u -> p u s"), p_d[:].rearrange("p (u s) -> p u s", u=4)).then_inc(lists_ready, 1)

            @block.tensor
            def _(pe):
                pe.wait_ge(g_ready, 1)
                pe.matmul(p_g[:, 0:CHUNKS], ones[0:1, :], fdf[:], start=True, stop=True).then_inc(g_spread, 1)
                pe.wait_ge(b_ready, 1)
                for g in range(G4):
                    mm = pe.matmul(p_b[0:1, g * P:(g + 1) * P], bcol[:, g:g + 1], ident[:], start=True, stop=True)
                mm.then_inc(b_turned, 1)
                for g in range(G4):
                    pe.wait_ge(rows_ready, g + 1)
                    wait(pe, lists_ready, g)
                    for bank, f in ((p_s, s_f), (p_d, d_f)):
                        for u in range(TILES_PER_CHUNK):
                            mm = pe.transpose(bank[:, u * P:(u + 1) * P], f[:, u * P:(u + 1) * P], ident[:])
                    mm.then_inc(rows_turned, 1)

        TC = TILES_PER_CHUNK
        with ExitStack() as c:
            idx = [sb(f"idx{i}", [P, TC], I32, ctx=c) for i in range(R)]
            msg = [sb(f"msg{i}", [P, TC, ROW], ctx=c) for i in range(R)]
            sel_bf = [sb(f"sel_bf{i}", [P, TC, P], BF16, ctx=c) for i in range(2)]
            sel = [sb(f"sel{i}", [P, TC * P], ctx=c) for i in range(R)]
            sel_t = [sb(f"sel_t{i}", [P, TC * P], BF16, ctx=c) for i in range(2)]
            lg = [sb(f"lg{i}", [P, TC, H], ctx=c) for i in range(2)]
            qs = sb("qs", [P, D], ctx=c)
            qq = sb("qq", [P, H, WRAP], ctx=c)
            feat = [sb(f"qfeat{i}", [P, FEAT], ctx=c) for i in range(3)]
            feat_t = [sb(f"qfeat_t{i}", [P, FEAT], ctx=c) for i in range(3)]
            ry = sb("ry", [P, H], ctx=c)
            yn = sb("yn", [P, D], ctx=c)
            yt = sb("yt", [P, D], ctx=c)
            p_st = c.enter_context(nc.psum_tensor("p_st", [P, 2 * TC * P], BF16))
            p_m = [ps(f"p_m{i}", [P, 512], c) for i in range(2)]
            p_ft = [ps(f"p_ft{i}", [P, 512], c) for i in range(2)]
            p_y = ps("p_y", [P, 512], c)
            p_o = ps("p_o", [P, 512], c)
            p_eb = ps("p_e", [P, 512], c)
            q_in = sem("q_in", c)
            q_doubled = sem("q_doubled", c)
            feat_ready = sem("qfeat_ready", c)
            feat_turned = sem("feat_turned", c)
            feat_t_ready = sem("feat_t_ready", c)
            feat_t_used = sem("feat_t_used", c)
            y_taken = sem("y_taken", c)
            yt_in_psum = sem("yt_in_psum", c)
            yt_ready = sem("yt_ready", c)
            mix_ready = sem("mix_ready", c)
            mix_added = sem("mix_added", c)
            idx_ready = sem("idx_ready", c)
            gather_opened = sem("gather_opened", c)
            gathered = [sem(f"gathered{i}", c) for i in range(R)]
            sel_ready = sem("sel_ready", c)
            sel_wide = sem("sel_wide", c)
            sel_turned = sem("sel_turned", c)
            sel_t_ready = sem("sel_t_ready", c)
            dst_spread = sem("dst_spread", c)
            logit_ready = sem("logit_ready", c)
            weight_ready = sem("weight_ready", c)
            msg_ready = sem("msg_ready", c)
            msg_summed = sem("msg_summed", c)
            acc_added = sem("acc_added", c)
            block = c.enter_context(nc.Block())
            AHEAD = R - 1

            def rounds(eng, body):
                for k in range(OCT):
                    body(k, k, 0, None)
                with eng.Fori(1, T) as i:
                    for k in range(OCT):
                        body(i * OCT + k, k, i, i - 1)
                for k in range(OCT):
                    body(T * OCT + k, k, None, T - 1)
                with eng.Fori(T + 1, STEPS // OCT) as i:
                    for k in range(OCT):
                        body(i * OCT + k, k, None, None)

            def units(k):
                return (H - 1, H) if k == OCT - 1 else (k,)

            def pe_st(j):
                return p_st[:, (j % 2) * TC * P:(j % 2 + 1) * TC * P]

            def p_e(j):
                return p_eb[:, (j % 2) * TC * 2 * H:(j % 2 + 1) * TC * 2 * H]

            @block.gpsimd
            def _(pool):
                def body(s, j):
                    wait(pool, msg_summed, s - (R - 1))
                    pool.wait_ge(idx_ready, s + 1)
                    pool.sem_inc(gather_opened, 1)
                    for u in range(TC):
                        pool.indirect_dma_start(msg[j][:, u, :], None, node_rows,
                                                bass.IndirectOffsetOnAxis(ap=idx[j][:, u:u + 1], axis=0)).then_inc(gathered[j], 16)
                ring(pool, STEPS, R, body)

            @block.sync
            def _(sp):
                sp.dma_start(qs[:], qn_dram[0:P, :]).then_inc(q_in, 16)
                with sp.Fori(1, T) as t:
                    sp.wait_ge(q_doubled, t)
                    sp.dma_start(qs[:], qn_dram[bass.ts(t, P), :]).then_inc(q_in, 16)

            @block.scalar
            def _(act):
                def index(s, j):
                    if not (isinstance(s, int) and s < R):
                        act.wait_ge(gathered[j], (s - j) * (16 * TC // R))
                    act.copy(idx[j][:], src_t[:, bass.ds(s, 1), :].rearrange("p s u -> p (s u)")).then_inc(idx_ready, 1)

                def widen(s, j):
                    act.wait_ge(sel_ready, s + 1)
                    wait(act, msg_summed, s - (R - 1))
                    act.copy(sel[j][:], sel_bf[j % 2][:].rearrange("p u d -> p (u d)")).then_inc(sel_wide, 1)
                    act.wait_ge(sel_turned, s + 1)
                    wait(act, dst_spread, s - 1)
                    act.copy(sel_t[j % 2][:], pe_st(j)).then_inc(sel_t_ready, 1)

                def take(n, u):
                    act.wait_ge(feat_turned, n + 1)
                    wait(act, feat_t_used, n - 2)
                    act.copy(feat_t[u % 3][:], p_ft[u % 2][:]).then_inc(feat_t_ready, 1)

                def body(s, k, tile, last):
                    j = k % R
                    index(s + AHEAD, (j + AHEAD) % R)
                    widen(s + 1, (j + 1) % R)
                    act.wait_ge(logit_ready, s + 1)
                    act.activation(msg[j][:, :, D:ROW], lg[j % 2][:], ACT.Exp).then_inc(weight_ready, 1)
                    if last is not None and k == 3:
                        act.wait_ge(yt_in_psum, last + 1)
                        act.copy(yt[:], p_o[:, 0:D]).then_inc(yt_ready, 1)
                    if tile is not None:
                        for u in units(k):
                            take(tile * UNITS + u, u)

                for s in range(AHEAD):
                    index(s, s)
                widen(0, 0)
                rounds(act, body)

            @block.vector
            def _(dve):
                def select(s, j):
                    wait(dve, sel_wide, s - 1)
                    wait(dve, sel_turned, s - 1)
                    for u in range(TC):
                        a = dve.tensor_scalar(sel_bf[j % 2][:, u, :], iota_bf[:], dst_t[:, bass.ds(s, 1), u:u + 1].rearrange("p s u -> p (s u)"),
                                              None, ALU.is_equal)
                    a.then_inc(sel_ready, 1)

                def accumulate(s, j):
                    b = dve.value_load(blk_row[0:1, bass.ds(s, 1)], min_val=0, max_val=T - 1)
                    a = acc[:, bass.ds(b, 1), :].rearrange("p a f -> p (a f)")
                    dve.wait_ge(msg_summed, s + 1)
                    dve.tensor_tensor(a, a, p_m[j % 2][:, 0:ROW], ALU.add).then_inc(acc_added, 1)

                def query(k, tile, last):
                    if last is not None and k == 1:
                        dve.wait_ge(feat_t_used, last * UNITS + UNITS)
                        y3 = p_y[:, 0:H * V1].rearrange("p (h e) -> p h e", h=H)
                        dve.reciprocal(ry[:], y3[:, :, 0])
                        dve.drain()
                        dve.tensor_tensor(yn[:].rearrange("p (h e) -> p h e", h=H), y3[:, :, 1:V1],
                                          ry[:].unsqueeze(2).broadcast_to([P, H, C]), ALU.mult).then_inc(y_taken, 1)
                    if last is not None and k == 5:
                        r = resid[:, bass.ds(last, 1), :].rearrange("p a f -> p (a f)")
                        dve.wait_ge(mix_ready, last + 1)
                        dve.tensor_tensor(r, r, p_o[:, 0:D], ALU.add).then_inc(mix_added, 1)
                        dve.drain()
                        dve.tensor_tensor(r, r, b_proj[:], ALU.add)
                    if tile is not None:
                        if k == 0:
                            dve.wait_ge(q_in, tile * 16 + 16)
                            dve.tensor_copy(qq[:, :, 0:C], qs[:].rearrange("p (h e) -> p h e", h=H))
                            dve.tensor_copy(qq[:, :, C:WRAP], qs[:].rearrange("p (h e) -> p h e", h=H)[:, :, 0:WRAP - C]).then_inc(q_doubled, 1)
                            dve.drain()
                        for u in units(k):
                            wait(dve, feat_turned, tile * UNITS + (u - 2))
                            products(dve, feat[u % 3], qq, u, feat_ready)

                def body(s, k, tile, last):
                    j = k % R
                    select(s + 1, j + 1)
                    dve.wait_ge(gathered[j], (s - j) * (16 * TC // R) + 16 * TC)
                    dve.wait_ge(dst_spread, s + 1)
                    pe3 = p_e(j).rearrange("p (u a) -> p u a", u=TC)
                    l = lg[j % 2]
                    dve.tensor_tensor(l[:], msg[j][:, :, D:ROW], pe3[:, :, 0:H], ALU.add)
                    dve.drain()
                    dve.scalar_tensor_tensor(out=l[:], in0=l[:], scalar=SLOPE, in1=l[:], op0=ALU.mult, op1=ALU.max)
                    dve.drain()
                    dve.tensor_tensor(l[:], l[:], pe3[:, :, H:2 * H], ALU.subtract).then_inc(logit_ready, 1)
                    if not (isinstance(s, int) and s < 2):
                        accumulate(s - 2, j - 2)
                    query(k, tile, last)
                    dve.wait_ge(weight_ready, s + 1)
                    m4 = msg[j][:, :, 0:D].rearrange("p u (h e) -> p u h e", h=H)
                    dve.tensor_tensor(m4, m4, msg[j][:, :, D:ROW].unsqueeze(3).broadcast_to([P, TC, H, C]), ALU.mult).then_inc(msg_ready, 1)

                select(0, 0)
                rounds(dve, body)
                for s in (STEPS - 2, STEPS - 1):
                    dve.drain()
                    accumulate(s, s % R)
                dve.drain()

            @block.tensor
            def _(pe):
                def turn(s, j):
                    pe.wait_ge(sel_ready, s + 1)
                    wait(pe, sel_t_ready, s)
                    for u in range(TC):
                        mm = pe.transpose(pe_st(j)[:, u * P:(u + 1) * P], sel_bf[j % 2][:, u, :], ident_bf[:])
                    mm.then_inc(sel_turned, 1)

                def spread(s, j):
                    b = pe.value_load(blk_row[0:1, bass.ds(s, 1)], min_val=0, max_val=T - 1)
                    wait(pe, logit_ready, s)
                    pe.wait_ge(sel_t_ready, s + 1)
                    for u in range(TC):
                        for part in range(3):
                            mm = pe.matmul(p_e(j)[:, u * 2 * H:(u + 1) * 2 * H], sel_t[j % 2][:, u * P:(u + 1) * P],
                                           adm_parts[:, bass.ds(b, 1), part, :].rearrange("p a f -> p (a f)"), start=(part == 0), stop=(part == 2))
                    mm.then_inc(dst_spread, 1)

                def aggregate(s, j):
                    wait(pe, acc_added, s - 1)
                    pe.wait_ge(msg_ready, s + 1)
                    pe.wait_ge(sel_wide, s + 1)
                    for u in range(TC):
                        mm = pe.matmul(p_m[j % 2][:, 0:ROW], sel[j][:, u * P:(u + 1) * P], msg[j][:, u, :], start=(u == 0), stop=(u == TC - 1))
                    mm.then_inc(msg_summed, 1)

                def turn_features(n, u):
                    pe.wait_ge(feat_ready, n + 1)
                    wait(pe, feat_t_ready, n if u == 0 else n - 1)
                    for m in range(FCH):
                        mm = pe.transpose(p_ft[u % 2][:, m * P:(m + 1) * P], feat[u % 3][:, m * P:(m + 1) * P], ident[:])
                    mm.then_inc(feat_turned, 1)

                def sum_features(tile, u):
                    if u == 0:
                        wait(pe, y_taken, tile)
                        pe.matmul(p_y[:, 0:H * V1], ones[0:1, :], vsum_w[:], start=True, stop=False, skip_group_check=True)
                    pe.wait_ge(feat_t_ready, tile * UNITS + (u + 1))
                    for m in range(FCH):
                        if u < H:
                            o, w = p_y[:, u * V1:(u + 1) * V1], mix_w[:, u, m, :]
                        else:
                            o, w = p_y[:, 2 * m * V1:(2 * m + 2) * V1], mix_tail[:, m, :]
                        mm = pe.matmul(o, feat_t[u % 3][:, m * P:(m + 1) * P], w, start=False, stop=(u == H and m == FCH - 1),
                                       skip_group_check=True)
                    mm.then_inc(feat_t_used, 1)

                def body(s, k, tile, last):
                    j = k % R
                    turn(s + 1, j + 1)
                    if not (isinstance(s, int) and s == 0):
                        aggregate(s - 1, (j - 1) % R)
                    if last is not None:
                        if k == 0:
                            sum_features(last, H)
                        if k == 2:
                            pe.wait_ge(y_taken, last + 1)
                            wait(pe, mix_added, last)
                            for m in range(2):
                                mm = pe.transpose(p_o[:, m * P:(m + 1) * P], yn[:, m * P:(m + 1) * P], ident[:])
                            mm.then_inc(yt_in_psum, 1)
                        if k == 4:
                            pe.wait_ge(yt_ready, last + 1)
                            for m in range(2):
                                mm = pe.matmul(p_o[:, 0:D], yt[:, m * P:(m + 1) * P], wp_t[:, m, :], start=(m == 0), stop=(m == 1))
                            mm.then_inc(mix_ready, 1)
                    if tile is not None:
                        for u in units(k):
                            turn_features(tile * UNITS + u, u)
                            if u == units(k)[0]:
                                spread(s + 1, j + 1)
                            if u:
                                sum_features(tile, u - 1)
                    else:
                        spread(s + 1, j + 1)

                turn(0, 0)
                spread(0, 0)
                rounds(pe, body)
                aggregate(STEPS - 1, (STEPS - 1) % R)

        with ExitStack() as c:
            block = c.enter_context(nc.Block())

            @block.vector
            def _(dve):
                w = acc[:, :, D:ROW]
                dve.tensor_scalar(w, w, TINY, None, ALU.max)
                dve.drain()
                dve.reciprocal(w, w)
                dve.drain()
                with dve.Fori(0, T) as t:
                    a = acc[:, bass.ds(t, 1), 0:D].rearrange("p a f -> p (a f)")
                    a3 = a.rearrange("p (h e) -> p h e", h=H)
                    r = resid[:, bass.ds(t, 1), :].rearrange("p a f -> p (a f)")
                    dve.tensor_tensor(a3, a3, acc[:, bass.ds(t, 1), D:ROW].rearrange("p a h -> p (a h)").unsqueeze(2).broadcast_to([P, H, C]), ALU.mult)
                    dve.drain()
                    dve.tensor_tensor(a, a, b_gnn[:], ALU.add)
                    dve.drain()
                    dve.scalar_tensor_tensor(out=r, in0=a, scalar=0.0, in1=r, op0=ALU.max, op1=ALU.add)
                dve.drain()
        early.close()

        late = ExitStack()
        xl = sb("xl", [P, T, D], ctx=late)
        top_w = sb("top_w", [P, T, 2], ctx=late)
        places = sb("places", [P, 2, T], I32, ctx=late)
        exp_row = sb("exp_row", [1, P], I32, ctx=late)
        g_b = sb("g_b", [P, D], ctx=late)
        be_b = sb("be_b", [P, D], ctx=late)
        with ExitStack() as c:
            gw = sb("gw", [P, 2, NEXP], ctx=c)
            gb = sb("gb", [P, NEXP], ctx=c)
            st = sb("m_st", [P, T, 6], ctx=c)
            ag = sb("m_ag", [P, T, 2], ctx=c)
            rs = sb("m_rs", [P, T], ctx=c)
            var_ready = sem("m_var_ready", c)
            std_ready = sem("m_std_ready", c)
            xt = [sb(f"m_xt{i}", [P, D], ctx=c) for i in range(2)]
            lgt = sb("m_lg", [P, NEXP], ctx=c)
            m8 = sb("m8", [P, 8], ctx=c)
            i8 = sb("i8", [P, 8], U32, ctx=c)
            top8 = sb("top8", [P, T, 8], ctx=c)
            idx8 = sb("idx8", [P, T, 8], U32, ctx=c)
            idf = sb("idf", [P, T, 2], ctx=c)
            oh = [sb(f"oh{i}", [P, T, NEXP], ctx=c) for i in range(2)]
            cnt = sb("cnt", [P, T, NEXP], ctx=c)
            tri = sb("tri", [P, P], ctx=c)
            pos = sb("pos", [P, T, NEXP], ctx=c)
            tot = sb("tot", [P, T, NEXP], ctx=c)
            toe = sb("toe", [P, NEXP, T], ctx=c)
            keep = sb("keep", [P, NEXP, T], ctx=c)
            run = sb("run", [P, NEXP, T], ctx=c)
            ti = sb("ti", [P, NEXP], I32, ctx=c)
            tf = sb("tf", [P, NEXP], ctx=c)
            zf = sb("zf", [P, NEXP], ctx=c)
            base = sb("base", [P, NEXP], ctx=c)
            placef = sb("placef", [P, 2, T], ctx=c)
            ecmp = sb("ecmp", [P, NEXP], ctx=c)
            ecol = sb("ecol", [P, 1], ctx=c)
            p_x = [ps(f"m_px{i}", [P, 512], c) for i in range(2)]
            p_l = [ps(f"m_pl{i}", [P, 512], c) for i in range(2)]
            p_w = [ps(f"m_pw{i}", [P, 512], c) for i in range(2)]
            p_t2 = [ps(f"m_pt{i}", [P, 512], c) for i in range(2)]
            w_in = sem("m_w_in", c)
            xl_ready = sem("xl_ready", c)
            x_turned = sem("x_turned", c)
            xt_ready = sem("m_xt_ready", c)
            logits = sem("logits", c)
            logits_taken = sem("logits_taken", c)
            tops = sem("tops", c)
            exps = sem("exps", c)
            cnt_ready = sem("cnt_ready", c)
            ranked = sem("ranked", c)
            tri_ready = sem("tri_ready", c)
            places_ready = sem("places_ready", c)
            sent = sem("sent", c)
            ecol_ready = sem("ecol_ready", c)
            erow_in_psum = sem("erow_in_psum", c)
            block = c.enter_context(nc.Block())
            HALF = T * NEXP // 2

            @block.sync
            def _(sp):
                sp.dma_start(gw[:], gate_w.rearrange("(c k) e -> k c e", k=P)).then_inc(w_in, 16)
                sp.dma_start(gb[:], bcast_rows(gate_b, NEXP)).then_inc(w_in, 16)
                sp.dma_start(g_b[:], bcast_rows(gamma, D)).then_inc(w_in, 16)
                sp.dma_start(be_b[:], bcast_rows(beta, D)).then_inc(w_in, 16)

            @block.vector
            def _(dve):
                def norm(t, s):
                    r = resid[:, bass.ds(t, 1), :].rearrange("p a f -> p (a f)")
                    dve.tensor_scalar(xl[:, bass.ds(t, 1), :].rearrange("p a f -> p (a f)"), r, ag[:, bass.ds(t, 1), 0:1].rearrange("p a b -> p (a b)"),
                                      rs[:, bass.ds(t, 1)], ALU.subtract, ALU.mult).then_inc(xl_ready, 1)

                def best(t, s):
                    dve.drain()
                    dve.wait_ge(logits, t + 1)
                    dve.tensor_tensor(lgt[:], p_l[s][:, 0:NEXP], gb[:], ALU.add).then_inc(logits_taken, 1)
                    dve.drain()
                    dve.max(m8[:], lgt[:])
                    dve.drain()
                    dve.max_index(i8[:], m8[:], lgt[:])
                    dve.tensor_copy(top8[:, bass.ds(t, 1), :], m8[:].unsqueeze(1))
                    dve.drain()
                    dve.tensor_copy(idx8[:, bass.ds(t, 1), :], i8[:].unsqueeze(1))

                def body(t, s):
                    norm(t, s)
                    if not (isinstance(t, int) and t == 0):
                        best(t - 1, 1 - s)

                dve.wait_ge(w_in, 64)
                with dve.Fori(0, T) as t:
                    dve.bn_stats(st[:, bass.ds(t, 1), :], resid[:, bass.ds(t, 1), :])
                dve.drain()
                moments(dve, ag, st)
                dve.tensor_scalar(rs[:], ag[:, :, 1], LN_EPS, None, ALU.add).then_inc(var_ready, 1)
                dve.wait_ge(std_ready, 1)
                dve.reciprocal(rs[:], rs[:])
                dve.drain()
                pairs(dve, T, body)
                best(T - 1, 1)
                dve.drain()
                dve.tensor_tensor(top_w[:, :, 1:2], top8[:, :, 1:2], top8[:, :, 0:1], ALU.subtract).then_inc(tops, 1)
                dve.tensor_copy(idf[:], idx8[:, :, 0:2])
                dve.drain()
                for k in range(2):
                    dve.tensor_tensor(oh[k][:], idf[:, :, k:k + 1].broadcast_to([P, T, NEXP]),
                                      iota_row[:, 0:NEXP].unsqueeze(1).broadcast_to([P, T, NEXP]), ALU.is_equal)
                dve.drain()
                dve.tensor_tensor(cnt[:], oh[0][:], oh[1][:], ALU.add)
                dve.drain()
                dve.tensor_tensor(cnt[:], cnt[:], valid[:].unsqueeze(2).broadcast_to([P, T, NEXP]), ALU.mult).then_inc(cnt_ready, 1)
                dve.wait_ge(exps, 1)
                dve.tensor_scalar(top_w[:, :, 0:1], top_w[:, :, 1:2], 1.0, None, ALU.add)
                dve.drain()
                dve.reciprocal(top_w[:, :, 0:1], top_w[:, :, 0:1])
                dve.drain()
                dve.tensor_tensor(top_w[:, :, 1:2], top_w[:, :, 1:2], top_w[:, :, 0:1], ALU.mult)
                dve.memset(keep[:], 1.0)
                dve.memset(zf[:], 0.0)
                dve.drain()
                dve.memset(keep[:, :, 0:1], 0.0)
                dve.wait_ge(ranked, 1)
                for k in range(2):
                    dve.tensor_copy(toe[:, :, k * (T // 2):(k + 1) * (T // 2)].rearrange("p e t -> p t e"),
                                    p_t2[k][:, 0:HALF].rearrange("p (t e) -> p t e", e=NEXP))
                dve.drain()
                dve.tensor_tensor_scan(run[:].rearrange("p e t -> p (e t)"), keep[:].rearrange("p e t -> p (e t)"),
                                       toe[:].rearrange("p e t -> p (e t)"), 0.0, ALU.mult, ALU.add)
                dve.drain()
                dve.tensor_scalar(tf[:], run[:, :, T - 1], float(P - 1), None, ALU.add)
                dve.drain()
                dve.tensor_copy(ti[:], tf[:])
                dve.drain()
                dve.tensor_scalar(ti[:], ti[:], P.bit_length() - 1, None, ALU.arith_shift_right)
                dve.drain()
                dve.tensor_copy(tf[:], ti[:])
                dve.drain()
                dve.tensor_tensor_scan(base[:], tf[:], zf[:], 0.0, ALU.add, ALU.add)
                dve.drain()
                dve.tensor_tensor(base[:], base[:], tf[:], ALU.subtract)
                dve.tensor_tensor(run[:], run[:], toe[:], ALU.subtract)
                dve.drain()
                dve.tensor_scalar(ecmp[:], base[:], iota_col[:], None, ALU.is_le)
                dve.scalar_tensor_tensor(out=pos[:], in0=base[:].unsqueeze(1).broadcast_to([P, T, NEXP]), scalar=float(P),
                                         in1=run[:].rearrange("p e t -> p t e"), op0=ALU.mult, op1=ALU.add)
                dve.drain()
                dve.tensor_reduce(ecol[:], ecmp[:, 1:NEXP], AXX, ALU.add).then_inc(ecol_ready, 1)
                for k in range(2):
                    half = pos[:, k * (T // 2):(k + 1) * (T // 2), :].rearrange("p t e -> p (t e)")
                    dve.tensor_tensor(half, half, p_w[k][:, 0:HALF], ALU.add)
                dve.drain()
                for k in range(2):
                    dve.tensor_tensor(oh[k][:], oh[k][:], pos[:], ALU.mult)
                dve.drain()
                for k in range(2):
                    dve.tensor_reduce(placef[:, k, :], oh[k][:], AXX, ALU.add)
                dve.drain()
                dve.tensor_copy(places[:], placef[:]).then_inc(places_ready, 1)
                dve.wait_ge(erow_in_psum, 1)
                dve.tensor_copy(exp_row[:], p_l[0][0:1, 0:P])

            @block.scalar
            def _(act):
                def body(t, s):
                    act.wait_ge(x_turned, t + 1)
                    wait(act, logits, t - 1)
                    act.copy(xt[s][:], p_x[s][:, 0:D]).then_inc(xt_ready, 1)
                act.wait_ge(var_ready, 1)
                act.sqrt(rs[:], rs[:]).then_inc(std_ready, 1)
                pairs(act, T, body)
                act.wait_ge(tops, 1)
                act.activation(top_w[:, :, 1:2], top_w[:, :, 1:2], ACT.Exp).then_inc(exps, 1)

            @block.tensor
            def _(pe):
                def gate(t, s):
                    pe.wait_ge(xt_ready, t + 1)
                    wait(pe, logits_taken, t - 1)
                    for k in range(2):
                        mm = pe.matmul(p_l[s][:, 0:NEXP], xt[s][:, k * P:(k + 1) * P], gw[:, k, :], start=(k == 0), stop=(k == 1))
                    mm.then_inc(logits, 1)

                def body(t, s):
                    pe.wait_ge(xl_ready, t + 1)
                    wait(pe, xt_ready, t - 1)
                    for k in range(2):
                        mm = pe.transpose(p_x[s][:, k * P:(k + 1) * P], xl[:, t, k * P:(k + 1) * P], ident[:])
                    mm.then_inc(x_turned, 1)
                    gate(t, s)

                for t in range(T):
                    body(t, t % 2)
                pe.wait_ge(cnt_ready, 1)
                pe.wait_ge(tri_ready, 1)
                for k in range(2):
                    half = cnt[:, k * (T // 2):(k + 1) * (T // 2), :].rearrange("p t e -> p (t e)")
                    pe.matmul(p_w[k][:, 0:HALF], tri[:], half, start=True, stop=True)
                    mm = pe.matmul(p_t2[k][:, 0:HALF], ones[:], half, start=True, stop=True)
                mm.then_inc(ranked, 1)
                pe.wait_ge(ecol_ready, 1)
                pe.wait_ge(logits_taken, T)
                pe.matmul(p_l[0][0:1, 0:P], ecol[:], ident[:], start=True, stop=True).then_inc(erow_in_psum, 1)

            @block.gpsimd
            def _(pool):
                pool.affine_select(out=tri[:], in_=ones[:], compare_op=ALU.is_ge, fill=0.0, base=-1,
                                   pattern=[[1, P]], channel_multiplier=-1).then_inc(tri_ready, 1)
                pool.wait_ge(places_ready, 1)
                for t in range(BLOCKS):
                    n = P if t < NFULL else NREST
                    for k in range(2):
                        pool.indirect_dma_start(slot_x, bass.IndirectOffsetOnAxis(ap=places[0:n, k, t:t + 1], axis=0),
                                                xl[0:n, t, :], None).then_inc(sent, 16)
                pool.wait_ge(sent, 2 * BLOCKS * 16)

        with ExitStack() as c:
            KF = FF // P
            wa = [sb(f"wa{i}", [P, 2, FF], ctx=c) for i in range(2)]
            wb = [sb(f"wb{i}", [P, KF, D], ctx=c) for i in range(2)]
            ba = [sb(f"ba{i}", [P, KF], ctx=c) for i in range(2)]
            bb = [sb(f"bb{i}", [P, D], ctx=c) for i in range(2)]
            xs = [sb(f"xs{i}", [P, D], ctx=c) for i in range(2)]
            xst = [sb(f"xst{i}", [P, D], ctx=c) for i in range(2)]
            ht = [sb(f"ht{i}", [P, FF], ctx=c) for i in range(2)]
            ysb = [sb(f"ysb{i}", [P, D], ctx=c) for i in range(2)]
            p_x = [ps(f"e_px{i}", [P, 512], c) for i in range(2)]
            p_h = [ps(f"e_ph{i}", [P, 512], c) for i in range(2)]
            p_y = [ps(f"e_py{i}", [P, 512], c) for i in range(2)]
            x_in = [sem(f"e_x_in{i}", c) for i in range(2)]
            w_in = [sem(f"e_w_in{i}", c) for i in range(2)]
            x_turned = sem("e_x_turned", c)
            xt_ready = sem("e_xt_ready", c)
            hidden = sem("hidden", c)
            ht_ready = sem("ht_ready", c)
            y_in_psum = sem("y_in_psum", c)
            y_ready = sem("y_ready", c)
            y_out = [sem(f"y_out{i}", c) for i in range(2)]
            block = c.enter_context(nc.Block())
            w1v = w1.rearrange("e (c k) f -> k e c f", k=P)
            w2v = w2.rearrange("e (c k) f -> k e c f", k=P)

            @block.sync
            def _(sp):
                def body(t, s):
                    e = sp.value_load(exp_row[0:1, bass.ds(t, 1)], min_val=0, max_val=NEXP - 1)
                    wait(sp, x_turned, t - 1)
                    sp.dma_start(xs[s][:], slot_x[bass.ts(t, P), :]).then_inc(x_in[s], 16)
                    wait(sp, hidden, t - 1)
                    sp.dma_start(wa[s][:], w1v[:, bass.ds(e, 1), :, :].rearrange("k a c f -> k (a c) f")).then_inc(w_in[s], 16)
                    wait(sp, y_ready, t - 1)
                    sp.dma_start(ba[s][:], b1_cols[bass.ds(e, 1), :, :].rearrange("a p c -> p (a c)")).then_inc(w_in[s], 16)
                    sp.dma_start(wb[s][:], w2v[:, bass.ds(e, 1), :, :].rearrange("k a c f -> k (a c) f")).then_inc(w_in[s], 16)
                    sp.dma_start(bb[s][:], b2[bass.ds(e, 1), :].broadcast_to([P, D])).then_inc(w_in[s], 16)
                pairs(sp, SLOT_TILES, body)

            @block.tensor
            def _(pe):
                def second(t, s):
                    pe.wait_ge(ht_ready, t + 1)
                    wait(pe, y_ready, t - 1)
                    for k in range(KF):
                        mm = pe.matmul(p_y[s][:, 0:D], ht[s][:, k * P:(k + 1) * P], wb[s][:, k, :], start=(k == 0), stop=(k == KF - 1))
                    mm.then_inc(y_in_psum, 1)

                def body(t, s):
                    pe.wait_ge(x_in[s], (t - s) * 8 + 16)
                    wait(pe, xt_ready, t - 1)
                    for k in range(2):
                        mm = pe.transpose(p_x[s][:, k * P:(k + 1) * P], xs[s][:, k * P:(k + 1) * P], ident[:])
                    mm.then_inc(x_turned, 1)
                    if not (isinstance(t, int) and t == 0):
                        second(t - 1, 1 - s)
                    pe.wait_ge(w_in[s], (t - s) * 32 + 64)
                    pe.wait_ge(xt_ready, t + 1)
                    wait(pe, ht_ready, t - 1)
                    for m in range(KF):
                        for k in range(2):
                            mm = pe.matmul(p_h[s][:, m * P:(m + 1) * P], wa[s][:, k, m * P:(m + 1) * P], xst[s][:, k * P:(k + 1) * P],
                                           start=(k == 0), stop=(k == 1))
                    mm.then_inc(hidden, 1)
                pairs(pe, SLOT_TILES, body)
                second(SLOT_TILES - 1, 1)

            @block.scalar
            def _(act):
                def body(t, s):
                    act.wait_ge(x_turned, t + 1)
                    wait(act, hidden, t - 1)
                    act.copy(xst[s][:], p_x[s][:, 0:D]).then_inc(xt_ready, 1)
                    act.wait_ge(hidden, t + 1)
                    act.wait_ge(w_in[s], (t - s) * 32 + 64)
                    wait(act, y_in_psum, t - 1)
                    for m in range(KF):
                        a = act.activation(ht[s][:, m * P:(m + 1) * P], p_h[s][:, m * P:(m + 1) * P], ACT.Relu, bias=ba[s][:, m:m + 1])
                    a.then_inc(ht_ready, 1)
                pairs(act, SLOT_TILES, body)

            @block.vector
            def _(dve):
                def body(t, s):
                    dve.wait_ge(y_in_psum, t + 1)
                    dve.wait_ge(w_in[s], (t - s) * 32 + 64)
                    wait(dve, y_out[s], (t - s) * 8)
                    dve.tensor_tensor(ysb[s][:], p_y[s][:, 0:D], bb[s][:], ALU.add).then_inc(y_ready, 1)
                pairs(dve, SLOT_TILES, body)

            @block.gpsimd
            def _(pool):
                def body(t, s):
                    pool.wait_ge(y_ready, t + 1)
                    pool.dma_start(slot_y[bass.ts(t, P), :], ysb[s][:]).then_inc(y_out[s], 16)
                pairs(pool, SLOT_TILES, body)
                for s in range(2):
                    pool.wait_ge(y_out[s], SLOT_TILES // 2 * 16)

        with ExitStack() as c:
            ya = [sb(f"ya{i}", [P, 2, D], ctx=c) for i in range(R)]
            st = [sb(f"f_st{i}", [P, 6], ctx=c) for i in range(R)]
            ag = [sb(f"f_ag{i}", [P, 2], ctx=c) for i in range(R)]
            rs = [sb(f"f_rs{i}", [P, 1], ctx=c) for i in range(R)]
            y_in = [sem(f"f_y_in{i}", c) for i in range(R)]
            ready = sem("f_ready", c)
            ya_used = sem("ya_used", c)
            var_ready = sem("f_var_ready", c)
            std_ready = sem("f_std_ready", c)
            stored = sem("stored", c)
            block = c.enter_context(nc.Block())

            @block.gpsimd
            def _(pool):
                for t in range(BLOCKS):
                    n = P if t < NFULL else NREST
                    wait(pool, ya_used, t - R + 1)
                    for k in range(2):
                        pool.indirect_dma_start(ya[t % R][0:n, k, :], None, slot_y,
                                                bass.IndirectOffsetOnAxis(ap=places[0:n, k, t:t + 1], axis=0)).then_inc(y_in[t % R], 16)

            @block.scalar
            def _(act):
                for t in range(BLOCKS):
                    n = P if t < NFULL else NREST
                    act.wait_ge(var_ready, t + 1)
                    act.sqrt(rs[t % R][0:n], rs[t % R][0:n]).then_inc(std_ready, 1)

            @block.vector
            def _(dve):
                def combine(t):
                    n = P if t < NFULL else NREST
                    s = t % R
                    y = xl[0:n, t, :]
                    dve.wait_ge(y_in[s], (t // R + 1) * 32)
                    for k in range(2):
                        dve.scalar_tensor_tensor(out=y, in0=ya[s][0:n, k, :], scalar=top_w[0:n, t, k:k + 1], in1=y, op0=ALU.mult, op1=ALU.add)
                        dve.drain()
                    dve.bn_stats(st[s][0:n], y).then_inc(ya_used, 1)
                    dve.tensor_tensor(resid[0:n, t, :], resid[0:n, t, :], be_b[0:n], ALU.add)
                    dve.drain()
                    dve.bn_aggr(ag[s][0:n], st[s][0:n])
                    dve.drain()
                    dve.tensor_scalar(rs[s][0:n], ag[s][0:n, 1:2], LN_EPS, None, ALU.add).then_inc(var_ready, 1)

                def finish(t):
                    n = P if t < NFULL else NREST
                    s = t % R
                    y = xl[0:n, t, :]
                    dve.wait_ge(std_ready, t + 1)
                    dve.reciprocal(rs[s][0:n], rs[s][0:n])
                    dve.drain()
                    dve.tensor_scalar(y, y, ag[s][0:n, 0:1], rs[s][0:n], ALU.subtract, ALU.mult)
                    dve.drain()
                    dve.tensor_tensor(y, y, g_b[0:n], ALU.mult)
                    dve.drain()
                    dve.tensor_tensor(y, y, resid[0:n, t, :], ALU.add).then_inc(ready, 1)

                for t in range(BLOCKS):
                    combine(t)
                    if t:
                        finish(t - 1)
                finish(BLOCKS - 1)

            @block.sync
            def _(sp):
                for t in range(BLOCKS):
                    n = P if t < NFULL else NREST
                    sp.wait_ge(ready, t + 1)
                    sp.dma_start(out[t * P:t * P + n, :], xl[0:n, t, :]).then_inc(stored, 16)
                sp.wait_ge(stored, BLOCKS * 16)
        late.close()


_INS = ['x', 'src', 'dst', 'L0_gnn_W', 'L0_gnn_att_src', 'L0_gnn_att_dst', 'L0_gnn_bias', 'L0_mix_Wqkv',
        'L0_mix_bqkv', 'L0_mix_Wproj', 'L0_mix_bproj', 'L0_mix_temperature', 'L0_ffn_gate_w', 'L0_ffn_gate_b',
        'L0_ffn_w1', 'L0_ffn_b1', 'L0_ffn_w2', 'L0_ffn_b2', 'L0_ffn_gamma', 'L0_ffn_beta']
_OUTS = [((N, D), 'float32')]


def kernel(**inputs):
    import numpy as _np
    import concourse.bacc as _bacc
    from concourse import mybir as _mybir
    from concourse.bass_utils import run_bass_kernel_spmd as _run

    nc = _bacc.Bacc("TRN2", target_bir_lowering=False, num_devices=1)
    arrays, args = {}, []
    for name in _INS:
        a = _np.ascontiguousarray(inputs[name])
        arrays[f"in_{name}_dram"] = a
        args.append(nc.dram_tensor(f"in_{name}_dram", a.shape, _mybir.dt.from_np(a.dtype), kind="ExternalInput").ap())
    for i, (shape, dtype) in enumerate(_OUTS):
        args.append(nc.dram_tensor(f"out_{i}_dram", shape, _mybir.dt.from_np(_np.dtype(dtype)), kind="ExternalOutput").ap())
    gps_layer(nc, *args)
    r = _run(nc, [arrays], core_ids=[0])
    return r.results[0]["out_0_dram"]
```

```python
from contextlib import ExitStack

import concourse.bass as bass
from concourse import mybir

F32 = mybir.dt.float32
BF16 = mybir.dt.bfloat16
I32 = mybir.dt.int32
U32 = mybir.dt.uint32
ALU = mybir.AluOpType
ACT = mybir.ActivationFunctionType
AXX = mybir.AxisListType.X
RMAX = bass.bass_isa.ReduceOp.max

P = 128
N = 6250
E = 200000
D = 256
H = 8
C = D // H
T = 50
NFULL = N // P
NREST = N - NFULL * P
BLOCKS = -(-N // P)
TILES_PER_CHUNK = 4
CHUNK = TILES_PER_CHUNK * P
CHUNKS = 392
STEPS = CHUNKS + BLOCKS - 1
ROW = D + H
V1 = C + 1
DIAGS = C // 2 + 1
FEAT = (DIAGS - 1) * C
FCH = FEAT // P
UNITS = H + 1
WRAP = C + DIAGS - 1
NEXP, FF = 16, 512
SLOT_ROWS = 2 * P
SLOT_TILES = (2 * N - NEXP) // SLOT_ROWS + NEXP
EXP_TILES = -(-N // SLOT_ROWS) + 1
SPARE = NEXP * EXP_TILES
WR = 4
YR = 8
assert SLOT_TILES % WR == 0
LN_EPS = 1e-5
NORM_EPS = 1e-12
TINY = 1e-37
A_COEF, B_COEF, C_COEF = 0.5, 1.0, 1.0
SCALE = float(C) ** 0.25
SLOPE = 0.2
PAD_DST = 1 << 20
R = 4
OCT = 8
assert STEPS % OCT == 0 and STEPS // OCT > T + 1 and OCT % R == 0
assert CHUNKS * CHUNK >= E and CHUNKS == OCT * (T - 1)


def wait(eng, sem, value):
    if isinstance(value, int) and value <= 0:
        return
    eng.wait_ge(sem, value)


def pairs(eng, count, body):
    body(0, 0)
    body(1, 1)
    with eng.Fori(1, count // 2) as i:
        body(i * 2, 0)
        body(i * 2 + 1, 1)


def ring(eng, count, slots, body):
    for j in range(slots):
        body(j, j)
    with eng.Fori(1, count // slots) as i:
        for j in range(slots):
            body(i * slots + j, j)


def ring_peeled(eng, count, slots, body):
    ring(eng, count - slots, slots, body)
    for j in range(slots):
        body(count - slots + j, j)


def moments(dve, mv, st):
    m, v = mv[:, :, 0], mv[:, :, 1]
    dve.tensor_tensor(m, st[:, :, 1], st[:, :, 4], ALU.subtract)
    dve.tensor_tensor(st[:, :, 0], st[:, :, 2], st[:, :, 5], ALU.add)
    dve.drain()
    dve.tensor_tensor(v, m, m, ALU.mult)
    dve.drain()
    dve.tensor_scalar(v, v, 0.25, None, ALU.mult)
    dve.tensor_tensor(m, st[:, :, 1], st[:, :, 4], ALU.add)
    dve.drain()
    dve.scalar_tensor_tensor(out=v, in0=st[:, :, 0], scalar=1.0 / D, in1=v, op0=ALU.mult, op1=ALU.add)
    dve.tensor_scalar(m, m, 0.5, None, ALU.mult)
    dve.drain()


def bcast_rows(ap, n):
    return ap.unsqueeze(0).broadcast_to([P, n])


def gps_layer(nc, x, src, dst, gnn_W, att_src, att_dst, gnn_bias, Wqkv, bqkv, Wproj, bproj, temperature,
              gate_w, gate_b, w1, b1, w2, b2, gamma, beta, out):
    top = ExitStack()

    def sb(name, shape, dt=F32, ctx=None):
        return (ctx or top).enter_context(nc.sbuf_tensor(name, shape, dt))

    def ps(name, shape, ctx):
        return ctx.enter_context(nc.psum_tensor(name, shape, F32))

    def sem(name, ctx=None):
        return (ctx or top).enter_context(nc.semaphore(name))

    with top:
        node_rows = nc.dram_tensor("node_rows", (T * P, ROW), F32).ap()
        qn_dram = nc.dram_tensor("qn_dram", ((T + 1) * P, D), F32).ap()
        src_pad = nc.dram_tensor("src_pad", (CHUNKS, CHUNK), I32).ap()
        dst_pad = nc.dram_tensor("dst_pad", (CHUNKS, CHUNK), I32).ap()
        slot_x = nc.dram_tensor("slot_x", ((SPARE + 1) * SLOT_ROWS, D), F32).ap()
        slot_y = nc.dram_tensor("slot_y", (SLOT_TILES * SLOT_ROWS, D), F32).ap()
        gram_dram = nc.dram_tensor("gram_dram", (H, C, 2 * C), F32).ap()
        sums_dram = nc.dram_tensor("sums_dram", (2, D), F32).ap()
        b1_cols = nc.dram_tensor("b1_cols", (NEXP, P, FF // P), F32).ap()

        resid = sb("resid", [P, T, D])
        ident = sb("ident", [P, P])
        iota_row = sb("iota_row", [P, P])
        iota_col = sb("iota_col", [P, 1])
        ones = sb("ones", [P, P])
        valid = sb("valid", [P, T])
        iota_bf = sb("iota_bf", [P, P], BF16)
        ident_bf = sb("ident_bf", [P, P], BF16)
        adm = sb("adm", [P, T, 2 * H])
        adm_parts = sb("adm_parts", [P, T, 3, 2 * H], BF16)

        b_gnn = sb("b_gnn", [P, D])
        acc = sb("acc", [P, T, ROW])
        early = ExitStack()
        w_cat = sb("w_cat", [P, 2, 2 * D + 2 * D + 2 * H], ctx=early)
        wp_t = sb("wp_t", [P, 2, D], ctx=early)
        b_qkv = sb("b_qkv", [P, 3 * D], ctx=early)
        b_proj = sb("b_proj", [P, D], ctx=early)
        ss_scale = sb("ss_scale", [P, 2 * H], ctx=early)
        nrm_scale = sb("nrm_scale", [P, 2 * H], ctx=early)
        mv = sb("mv", [P, T, 2], ctx=early)
        rstd = sb("rstd", [P, T], ctx=early)
        nmr = sb("nmr", [P, T], ctx=early)
        a_s = sb("a_s", [P, T, H], ctx=early)
        mix_w = sb("mix_w", [P, H, FCH, V1], ctx=early)
        mix_tail = sb("mix_tail", [P, H // 2, 2 * V1], ctx=early)
        vsum_w = sb("vsum_w", [1, H * V1], ctx=early)
        W_Q = D + 2 * H
        TAILW = 2 * C
        HT = FEAT // 2
        GK = HT + 1
        tg_sb = [sb(f"tg_sb{i}", [P, GK + P + 1], ctx=early) for i in range(2)]
        sum_sb = sb("sum_sb", [1, D], ctx=early)
        gcol = sb("gcol", [P, H, FCH], ctx=early)
        gtail = sb("gtail", [P, H // 2], ctx=early)
        coef = sb("coef", [P, FCH], ctx=early)
        tails = (A_COEF, SCALE ** 2 * B_COEF)

        with ExitStack() as c:
            raw = sb("raw", [P, 6, D], ctx=c)
            raw_w = sb("raw_w", [P, 2, D], ctx=c)
            raw_p = sb("raw_p", [P, 2, D], ctx=c)
            gw_t = sb("gw_t", [P, 2, D], ctx=c)
            att_bd = sb("att_bd", [P, 2, 2 * H], ctx=c)
            zrow = sb("zrow", [P, D], ctx=c)
            temp_b = sb("temp_b", [P, H], ctx=c)
            pad_i = sb("pad_i", [P, CHUNK], I32, ctx=c)
            pad_s = sb("pad_s", [P, CHUNK], I32, ctx=c)
            iota_i = sb("iota_i", [P, P], I32, ctx=c)
            iota_ci = sb("iota_ci", [P, 1], I32, ctx=c)
            b1_raw = sb("b1_raw", [NEXP * FF // P, P], ctx=c)
            b1_t = sb("b1_t", [P, NEXP * FF // P], ctx=c)
            st6 = sb("st6", [P, T, 6], ctx=c)
            pt = [ps(f"s1_pt{i}", [P, 512], c) for i in range(2)]
            pw = ps("s1_pw", [P, 512], c)
            x_zeroed = sem("x_zeroed", c)
            x_in = [sem(f"x_in{i}", c) for i in range(4)]
            x_rest_in = sem("x_rest_in", c)
            w_in = sem("w_in", c)
            b_in = sem("b_in", c)
            att_zeroed = sem("att_zeroed", c)
            att_in = sem("att_in", c)
            pads_set = sem("pads_set", c)
            scratch_out = sem("scratch_out", c)
            ident_ready = sem("ident_ready", c)
            turned = sem("turned", c)
            copied = sem("copied", c)
            b1_out = sem("b1_out", c)
            watt_ready = sem("watt_ready", c)
            iotas = sem("iotas", c)
            var_ready = sem("var_ready", c)
            std_ready = sem("std_ready", c)
            block = c.enter_context(nc.Block())

            turns = []
            for kc in range(2):
                for m in range(6):
                    turns.append((raw[:, m, kc * P:(kc + 1) * P],
                                  w_cat[:, kc, W_Q + m * P:W_Q + (m + 1) * P]))
                for m in range(2):
                    turns.append((raw_p[:, m, kc * P:(kc + 1) * P], wp_t[:, kc, m * P:(m + 1) * P]))
                    turns.append((raw_w[:, m, kc * P:(kc + 1) * P], gw_t[:, kc, m * P:(m + 1) * P]))

            @block.sync
            def _(sp):
                sp.wait_ge(x_zeroed, 1)
                for q in range(4):
                    n = NFULL // 4
                    sp.dma_start(resid[:, q * n:(q + 1) * n, :],
                                 x[q * n * P:(q + 1) * n * P, :].rearrange("(t p) f -> p t f", p=P)).then_inc(x_in[q], 16)
                sp.dma_start(resid[0:NREST, NFULL, :], x[NFULL * P:N, :]).then_inc(x_rest_in, 16)
                sp.dma_start(raw[:], Wqkv.rearrange("(m p) k -> p m k", p=P)).then_inc(w_in, 16)
                sp.dma_start(raw_w[:], gnn_W.rearrange("(m p) k -> p m k", p=P)).then_inc(w_in, 16)
                sp.dma_start(raw_p[:], Wproj.rearrange("(m p) k -> p m k", p=P)).then_inc(w_in, 16)
                sp.dma_start(b1_raw[:], b1.rearrange("e (c p) -> (e c) p", p=P)).then_inc(w_in, 16)
                sp.dma_start(w_cat[:, :, 0:D], gnn_W.rearrange("(c k) n -> k c n", k=P)).then_inc(w_in, 16)
                sp.wait_ge(att_zeroed, 1)
                for h in range(H):
                    p0 = (h % 4) * C
                    for k, a in enumerate((att_src, att_dst)):
                        sp.dma_start(att_bd[p0:p0 + C, h // 4, k * H + h:k * H + h + 1],
                                     a[h:h + 1, :].rearrange("a c -> c a")).then_inc(att_in, 16)
                sp.wait_ge(pads_set, 3)
                full = E // CHUNK
                rest = E - full * CHUNK
                for lst, pad, pads in ((src, src_pad, pad_s), (dst, dst_pad, pad_i)):
                    sp.dma_start(pad[0:full, :], lst[0:full * CHUNK].rearrange("(a b) -> a b", b=CHUNK)).then_inc(scratch_out, 16)
                    sp.dma_start(pad[full:full + 1, 0:rest], lst[full * CHUNK:E].unsqueeze(0)).then_inc(scratch_out, 16)
                    sp.dma_start(pad[full:full + 1, rest:CHUNK], pads[0:1, 0:CHUNK - rest]).then_inc(scratch_out, 16)
                    sp.dma_start(pad[full + 1:CHUNKS, :], pads[0:CHUNKS - full - 1, :]).then_inc(scratch_out, 16)
                sp.dma_start(slot_x[SPARE * SLOT_ROWS:(SPARE + 1) * SLOT_ROWS, :].rearrange("(t p) f -> p t f", p=P),
                             zrow[:].unsqueeze(1).broadcast_to([P, SLOT_ROWS // P, D])).then_inc(scratch_out, 16)
                sp.dma_start(qn_dram[T * P:(T + 1) * P, :], zrow[:]).then_inc(scratch_out, 16)
                sp.wait_ge(scratch_out, 10 * 16)
                sp.wait_ge(copied, len(turns) + 1)
                sp.dma_start(b1_cols.rearrange("e p c -> p e c"), b1_t[:].rearrange("p (e c) -> p e c", e=NEXP)).then_inc(b1_out, 16)
                sp.wait_ge(b1_out, 16)

            @block.gpsimd
            def _(pool):
                pool.memset(ident[:], 0.0)
                pool.memset(ones[:], 1.0)
                pool.memset(valid[:], 1.0)
                pool.iota(iota_i[:], [[1, P]], base=0, channel_multiplier=0)
                pool.iota(iota_ci[:], [[1, 1]], base=0, channel_multiplier=1).then_inc(iotas, 1)
                pool.drain()
                pool.affine_select(out=ident[:], in_=ident[:], compare_op=ALU.not_equal, fill=1.0, base=0,
                                   pattern=[[-1, P]], channel_multiplier=1).then_inc(ident_ready, 1)
                pool.affine_select(out=valid[:], in_=valid[:], compare_op=ALU.is_ge, fill=0.0, base=N - 1,
                                   pattern=[[-P, T]], channel_multiplier=-1)
                for ap, vec, n in ((b_qkv, bqkv, 3 * D), (b_proj, bproj, D), (b_gnn, gnn_bias, D)):
                    pool.dma_start(ap[:], bcast_rows(vec, n)).then_inc(b_in, 16)
                pool.dma_start(temp_b[:], bcast_rows(temperature.rearrange("a h b c -> (a h b c)"), H)).then_inc(b_in, 16)

            @block.vector
            def _(dve):
                dve.memset(resid[:, NFULL:T, :], 0.0).then_inc(x_zeroed, 1)
                dve.memset(att_bd[:], 0.0).then_inc(att_zeroed, 1)
                dve.memset(pad_s[:], 0).then_inc(pads_set, 1)
                dve.memset(pad_i[:], PAD_DST).then_inc(pads_set, 1)
                dve.memset(zrow[:], 0.0).then_inc(pads_set, 1)
                dve.memset(ss_scale[:, 0:H], SCALE * SCALE)
                dve.memset(ss_scale[:, H:2 * H], 1.0)
                dve.memset(nrm_scale[:, H:2 * H], SCALE)
                dve.wait_ge(iotas, 1)
                dve.tensor_copy(iota_row[:], iota_i[:])
                dve.tensor_copy(iota_bf[:], iota_i[:])
                dve.tensor_copy(iota_col[:], iota_ci[:])
                dve.wait_ge(ident_ready, 1)
                dve.tensor_copy(ident_bf[:], ident[:])
                for t in range(T):
                    if t % (NFULL // 4) == 0 and t < NFULL:
                        dve.wait_ge(x_in[t // (NFULL // 4)], 16)
                    if t == NFULL:
                        dve.wait_ge(x_rest_in, 16)
                    dve.bn_stats(st6[:, t, :], resid[:, t, :])
                dve.drain()
                moments(dve, mv, st6)
                dve.tensor_scalar(rstd[:], mv[:, :, 1], LN_EPS, None, ALU.add).then_inc(var_ready, 1)
                dve.wait_ge(std_ready, 1)
                dve.reciprocal(rstd[:], rstd[:])
                dve.drain()
                dve.scalar_tensor_tensor(out=nmr[:], in0=mv[:, :, 0], scalar=-1.0, in1=rstd[:], op0=ALU.mult, op1=ALU.mult)
                dve.wait_ge(b_in, 4 * 16)
                dve.tensor_scalar(nrm_scale[:, 0:H], temp_b[:], SCALE * SCALE, None, ALU.mult)

            @block.tensor
            def _(pe):
                pe.wait_ge(ident_ready, 1)
                pe.wait_ge(w_in, 5 * 16)
                for n, (a, _) in enumerate(turns):
                    if n >= 2:
                        pe.wait_ge(copied, n - 1)
                    pe.transpose(pt[n % 2][:, 0:P], a, ident[:]).then_inc(turned, 1)
                n = len(turns)
                pe.wait_ge(copied, n - 1)
                pe.transpose(pt[n % 2][:, 0:NEXP * FF // P], b1_raw[:], ident[0:NEXP * FF // P, 0:NEXP * FF // P]).then_inc(turned, 1)
                pe.wait_ge(copied, n)
                pe.wait_ge(att_in, 2 * H * 16)
                for m in range(2):
                    for kc in range(2):
                        mm = pe.matmul(pw[:, m * 2 * H:(m + 1) * 2 * H], gw_t[:, kc, m * P:(m + 1) * P], att_bd[:, kc, :],
                                       start=(kc == 0), stop=(kc == 1))
                mm.then_inc(watt_ready, 1)

            @block.scalar
            def _(act):
                for n, (_, b) in enumerate(turns):
                    act.wait_ge(turned, n + 1)
                    act.copy(b, pt[n % 2][:, 0:P]).then_inc(copied, 1)
                n = len(turns)
                act.wait_ge(turned, n + 1)
                act.copy(b1_t[:], pt[n % 2][:, 0:NEXP * FF // P]).then_inc(copied, 1)
                act.wait_ge(var_ready, 1)
                act.sqrt(rstd[:], rstd[:]).then_inc(std_ready, 1)
                act.wait_ge(watt_ready, 1)
                act.copy(w_cat[:, :, D:D + 2 * H], pw[:, 0:4 * H].rearrange("p (m a) -> p m a", m=2))

        def products(eng, feat, wrapped, u):
            if u < H:
                base = wrapped[:, u, 0:1]
                whole = [base.ap[0][0], P]
                return eng.tensor_tensor(feat.rearrange("p (d i) -> p d i", i=C),
                                         bass.AP(base.tensor, base.offset, [whole, [0, DIAGS - 1], [1, C]]),
                                         bass.AP(base.tensor, base.offset, [whole, [1, DIAGS - 1], [1, C]]), ALU.mult)
            tail = feat.rearrange("p (h a i) -> p h a i", h=H, a=2)
            eng.tensor_tensor(tail[:, :, 0, :], wrapped[:, :, 0:C], wrapped[:, :, DIAGS - 1:WRAP], ALU.mult)
            return eng.tensor_copy(tail[:, :, 1, :], wrapped[:, :, 0:C])

        with ExitStack() as c:
            xn = [sb(f"xn{i}", [P, D], ctx=c) for i in range(2)]
            xt = [sb(f"xt{i}", [P, 2, P], ctx=c) for i in range(2)]
            row = [sb(f"row{i}", [P, ROW], ctx=c) for i in range(2)]
            qk = [sb(f"qk{i}", [P, 2 * D], ctx=c) for i in range(2)]
            v = [sb(f"v{i}", [P, D], ctx=c) for i in range(2)]
            sq = sb("sq", [P, 2 * D], ctx=c)
            nrm = sb("nrm", [P, 2 * H], ctx=c)
            inv = [sb(f"inv{i}", [P, 2 * H], ctx=c) for i in range(2)]
            qst = [sb(f"qst{i}", [P, D], ctx=c) for i in range(2)]
            k1 = [sb(f"k1_{i}", [P, 2, P + 1], ctx=c) for i in range(2)]
            km = [sb(f"km{i}", [P, D], ctx=c) for i in range(2)]
            vm = [sb(f"vm{i}", [P, D], ctx=c) for i in range(2)]
            kk = [sb(f"kk{i}", [P, H, WRAP], ctx=c) for i in range(2)]
            feat = [sb(f"kfeat{i}", [P, H, FEAT], ctx=c) for i in range(2)]
            tail1 = [sb(f"ktail{i}", [P, 2, FEAT // 2 + 1], ctx=c) for i in range(2)]
            zeros = sb("zeros", [P, 512], ctx=c)
            vmask = sb("vmask", [P, T], ctx=c)
            mask = [sb(f"mask{i}", [P, 1], ctx=c) for i in range(2)]
            p_t = ps("p_t", [P, 512], c)
            p_row = ps("p_row", [P, 512], c)
            p_qk = ps("p_qk", [P, 512], c)
            p_v = ps("p_v", [P, 512], c)
            p_main = [ps(f"p_main{i}", [P, 512], c) for i in range(2)]
            p_tg = [ps(f"p_tg{i}", [P, 512], c) for i in range(2)]
            KV_UNITS = 5
            main_sb = [feat[0][:, g, :] for g in range(2)]
            zeroed = sem("zeroed", c)
            ones_set = sem("ones_set", c)
            xn_ready = sem("xn_ready", c)
            xt_in_psum = sem("xt_in_psum", c)
            xt_ready = sem("xt_ready", c)
            projected = sem("projected", c)
            row_ready = sem("row_ready", c)
            qkv_taken = sem("qkv_taken", c)
            squared = sem("squared", c)
            squares_ready = sem("squares_ready", c)
            norms_ready = sem("norms_ready", c)
            k_ready = sem("k_ready", c)
            masked = sem("masked", c)
            q_ready = sem("q_ready", c)
            dve_feats = sem("dve_feats", c)
            pool_feats = sem("pool_feats", c)
            summed = sem("summed", c)
            row_out = [sem(f"row_out{i}", c) for i in range(2)]
            q_out = [sem(f"q_out{i}", c) for i in range(2)]
            sums_ready = sem("sums_ready", c)
            main_turned = sem("main_turned", c)
            block = c.enter_context(nc.Block())

            @block.scalar
            def _(act):
                def normalise(t, s):
                    act.activation(xn[s][:], resid[:, bass.ds(t, 1), :].rearrange("p a f -> p (a f)"), ACT.Identity,
                                   bias=nmr[:, bass.ds(t, 1)], scale=rstd[:, bass.ds(t, 1)]).then_inc(xn_ready, 1)

                def take_xt(t, s):
                    act.wait_ge(xt_in_psum, t + 1)
                    wait(act, projected, t - 1)
                    act.copy(xt[s][:], p_t[:, 0:D].rearrange("p (a b) -> p a b", a=2)).then_inc(xt_ready, 1)

                def body(t, s):
                    act.wait_ge(projected, t + 1)
                    wait(act, row_out[s], (t - s) * 8)
                    act.copy(row[s][:], p_row[:, 0:ROW])
                    act.copy(a_s[:, bass.ds(t, 1), :], p_row[:, D:D + H].unsqueeze(1))
                    act.copy(adm[:, bass.ds(t, 1), 0:H], p_row[:, ROW:ROW + H].unsqueeze(1)).then_inc(row_ready, 1)
                    act.wait_ge(qkv_taken, t + 1)
                    act.activation(sq[:], qk[s][:], ACT.Square).then_inc(squared, 1)
                    if not (isinstance(t, int) and t == T - 1):
                        take_xt(t + 1, 1 - s)
                    if not (isinstance(t, int) and t >= T - 2):
                        normalise(t + 2, s)
                    act.wait_ge(squares_ready, t + 1)
                    act.sqrt(nrm[:], nrm[:]).then_inc(norms_ready, 1)
                    wait(act, summed, t - 1)
                    act.activation(vm[s][:], v[s][:], ACT.Copy, scale=mask[s][:])
                    act.wait_ge(k_ready, t + 1)
                    act.activation(km[s][:].rearrange("p (h e) -> p h e", h=H), kk[s][:, :, 0:C], ACT.Copy,
                                   scale=mask[s][:]).then_inc(masked, 1)

                normalise(0, 0)
                normalise(1, 1)
                take_xt(0, 0)
                act.wait_ge(ones_set, 1)
                ring_peeled(act, T, 2, body)
                act.wait_ge(summed, T)
                for g in range(2):
                    act.copy(main_sb[g], p_main[g][:])
                    a = act.copy(tg_sb[g][:], p_tg[g][:, 0:GK + P + 1])
                a.then_inc(sums_ready, 1)

            @block.tensor
            def _(pe):
                pe.wait_ge(zeroed, 1)
                for bank in p_main + p_tg:
                    pe.matmul(bank[:], zeros[:, 0:P], zeros[:], start=True, stop=False, skip_group_check=True)

                def add_sum(o, w, x):
                    return pe.matmul(o, w, x, start=False, stop=False, skip_group_check=True)

                def turn(t, s):
                    pe.wait_ge(xn_ready, t + 1)
                    wait(pe, xt_ready, t)
                    pe.transpose(p_t[:, 0:P], xn[s][:, 0:P], ident[:])
                    pe.transpose(p_t[:, P:D], xn[s][:, P:D], ident[:]).then_inc(xt_in_psum, 1)

                def sums(t, s):
                    pe.wait_ge(masked, t + 1)
                    pe.wait_ge(dve_feats, t + 1)
                    pe.wait_ge(pool_feats, t + 1)
                    for g in range(2):
                        add_sum(p_tg[g][:, GK:GK + P + 1], km[s][:, g * P:(g + 1) * P], k1[s][:, g, :])
                        add_sum(p_tg[g][:, 0:GK], vm[s][:, g * P:(g + 1) * P], tail1[s][:, g, :])
                    for u in range(H):
                        mm = add_sum(p_main[u // 4][(u % 4) * C:(u % 4 + 1) * C, :], vm[s][:, u * C:(u + 1) * C], feat[s][:, u, :])
                    mm.then_inc(summed, 1)

                def body(t, s):
                    pe.wait_ge(xt_ready, t + 1)
                    wait(pe, row_ready, t)
                    wait(pe, qkv_taken, t)
                    for o, lo, hi in ((p_row[:, 0:W_Q], 0, W_Q), (p_qk[:], W_Q, W_Q + 2 * D), (p_v[:, 0:D], W_Q + 2 * D, W_Q + 3 * D)):
                        for kc in range(2):
                            mm = pe.matmul(o, xt[s][:, kc, :], w_cat[:, kc, lo:hi], start=(kc == 0), stop=(kc == 1))
                    mm.then_inc(projected, 1)
                    if not (isinstance(t, int) and t == T - 1):
                        turn(t + 1, 1 - s)
                    if not (isinstance(t, int) and t < 2):
                        sums(t - 2, s)

                turn(0, 0)
                ring_peeled(pe, T, 2, body)
                sums(T - 2, 0)
                sums(T - 1, 1)
                pe.wait_ge(sums_ready, 1)
                for g, bank in enumerate((p_row, p_qk)):
                    for m in range(FCH):
                        pe.transpose(bank[:, m * P:(m + 1) * P], main_sb[g][:, m * P:(m + 1) * P], ident[:])
                for m in range(FCH):
                    mm = pe.transpose(p_v[:, m * P:(m + 1) * P], tg_sb[m // 2][:, (m % 2) * P:(m % 2 + 1) * P], ident[:])
                mm.then_inc(main_turned, 1)

            @block.vector
            def _(dve):
                dve.memset(zeros[:], 0.0).then_inc(zeroed, 1)
                dve.tensor_scalar(vmask[:], valid[:], 1.0 / N, None, ALU.mult)
                for s in range(2):
                    dve.memset(k1[s][:], 1.0)
                    dve.memset(tail1[s][:], 1.0)
                dve.memset(mix_tail[:], 0.0)
                dve.memset(vsum_w[:], SCALE ** 4 * C_COEF)
                dve.memset(coef[:], 2 * A_COEF)
                dve.drain()
                dve.memset(coef[0:C, 0:1], A_COEF).then_inc(ones_set, 1)
                dve.drain()

                def features(t, s, units):
                    for u in units:
                        a = products(dve, feat[s][:, u, :], kk[s], u)
                    return a

                def body(t, s):
                    first = isinstance(t, int) and t == 0
                    dve.wait_ge(projected, t + 1)
                    wait(dve, masked, t - 1)
                    wait(dve, pool_feats, t - 1)
                    dve.tensor_tensor(qk[s][:], p_qk[:], b_qkv[:, 0:2 * D], ALU.add)
                    dve.tensor_copy(mask[s][:], vmask[:, bass.ds(t, 1)])
                    dve.tensor_tensor(v[s][:], p_v[:, 0:D], b_qkv[:, 2 * D:3 * D], ALU.add).then_inc(qkv_taken, 1)
                    if not first:
                        wait(dve, summed, t - 2)
                        features(t - 1, 1 - s, (0, 1))
                    dve.wait_ge(squared, t + 1)
                    dve.tensor_reduce(nrm[:], sq[:].rearrange("p (h e) -> p h e", e=C), AXX, ALU.add)
                    dve.drain()
                    dve.tensor_tensor(nrm[:], nrm[:], ss_scale[:], ALU.mult).then_inc(squares_ready, 1)
                    if not first:
                        features(t - 1, 1 - s, (2, 3))
                    dve.wait_ge(norms_ready, t + 1)
                    dve.tensor_scalar(nrm[:], nrm[:], NORM_EPS, None, ALU.max)
                    dve.drain()
                    dve.reciprocal(nrm[:], nrm[:])
                    dve.drain()
                    dve.tensor_tensor(inv[s][:], nrm[:], nrm_scale[:], ALU.mult)
                    dve.drain()
                    dve.tensor_tensor(kk[s][:, :, 0:C], qk[s][:, D:2 * D].rearrange("p (h e) -> p h e", h=H),
                                      inv[s][:, H:2 * H].unsqueeze(2).broadcast_to([P, H, C]), ALU.mult)
                    if not first:
                        features(t - 1, 1 - s, range(4, KV_UNITS)).then_inc(dve_feats, 1)
                    dve.drain()
                    wait(dve, summed, t - 1)
                    dve.tensor_copy(k1[s][:, :, 0:P].rearrange("p g (j e) -> p g j e", e=C), kk[s][:, :, 0:C].rearrange("p (g j) e -> p g j e", g=2))
                    dve.tensor_copy(kk[s][:, :, C:WRAP], kk[s][:, :, 0:WRAP - C]).then_inc(k_ready, 1)
                    dve.drain()

                ring_peeled(dve, T, 2, body)
                dve.wait_ge(summed, T - 2)
                features(T - 1, 1, range(KV_UNITS)).then_inc(dve_feats, 1)
                dve.wait_ge(main_turned, 1)
                for g, bank in enumerate((p_row, p_qk)):
                    for m in range(FCH):
                        dve.tensor_scalar(mix_w[:, 4 * g:4 * g + 4, m, 1:V1], bank[:, m * P:(m + 1) * P].rearrange("p (j e) -> p j e", j=4),
                                          coef[:, m:m + 1], None, ALU.mult)
                for h in range(H):
                    for a, k in enumerate(tails):
                        p0, q0 = (h % 2) * TAILW + a * C, (h // 2) * P + (h % 4) * C
                        dve.tensor_scalar(mix_tail[p0:p0 + C, h // 2, (h % 2) * V1 + 1:(h % 2 + 1) * V1], p_v[p0:p0 + C, q0:q0 + C], k, None, ALU.mult)

            @block.gpsimd
            def _(pool):
                def body(t, s):
                    pool.wait_ge(k_ready, t + 1)
                    wait(pool, q_out[s], (t - s) * 8)
                    pool.tensor_tensor(qst[s][:].rearrange("p (h e) -> p h e", h=H), qk[s][:, 0:D].rearrange("p (h e) -> p h e", h=H),
                                       inv[s][:, 0:H].unsqueeze(2).broadcast_to([P, H, C]), ALU.mult).then_inc(q_ready, 1)
                    wait(pool, summed, t - 1)
                    for u in range(KV_UNITS, H):
                        products(pool, feat[s][:, u, :], kk[s], u)
                    tail = tail1[s][:, :, 0:HT].rearrange("p g (j a i) -> p g j a i", j=4, a=2)
                    k4 = kk[s][:].rearrange("p (g j) e -> p g j e", g=2)
                    pool.tensor_tensor(tail[:, :, :, 0, :], k4[:, :, :, 0:C], k4[:, :, :, DIAGS - 1:WRAP], ALU.mult)
                    pool.tensor_copy(tail[:, :, :, 1, :], k4[:, :, :, 0:C]).then_inc(pool_feats, 1)

                pairs(pool, T, body)

            @block.sync
            def _(sp):
                def body(t, s):
                    sp.wait_ge(row_ready, t + 1)
                    sp.dma_start(node_rows[bass.ts(t, P), :], row[s][:]).then_inc(row_out[s], 16)
                    sp.wait_ge(q_ready, t + 1)
                    sp.dma_start(qn_dram[bass.ts(t, P), :], qst[s][:]).then_inc(q_out[s], 16)

                pairs(sp, T, body)
                for s in range(2):
                    sp.wait_ge(row_out[s], T // 2 * 16)
                    sp.wait_ge(q_out[s], T // 2 * 16)

        G4 = 4
        SP_ = G4 * P
        dst_t = sb("dst_t", [P, SP_, TILES_PER_CHUNK], ctx=early)
        blk_row = sb("blk_row", [1, SP_], I32, ctx=early)
        slot_row = sb("slot_row", [1, SP_], I32, ctx=early)
        need_row = sb("need_row", [1, SP_], I32, ctx=early)
        first_row = sb("first_row", [1, CHUNKS], I32, ctx=early)
        with ExitStack() as c:
            fd = sb("fd", [1, CHUNKS], I32, ctx=c)
            fdf = sb("fdf", [1, CHUNKS], ctx=c)
            ci = sb("ci", [1, CHUNKS], I32, ctx=c)
            cf = sb("cf", [1, CHUNKS], ctx=c)
            scol = sb("scol", [P, G4], ctx=c)
            cmp = sb("cmp", [P, G4, CHUNKS], ctx=c)
            ccol = sb("ccol", [P, G4], ctx=c)
            bcol = sb("bcol", [P, G4], ctx=c)
            b128 = sb("b128", [P, G4], ctx=c)
            cidx = sb("cidx", [P, G4], I32, ctx=c)
            quad = sb("quad", [P, G4], I32, ctx=c)
            slotcol = sb("slotcol", [P, G4], ctx=c)
            needcol = sb("needcol", [P, G4], ctx=c)
            d_rows = [sb(f"d_rows{i}", [P, CHUNK], I32, ctx=c) for i in range(G4)]
            d_f = sb("d_f", [P, CHUNK], ctx=c)
            gmax = sb("gmax", [P, H], ctx=c)
            gmax_all = sb("gmax_all", [P, H], ctx=c)
            shift = sb("shift", [P, T, H], ctx=c)
            p_g = ps("p_g", [P, 512], c)
            p_b = ps("p_b", [P, 512], c)
            p_slot = ps("p_slot", [P, 512], c)
            p_need = ps("p_need", [P, 512], c)
            p_d = ps("p_d", [P, 512], c)
            first_in = sem("first_in", c)
            sums_out = sem("sums_out", c)
            gcol_in = sem("gcol_in", c)
            chunk_nr = sem("chunk_nr", c)
            g_ready = sem("g_ready", c)
            g_spread = sem("g_spread", c)
            b_ready = sem("b_ready", c)
            b_turned = sem("b_turned", c)
            rows_in = [sem(f"rows_in{i}", c) for i in range(G4)]
            rows_ready = sem("rows_ready", c)
            rows_turned = sem("rows_turned", c)
            lists_ready = sem("lists_ready", c)
            gmax_part = sem("gmax_part", c)
            gmax_ready = sem("gmax_ready", c)
            block = c.enter_context(nc.Block())

            @block.sync
            def _(sp):
                sp.dma_start(fd[:], dst_pad[:, 0:1].rearrange("c a -> a c"), allow_slow_non_contiguous=True).then_inc(first_in, 16)
                for h in range(H):
                    j, g = h % 4, h // 4
                    blk = tg_sb[g][j * C:(j + 1) * C, GK + j * C:GK + (j + 1) * C]
                    for half in range(2):
                        sp.dma_start(gram_dram[h, :, half * C:(half + 1) * C], blk).then_inc(sums_out, 16)
                for g in range(2):
                    for k, col in enumerate((GK + P, HT)):
                        sp.dma_start(sums_dram[k, g * P:(g + 1) * P].unsqueeze(1), tg_sb[g][:, col:col + 1],
                                     allow_slow_non_contiguous=True).then_inc(sums_out, 16)
                sp.wait_ge(sums_out, (2 * H + 4) * 16)
                gt, st = gram_dram.tensor, sums_dram.tensor
                HW = C * 2 * C
                for dd in range(4):
                    for m in range(FCH):
                        sp.dma_start(gcol[dd * C:(dd + 1) * C, :, m], bass.AP(gt, dd + 4 * m, [[2 * C + 1, C], [HW, H]]),
                                     allow_slow_non_contiguous=True).then_inc(gcol_in, 16)
                for hh in range(2):
                    sp.dma_start(gtail[hh * TAILW:hh * TAILW + C, :], bass.AP(gt, hh * HW + DIAGS - 1, [[2 * C + 1, C], [2 * HW, H // 2]]),
                                 allow_slow_non_contiguous=True).then_inc(gcol_in, 16)
                    sp.dma_start(gtail[hh * TAILW + C:(hh + 1) * TAILW, :], bass.AP(st, hh * C, [[1, C], [2 * C, H // 2]]),
                                 allow_slow_non_contiguous=True).then_inc(gcol_in, 16)
                sp.dma_start(sum_sb[:], sums_dram[1:2, :]).then_inc(gcol_in, 16)

            @block.gpsimd
            def _(pool):
                pool.iota(ci[:], [[1, CHUNKS]], base=0, channel_multiplier=0).then_inc(chunk_nr, 1)
                pool.wait_ge(gmax_part, 1)
                pool.partition_all_reduce(gmax_all[:], gmax[:], P, RMAX).then_inc(gmax_ready, 1)
                pool.wait_ge(b_ready, 1)
                for g in range(G4):
                    pool.indirect_dma_start(d_rows[g][:], None, dst_pad, bass.IndirectOffsetOnAxis(ap=cidx[:, g:g + 1], axis=0)).then_inc(rows_in[g], 16)

            @block.vector
            def _(dve):
                dve.tensor_reduce(gmax[:], a_s[:].rearrange("p t h -> p h t"), AXX, ALU.max).then_inc(gmax_part, 1)
                dve.wait_ge(first_in, 16)
                dve.wait_ge(chunk_nr, 1)
                dve.tensor_scalar(fd[:], fd[:], P.bit_length() - 1, None, ALU.arith_shift_right)
                dve.tensor_copy(cf[:], ci[:])
                for g in range(G4):
                    dve.tensor_scalar(scol[:, g:g + 1], iota_col[:], float(g * P), None, ALU.add)
                dve.drain()
                dve.tensor_copy(fdf[:], fd[:])
                dve.drain()
                dve.tensor_tensor(fdf[:], fdf[:], cf[:], ALU.add).then_inc(g_ready, 1)
                dve.wait_ge(g_spread, 1)
                for g in range(G4):
                    dve.tensor_scalar(cmp[:, g, 1:CHUNKS], p_g[:, 1:CHUNKS], scol[:, g:g + 1], None, ALU.is_le)
                dve.drain()
                dve.tensor_reduce(ccol[:], cmp[:, :, 1:CHUNKS], AXX, ALU.add)
                dve.drain()
                dve.tensor_copy(cidx[:], ccol[:])
                dve.tensor_tensor(bcol[:], scol[:], ccol[:], ALU.subtract)
                dve.tensor_scalar(needcol[:], ccol[:], 1.0, None, ALU.add)
                dve.tensor_copy(first_row[:], fdf[:])
                dve.drain()
                dve.tensor_scalar(quad[:], cidx[:], R.bit_length() - 1, None, ALU.arith_shift_right)
                dve.tensor_scalar(b128[:], bcol[:], float(P), None, ALU.mult)
                dve.drain()
                dve.tensor_copy(slotcol[:], quad[:])
                dve.drain()
                dve.scalar_tensor_tensor(out=slotcol[:], in0=slotcol[:], scalar=-float(R), in1=ccol[:], op0=ALU.mult, op1=ALU.add).then_inc(b_ready, 1)
                dve.wait_ge(gmax_ready, 1)
                dve.tensor_tensor(shift[:], adm[:, :, 0:H], gmax_all[:].unsqueeze(1).broadcast_to([P, T, H]), ALU.add)
                dve.memset(acc[:], 0.0)
                dve.drain()
                dve.scalar_tensor_tensor(out=adm[:, :, H:2 * H], in0=shift[:], scalar=SLOPE, in1=shift[:], op0=ALU.mult, op1=ALU.max)
                dve.drain()
                for part in range(3):
                    dve.tensor_copy(adm_parts[:, :, part, :], adm[:])
                    dve.drain()
                    if part < 2:
                        dve.tensor_tensor(adm[:], adm[:], adm_parts[:, :, part, :], ALU.subtract)
                        dve.drain()
                dve.wait_ge(b_turned, 1)
                dve.tensor_scalar(blk_row[:], p_b[0:1, :], float(T - 1), None, ALU.min)
                dve.tensor_copy(slot_row[:], p_slot[0:1, :])
                dve.tensor_copy(need_row[:], p_need[0:1, :])
                for g in range(G4):
                    dve.wait_ge(rows_in[g], 16)
                    wait(dve, rows_turned, g)
                    dve.tensor_copy(d_f[:], d_rows[g][:])
                    dve.drain()
                    dve.tensor_scalar(d_f[:], d_f[:], b128[:, g:g + 1], None, ALU.subtract).then_inc(rows_ready, 1)
                    dve.wait_ge(rows_turned, g + 1)
                    dve.tensor_copy(dst_t[:, g * P:(g + 1) * P, :].rearrange("p s u -> p u s"), p_d[:].rearrange("p (u s) -> p u s", u=4)).then_inc(lists_ready, 1)
                dve.wait_ge(gcol_in, (4 * FCH + 5) * 16)
                dve.tensor_scalar(vsum_w[:].rearrange("p (h e) -> p h e", h=H)[:, :, 1:V1],
                                  sum_sb[:].rearrange("p (h e) -> p h e", h=H), SCALE ** 4 * C_COEF, None, ALU.mult)
                dve.tensor_tensor(mix_w[:, :, :, 0], gcol[:], coef[:].unsqueeze(1).broadcast_to([P, H, FCH]), ALU.mult)
                for hh in range(2):
                    for a, k in enumerate(tails):
                        p0 = hh * TAILW + a * C
                        dve.tensor_scalar(mix_tail[p0:p0 + C, :, hh * V1], gtail[p0:p0 + C, :], k, None, ALU.mult)

            @block.tensor
            def _(pe):
                pe.wait_ge(g_ready, 1)
                pe.matmul(p_g[:, 0:CHUNKS], ones[0:1, :], fdf[:], start=True, stop=True).then_inc(g_spread, 1)
                pe.wait_ge(b_ready, 1)
                for g in range(G4):
                    for bank, col in ((p_b, bcol), (p_slot, slotcol), (p_need, needcol)):
                        mm = pe.matmul(bank[0:1, g * P:(g + 1) * P], col[:, g:g + 1], ident[:], start=True, stop=True)
                mm.then_inc(b_turned, 1)
                for g in range(G4):
                    pe.wait_ge(rows_ready, g + 1)
                    wait(pe, lists_ready, g)
                    d3 = d_f[:].rearrange("c (p u) -> c u p", u=TILES_PER_CHUNK)
                    for u in range(TILES_PER_CHUNK):
                        mm = pe.transpose(p_d[:, u * P:(u + 1) * P], d3[:, u, :], ident[:])
                    mm.then_inc(rows_turned, 1)

        TC = TILES_PER_CHUNK
        with ExitStack() as c:
            idx = [sb(f"idx{i}", [P, TC], I32, ctx=c) for i in range(R)]
            rows_g = sb("rows_g", [P, R, TC, ROW], ctx=c)
            msg = [sb(f"msg{i}", [P, TC, ROW], ctx=c) for i in range(2)]
            sel_bf = [sb(f"sel_bf{i}", [P, TC, P], BF16, ctx=c) for i in range(2)]
            sel = [sb(f"sel{i}", [P, TC * P], ctx=c) for i in range(2)]
            sel_t = [sb(f"sel_t{i}", [P, TC * P], BF16, ctx=c) for i in range(2)]
            lg = [sb(f"lg{i}", [P, TC, H], ctx=c) for i in range(2)]
            qs = sb("qs", [P, D], ctx=c)
            qq = sb("qq", [P, H, WRAP], ctx=c)
            feat = [sb(f"qfeat{i}", [P, FEAT], ctx=c) for i in range(3)]
            feat_t = [sb(f"qfeat_t{i}", [P, FEAT], ctx=c) for i in range(3)]
            ry = sb("ry", [P, H], ctx=c)
            yn = sb("yn", [P, D], ctx=c)
            yt = sb("yt", [P, D], ctx=c)
            p_st = c.enter_context(nc.psum_tensor("p_st", [P, 2 * TC * P], BF16))
            p_m = [ps(f"p_m{i}", [P, 512], c) for i in range(2)]
            p_ft = [ps(f"p_ft{i}", [P, 512], c) for i in range(2)]
            p_y = ps("p_y", [P, 512], c)
            p_o = ps("p_o", [P, 512], c)
            p_eb = ps("p_e", [P, 512], c)
            q_in = sem("q_in", c)
            q_doubled = sem("q_doubled", c)
            feat_ready = sem("qfeat_ready", c)
            feat_turned = sem("feat_turned", c)
            feat_t_ready = sem("feat_t_ready", c)
            feat_t_used = sem("feat_t_used", c)
            y_taken = sem("y_taken", c)
            yt_in_psum = sem("yt_in_psum", c)
            yt_ready = sem("yt_ready", c)
            mix_ready = sem("mix_ready", c)
            mix_added = sem("mix_added", c)
            idx_in = [sem(f"idx_in{i}", c) for i in range(R)]
            chunks_in = sem("chunks_in", c)
            gather_opened = sem("gather_opened", c)
            gathered = [sem(f"gathered{i}", c) for i in range(R)]
            sel_ready = sem("sel_ready", c)
            sel_wide = sem("sel_wide", c)
            sel_turned = sem("sel_turned", c)
            sel_t_ready = sem("sel_t_ready", c)
            dst_spread = sem("dst_spread", c)
            logit_ready = sem("logit_ready", c)
            weight_ready = sem("weight_ready", c)
            msg_ready = sem("msg_ready", c)
            msg_summed = sem("msg_summed", c)
            acc_added = sem("acc_added", c)
            block = c.enter_context(nc.Block())

            def rounds(eng, body):
                for k in range(OCT):
                    body(k, k, 0, None)
                with eng.Fori(1, T) as i:
                    for k in range(OCT):
                        body(i * OCT + k, k, i, i - 1)
                for k in range(OCT):
                    body(T * OCT + k, k, None, T - 1)
                with eng.Fori(T + 1, STEPS // OCT) as i:
                    for k in range(OCT):
                        body(i * OCT + k, k, None, None)

            def units(k):
                return (H - 1, H) if k == OCT - 1 else (k,)

            def pe_st(j):
                return p_st[:, (j % 2) * TC * P:(j % 2 + 1) * TC * P]

            def p_e(j):
                return p_eb[:, (j % 2) * TC * 2 * H:(j % 2 + 1) * TC * 2 * H]

            def chunk_in(ch, j):
                return (ch - j) * (16 * TC // R) + 16 * TC

            @block.gpsimd
            def _(pool):
                def last_use(ch):
                    return pool.value_load(first_row[0:1, bass.ds(ch - (R - 1), 1)], min_val=1, max_val=STEPS)

                def body(ch, j, done):
                    if done is not None:
                        pool.wait_ge(msg_ready, done)
                    pool.wait_ge(idx_in[j], (ch - j) * (16 // R) + 16)
                    pool.sem_inc(gather_opened, 1)
                    for u in range(TC):
                        pool.indirect_dma_start(rows_g[:, j, u, :], None, node_rows,
                                                bass.IndirectOffsetOnAxis(ap=idx[j][:, u:u + 1], axis=0)).then_inc(gathered[j], 16)
                    if not (isinstance(ch, int) and ch == 0):
                        k = (j - 1) % R
                        pool.wait_ge(gathered[k], chunk_in(ch - 1, k))
                        pool.sem_inc(chunks_in, 1)

                for j in range(R):
                    body(j, j, None)
                with pool.Fori(1, CHUNKS // R) as i:
                    done = [last_use(i * R + j) for j in range(R)]
                    for j in range(R):
                        body(i * R + j, j, done[j])
                pool.wait_ge(gathered[R - 1], chunk_in(CHUNKS - 1, R - 1))
                pool.sem_inc(chunks_in, 1)

            @block.sync
            def _(sp):
                def body(ch, j):
                    if not (isinstance(ch, int) and ch < R):
                        sp.wait_ge(gathered[j], chunk_in(ch - R, j))
                    sp.dma_start(idx[j][:], src_pad[bass.ds(ch, 1), :].rearrange("a (p u) -> (a p) u", u=TC)).then_inc(idx_in[j], 16)

                for j in range(R):
                    body(j, j)
                with sp.Fori(1, CHUNKS // R) as i:
                    for j in range(R):
                        body(i * R + j, j)

            @block.scalar
            def _(act):
                def query(t):
                    wait(act, q_doubled, t)
                    act.dma_start(qs[:], qn_dram[bass.ts(t, P), :]).then_inc(q_in, 16)

                def widen(s, j):
                    act.wait_ge(sel_ready, s + 1)
                    wait(act, msg_summed, s - 1)
                    act.copy(sel[j % 2][:], sel_bf[j % 2][:].rearrange("p u d -> p (u d)")).then_inc(sel_wide, 1)

                def take_turned(s, j):
                    need = act.value_load(need_row[0:1, bass.ds(s, 1)], min_val=1, max_val=CHUNKS)
                    act.wait_ge(chunks_in, need)
                    act.wait_ge(sel_turned, s + 1)
                    wait(act, dst_spread, s - 1)
                    act.copy(sel_t[j % 2][:], pe_st(j)).then_inc(sel_t_ready, 1)

                def take(n, u):
                    act.wait_ge(feat_turned, n + 1)
                    wait(act, feat_t_used, n - 2)
                    act.copy(feat_t[u % 3][:], p_ft[u % 2][:]).then_inc(feat_t_ready, 1)

                def body(s, k, tile, last):
                    j = k % R
                    take_turned(s + 1, j + 1)
                    wait(act, msg_summed, s - 1)
                    act.wait_ge(logit_ready, s + 1)
                    act.activation(msg[j % 2][:, :, D:ROW], lg[j % 2][:], ACT.Exp).then_inc(weight_ready, 1)
                    widen(s + 1, j + 1)
                    if last is not None and k == 3:
                        act.wait_ge(yt_in_psum, last + 1)
                        act.copy(yt[:], p_o[:, 0:D]).then_inc(yt_ready, 1)
                    if tile is not None:
                        for u in units(k):
                            take(tile * UNITS + u, u)
                        if k == 1:
                            query(tile + 1)

                query(0)
                widen(0, 0)
                take_turned(0, 0)
                rounds(act, body)
                act.wait_ge(q_in, (T + 1) * 16)

            @block.vector
            def _(dve):
                def select(s, j):
                    wait(dve, sel_wide, s - 1)
                    wait(dve, sel_turned, s - 1)
                    for u in range(TC):
                        a = dve.tensor_scalar(sel_bf[j % 2][:, u, :], iota_bf[:], dst_t[:, bass.ds(s, 1), u:u + 1].rearrange("p s u -> p (s u)"),
                                              None, ALU.is_equal)
                    a.then_inc(sel_ready, 1)

                def block_of(s):
                    return dve.value_load(blk_row[0:1, bass.ds(s, 1)], min_val=0, max_val=T - 1)

                def accumulate(s, j, b):
                    a = acc[:, bass.ds(b, 1), :].rearrange("p a f -> p (a f)")
                    dve.wait_ge(msg_summed, s + 1)
                    dve.tensor_tensor(a, a, p_m[j % 2][:, 0:ROW], ALU.add).then_inc(acc_added, 1)

                def query(k, tile, last):
                    if last is not None and k == 1:
                        dve.wait_ge(feat_t_used, last * UNITS + UNITS)
                        y3 = p_y[:, 0:H * V1].rearrange("p (h e) -> p h e", h=H)
                        dve.reciprocal(ry[:], y3[:, :, 0])
                        dve.drain()
                        dve.tensor_tensor(yn[:].rearrange("p (h e) -> p h e", h=H), y3[:, :, 1:V1],
                                          ry[:].unsqueeze(2).broadcast_to([P, H, C]), ALU.mult).then_inc(y_taken, 1)
                    if last is not None and k == 5:
                        r = resid[:, bass.ds(last, 1), :].rearrange("p a f -> p (a f)")
                        dve.wait_ge(mix_ready, last + 1)
                        dve.tensor_tensor(r, r, p_o[:, 0:D], ALU.add).then_inc(mix_added, 1)
                        dve.drain()
                        dve.tensor_tensor(r, r, b_proj[:], ALU.add)
                    if tile is not None:
                        if k == 0:
                            dve.wait_ge(q_in, tile * 16 + 16)
                            dve.tensor_copy(qq[:, :, 0:C], qs[:].rearrange("p (h e) -> p h e", h=H))
                            dve.tensor_copy(qq[:, :, C:WRAP], qs[:].rearrange("p (h e) -> p h e", h=H)[:, :, 0:WRAP - C]).then_inc(q_doubled, 1)
                            dve.drain()
                        for u in units(k):
                            wait(dve, feat_turned, tile * UNITS + (u - 2))
                            products(dve, feat[u % 3][:], qq, u).then_inc(feat_ready, 1)

                def body(s, k, tile, last):
                    j = k % R
                    if not (isinstance(s, int) and s < 2):
                        b = block_of(s - 2)
                    slot = dve.value_load(slot_row[0:1, bass.ds(s, 1)], min_val=0, max_val=R - 1)
                    select(s + 1, j + 1)
                    dve.wait_ge(dst_spread, s + 1)
                    g3 = rows_g[:, bass.ds(slot, 1), :, :].rearrange("p a u f -> p (a u) f")
                    pe3 = p_e(j).rearrange("p (u a) -> p u a", u=TC)
                    l = lg[j % 2]
                    dve.tensor_tensor(l[:], g3[:, :, D:ROW], pe3[:, :, 0:H], ALU.add)
                    dve.drain()
                    dve.scalar_tensor_tensor(out=l[:], in0=l[:], scalar=SLOPE, in1=l[:], op0=ALU.mult, op1=ALU.max)
                    dve.drain()
                    dve.tensor_tensor(l[:], l[:], pe3[:, :, H:2 * H], ALU.subtract).then_inc(logit_ready, 1)
                    if not (isinstance(s, int) and s < 2):
                        accumulate(s - 2, j - 2, b)
                    query(k, tile, last)
                    dve.wait_ge(weight_ready, s + 1)
                    m4 = msg[j % 2][:, :, 0:D].rearrange("p u (h e) -> p u h e", h=H)
                    dve.tensor_tensor(m4, g3[:, :, 0:D].rearrange("p u (h e) -> p u h e", h=H), msg[j % 2][:, :, D:ROW].unsqueeze(3).broadcast_to([P, TC, H, C]), ALU.mult).then_inc(msg_ready, 1)

                select(0, 0)
                rounds(dve, body)
                for s in (STEPS - 2, STEPS - 1):
                    dve.drain()
                    accumulate(s, s % R, block_of(s))
                dve.drain()

            @block.tensor
            def _(pe):
                def turn(s, j):
                    pe.wait_ge(sel_ready, s + 1)
                    wait(pe, sel_t_ready, s)
                    for u in range(TC):
                        mm = pe.transpose(pe_st(j)[:, u * P:(u + 1) * P], sel_bf[j % 2][:, u, :], ident_bf[:])
                    mm.then_inc(sel_turned, 1)

                def block_of(s):
                    return pe.value_load(blk_row[0:1, bass.ds(s, 1)], min_val=0, max_val=T - 1)

                def spread(s, j, b):
                    wait(pe, logit_ready, s)
                    pe.wait_ge(sel_t_ready, s + 1)
                    for u in range(TC):
                        for part in range(3):
                            mm = pe.matmul(p_e(j)[:, u * 2 * H:(u + 1) * 2 * H], sel_t[j % 2][:, u * P:(u + 1) * P],
                                           adm_parts[:, bass.ds(b, 1), part, :].rearrange("p a f -> p (a f)"), start=(part == 0), stop=(part == 2))
                    mm.then_inc(dst_spread, 1)

                def aggregate(s, j):
                    wait(pe, acc_added, s - 1)
                    pe.wait_ge(msg_ready, s + 1)
                    pe.wait_ge(sel_wide, s + 1)
                    for u in range(TC):
                        mm = pe.matmul(p_m[j % 2][:, 0:ROW], sel[j % 2][:, u * P:(u + 1) * P], msg[j % 2][:, u, :], start=(u == 0), stop=(u == TC - 1))
                    mm.then_inc(msg_summed, 1)

                def turn_features(n, u):
                    pe.wait_ge(feat_ready, n + 1)
                    wait(pe, feat_t_ready, n if u == 0 else n - 1)
                    for m in range(FCH):
                        mm = pe.transpose(p_ft[u % 2][:, m * P:(m + 1) * P], feat[u % 3][:, m * P:(m + 1) * P], ident[:])
                    mm.then_inc(feat_turned, 1)

                def sum_features(tile, u):
                    if u == 0:
                        wait(pe, y_taken, tile)
                        pe.matmul(p_y[:, 0:H * V1], ones[0:1, :], vsum_w[:], start=True, stop=False, skip_group_check=True)
                    pe.wait_ge(feat_t_ready, tile * UNITS + (u + 1))
                    for m in range(FCH):
                        if u < H:
                            o, w = p_y[:, u * V1:(u + 1) * V1], mix_w[:, u, m, :]
                        else:
                            o, w = p_y[:, 2 * m * V1:(2 * m + 2) * V1], mix_tail[:, m, :]
                        mm = pe.matmul(o, feat_t[u % 3][:, m * P:(m + 1) * P], w, start=False, stop=(u == H and m == FCH - 1),
                                       skip_group_check=True)
                    mm.then_inc(feat_t_used, 1)

                def body(s, k, tile, last):
                    j = k % R
                    b = block_of(s + 1)
                    turn(s + 1, j + 1)
                    if not (isinstance(s, int) and s == 0):
                        aggregate(s - 1, (j - 1) % R)
                    if last is not None:
                        if k == 0:
                            sum_features(last, H)
                        if k == 2:
                            pe.wait_ge(y_taken, last + 1)
                            wait(pe, mix_added, last)
                            for m in range(2):
                                mm = pe.transpose(p_o[:, m * P:(m + 1) * P], yn[:, m * P:(m + 1) * P], ident[:])
                            mm.then_inc(yt_in_psum, 1)
                        if k == 4:
                            pe.wait_ge(yt_ready, last + 1)
                            for m in range(2):
                                mm = pe.matmul(p_o[:, 0:D], yt[:, m * P:(m + 1) * P], wp_t[:, m, :], start=(m == 0), stop=(m == 1))
                            mm.then_inc(mix_ready, 1)
                    if tile is not None:
                        for u in units(k):
                            turn_features(tile * UNITS + u, u)
                            if u == units(k)[0]:
                                spread(s + 1, j + 1, b)
                            if u:
                                sum_features(tile, u - 1)
                    else:
                        spread(s + 1, j + 1, b)

                turn(0, 0)
                spread(0, 0, block_of(0))
                rounds(pe, body)
                aggregate(STEPS - 1, (STEPS - 1) % R)

        early.close()

        late = ExitStack()
        PHASES, TP = 5, T // 5
        xl = acc[:, :, 0:D]
        top_w = sb("top_w", [P, T, 2], ctx=late)
        places = sb("places", [P, 2, T], I32, ctx=late)
        y_places = sb("y_places", [P, 2, T], I32, ctx=late)
        exp_row = sb("exp_row", [1, P], I32, ctx=late)
        tile_row = sb("tile_row", [1, P], I32, ctx=late)
        g_b = sb("g_b", [P, D], ctx=late)
        be_b = sb("be_b", [P, D], ctx=late)
        with ExitStack() as c:
            gw = sb("gw", [P, 2, NEXP], ctx=c)
            gb = sb("gb", [P, NEXP], ctx=c)
            st = sb("m_st", [P, T, 6], ctx=c)
            ag = sb("m_ag", [P, T, 2], ctx=c)
            rs = sb("m_rs", [P, T], ctx=c)
            var_ready = sem("m_var_ready", c)
            std_ready = sem("m_std_ready", c)
            xt = [sb(f"m_xt{i}", [P, 2 * D], ctx=c) for i in range(2)]
            lgt = sb("m_lg", [P, T, NEXP], ctx=c)
            top8 = sb("top8", [P, T, 8], ctx=c)
            idx8 = sb("idx8", [P, T, 8], U32, ctx=c)
            idf = sb("idf", [P, T, 2], ctx=c)
            oh = [sb(f"oh{i}", [P, T, NEXP], ctx=c) for i in range(2)]
            oh_pos = [sb(f"oh_pos{i}", [P, TP, NEXP], ctx=c) for i in range(2)]
            moved = sb("moved", [P, NEXP], ctx=c)
            placey = sb("placey", [P, 2, T], ctx=c)
            cnt = sb("cnt", [P, TP, NEXP], ctx=c)
            tri = sb("tri", [P, P], ctx=c)
            pos = sb("pos", [P, TP, NEXP], ctx=c)
            toe = sb("toe", [P, NEXP, TP], ctx=c)
            keep = sb("keep", [P, NEXP, TP], ctx=c)
            run = sb("run", [P, NEXP, TP], ctx=c)
            offs = sb("offs", [P, NEXP], ctx=c)
            offs_i = sb("offs_i", [1, NEXP], I32, ctx=c)
            ti = sb("ti", [P, NEXP], I32, ctx=c)
            tf = sb("tf", [P, NEXP], ctx=c)
            zf = sb("zf", [P, NEXP], ctx=c)
            ends = sb("ends", [P, NEXP], ctx=c)
            base = sb("base", [P, NEXP], ctx=c)
            placef = sb("placef", [P, 2, T], ctx=c)
            ecmp = sb("ecmp", [P, NEXP], ctx=c)
            ecol = sb("ecol", [P, 2], ctx=c)
            used = sb("used", [P, 1], ctx=c)
            begin = sb("begin", [P, 1], ctx=c)
            zpad = sb("zpad", [P, SLOT_ROWS // P, D], ctx=c)
            p_x = [ps(f"m_px{i}", [P, 512], c) for i in range(2)]
            p_l = [ps(f"m_pl{i}", [P, 512], c) for i in range(2)]
            p_r = [ps(f"m_pr{i}", [P, 512], c) for i in range(2)]
            p_e = ps("m_pe", [P, 512], c)
            w_in = sem("m_w_in", c)
            scaled = sem("scaled", c)
            biased = sem("biased", c)
            xl_ready = sem("xl_ready", c)
            x_turned = sem("x_turned", c)
            xt_ready = sem("m_xt_ready", c)
            logits = sem("logits", c)
            logits_taken = sem("logits_taken", c)
            tops = sem("tops", c)
            exps = sem("exps", c)
            cnt_ready = sem("cnt_ready", c)
            ranked = sem("ranked", c)
            tri_ready = sem("tri_ready", c)
            places_ready = sem("places_ready", c)
            ends_ready = sem("ends_ready", c)
            padded = sem("padded", c)
            sent = sem("sent", c)
            ecol_ready = sem("ecol_ready", c)
            erow_in_psum = sem("erow_in_psum", c)
            block = c.enter_context(nc.Block())
            PC = TP * NEXP
            GT = 5
            GROUPS = TP // GT
            AHEAD = 3

            @block.sync
            def _(sp):
                sp.dma_start(gw[:], gate_w.rearrange("(c k) e -> k c e", k=P)).then_inc(w_in, 16)
                sp.dma_start(gb[:], bcast_rows(gate_b, NEXP)).then_inc(w_in, 16)
                sp.dma_start(g_b[:], bcast_rows(gamma, D)).then_inc(w_in, 16)
                sp.dma_start(be_b[:], bcast_rows(beta, D)).then_inc(w_in, 16)
                sp.wait_ge(ends_ready, 1)
                for e in range(NEXP):
                    n = sp.value_load(offs_i[0:1, e:e + 1], min_val=e * EXP_TILES * SLOT_ROWS, max_val=e * EXP_TILES * SLOT_ROWS + N)
                    sp.dma_start(slot_x[bass.ds(n, SLOT_ROWS), :].rearrange("(p a) f -> p a f", p=P), zpad[:]).then_inc(padded, 16)
                sp.wait_ge(padded, NEXP * 16)

            @block.vector
            def _(dve):
                def scale(ph):
                    for g in range(ph * GROUPS, (ph + 1) * GROUPS):
                        a4 = acc[:, g * GT:(g + 1) * GT, 0:D].rearrange("p t (h e) -> p t h e", h=H)
                        dve.tensor_tensor(a4, a4, acc[:, g * GT:(g + 1) * GT, D:ROW].unsqueeze(3).broadcast_to([P, GT, H, C]), ALU.mult).then_inc(scaled, 1)

                def residual(ph):
                    for g in range(ph * GROUPS, (ph + 1) * GROUPS):
                        r = resid[:, g * GT:(g + 1) * GT, :]
                        dve.wait_ge(biased, g + 1)
                        dve.scalar_tensor_tensor(out=r, in0=acc[:, g * GT:(g + 1) * GT, 0:D], scalar=0.0, in1=r, op0=ALU.max, op1=ALU.add)
                    dve.drain()
                    for t in range(ph * TP, (ph + 1) * TP):
                        dve.bn_stats(st[:, t, :], resid[:, t, :])
                    if ph + AHEAD < PHASES:
                        scale(ph + AHEAD)
                    dve.drain()
                    span = slice(ph * TP, (ph + 1) * TP)
                    moments(dve, ag[:, span, :], st[:, span, :])
                    dve.tensor_scalar(rs[:, span], ag[:, span, 1], LN_EPS, None, ALU.add).then_inc(var_ready, 1)

                def norm(ph):
                    span = slice(ph * TP, (ph + 1) * TP)
                    dve.wait_ge(std_ready, ph + 1)
                    dve.reciprocal(rs[:, span], rs[:, span])
                    dve.drain()
                    for t in range(ph * TP, (ph + 1) * TP):
                        dve.tensor_scalar(xl[:, t, :], resid[:, t, :], ag[:, t, 0:1], rs[:, t:t + 1], ALU.subtract, ALU.mult).then_inc(xl_ready, 1)

                w = acc[:, :, D:ROW]
                dve.tensor_scalar(w, w, TINY, None, ALU.max)
                dve.drain()
                dve.reciprocal(w, w)
                dve.drain()
                for ph in range(AHEAD):
                    scale(ph)
                dve.memset(zpad[:], 0.0)
                dve.memset(keep[:], 1.0)
                dve.memset(zf[:], 0.0)
                dve.tensor_scalar(offs[:], iota_row[:, 0:NEXP], float(EXP_TILES * SLOT_ROWS), None, ALU.mult)
                dve.drain()
                dve.memset(keep[:, :, 0:1], 0.0)
                dve.wait_ge(w_in, 64)
                def choose(ph):
                    tiles = range(ph * TP, (ph + 1) * TP)
                    span = slice(ph * TP, (ph + 1) * TP)
                    dve.wait_ge(logits, (ph + 1) * TP // 2)
                    dve.tensor_tensor(lgt[:, span, :], p_l[ph % 2][:, 0:PC].rearrange("p (t e) -> p t e", e=NEXP),
                                      gb[:].unsqueeze(1).broadcast_to([P, TP, NEXP]), ALU.add).then_inc(logits_taken, 1)
                    dve.drain()
                    for t in tiles:
                        dve.max(top8[:, t, :], lgt[:, t, :])
                    dve.drain()
                    for t in tiles:
                        dve.max_index(idx8[:, t, :], top8[:, t, :], lgt[:, t, :])
                    dve.drain()
                    dve.tensor_copy(idf[:, span, :], idx8[:, span, 0:2])
                    dve.drain()
                    for k in range(2):
                        dve.tensor_tensor(oh[k][:, span, :], idf[:, span, k:k + 1].broadcast_to([P, TP, NEXP]),
                                          iota_row[:, 0:NEXP].unsqueeze(1).broadcast_to([P, TP, NEXP]), ALU.is_equal)
                    dve.drain()
                    dve.tensor_tensor(cnt[:], oh[0][:, span, :], oh[1][:, span, :], ALU.add)
                    dve.drain()
                    dve.tensor_tensor(cnt[:], cnt[:], valid[:, span].unsqueeze(2).broadcast_to([P, TP, NEXP]), ALU.mult).then_inc(cnt_ready, 1)

                def place(ph):
                    span = slice(ph * TP, (ph + 1) * TP)
                    dve.wait_ge(ranked, ph + 1)
                    dve.tensor_copy(toe[:].rearrange("p e t -> p t e"), p_r[ph % 2][:, PC:2 * PC].rearrange("p (t e) -> p t e", e=NEXP))
                    dve.drain()
                    dve.tensor_tensor_scan(run[:].rearrange("p e t -> p (e t)"), keep[:].rearrange("p e t -> p (e t)"),
                                           toe[:].rearrange("p e t -> p (e t)"), 0.0, ALU.mult, ALU.add)
                    dve.drain()
                    dve.tensor_tensor(toe[:], run[:], toe[:], ALU.subtract)
                    dve.drain()
                    dve.tensor_tensor(pos[:], toe[:].rearrange("p e t -> p t e"), p_r[ph % 2][:, 0:PC].rearrange("p (t e) -> p t e", e=NEXP), ALU.add)
                    dve.drain()
                    dve.tensor_tensor(pos[:], pos[:], offs[:].unsqueeze(1).broadcast_to([P, TP, NEXP]), ALU.add)
                    dve.drain()
                    dve.tensor_tensor(offs[:], offs[:], run[:, :, TP - 1], ALU.add)
                    for k in range(2):
                        dve.tensor_tensor(oh_pos[k][:], oh[k][:, span, :], pos[:], ALU.mult)
                    dve.drain()
                    for k in range(2):
                        dve.tensor_reduce(placef[:, k, span], oh_pos[k][:], AXX, ALU.add)
                    dve.drain()
                    dve.tensor_copy(places[:, :, span], placef[:, :, span]).then_inc(places_ready, 1)

                for ph in range(PHASES + 1):
                    if ph < PHASES:
                        residual(ph)
                    if ph:
                        choose(ph - 1)
                    if ph < PHASES:
                        norm(ph)
                    if ph:
                        place(ph - 1)
                dve.tensor_copy(offs_i[:], offs[0:1, :]).then_inc(ends_ready, 1)
                dve.tensor_tensor(top_w[:, :, 1:2], top8[:, :, 1:2], top8[:, :, 0:1], ALU.subtract).then_inc(tops, 1)
                dve.tensor_scalar(tf[:], iota_row[:, 0:NEXP], -float(EXP_TILES * SLOT_ROWS), None, ALU.mult)
                dve.drain()
                dve.tensor_tensor(tf[:], offs[:], tf[:], ALU.add)
                dve.drain()
                dve.tensor_scalar(tf[:], tf[:], float(SLOT_ROWS - 1), None, ALU.add)
                dve.drain()
                dve.tensor_copy(ti[:], tf[:])
                dve.drain()
                dve.tensor_scalar(ti[:], ti[:], SLOT_ROWS.bit_length() - 1, None, ALU.arith_shift_right)
                dve.drain()
                dve.tensor_copy(tf[:], ti[:])
                dve.drain()
                dve.tensor_tensor_scan(ends[:], tf[:], zf[:], 0.0, ALU.add, ALU.add)
                dve.drain()
                dve.tensor_tensor(base[:], ends[:], tf[:], ALU.subtract)
                dve.tensor_scalar(moved[:], iota_row[:, 0:NEXP], float(EXP_TILES), None, ALU.mult)
                dve.drain()
                dve.tensor_tensor(moved[:], base[:], moved[:], ALU.subtract)
                dve.drain()
                dve.tensor_scalar(moved[:], moved[:], float(SLOT_ROWS), None, ALU.mult)
                dve.tensor_tensor(used[:], ends[:, NEXP - 1:NEXP], iota_col[:], ALU.is_gt)
                dve.drain()
                dve.tensor_scalar(ecmp[:], base[:], iota_col[:], None, ALU.is_le)
                dve.drain()
                dve.tensor_reduce(ecol[:, 0:1], ecmp[:, 1:NEXP], AXX, ALU.add)
                dve.tensor_tensor(base[:], base[:], ecmp[:], ALU.mult)
                dve.drain()
                dve.tensor_reduce(begin[:], base[:], AXX, ALU.max)
                dve.drain()
                dve.scalar_tensor_tensor(out=begin[:], in0=ecol[:, 0:1], scalar=float(EXP_TILES), in1=begin[:], op0=ALU.mult, op1=ALU.subtract)
                dve.drain()
                dve.scalar_tensor_tensor(out=begin[:], in0=begin[:], scalar=float(SPARE), in1=iota_col[:], op0=ALU.subtract, op1=ALU.add)
                dve.drain()
                dve.tensor_tensor(begin[:], begin[:], used[:], ALU.mult)
                dve.drain()
                dve.tensor_scalar(ecol[:, 1:2], begin[:], float(SPARE), None, ALU.add).then_inc(ecol_ready, 1)
                for k in range(2):
                    dve.tensor_tensor(oh[k][:], oh[k][:], moved[:].unsqueeze(1).broadcast_to([P, T, NEXP]), ALU.mult)
                dve.drain()
                for k in range(2):
                    dve.tensor_reduce(placey[:, k, :], oh[k][:], AXX, ALU.add)
                dve.drain()
                dve.tensor_tensor(placey[:], placey[:], placef[:], ALU.add)
                dve.drain()
                dve.tensor_copy(y_places[:], placey[:])
                dve.wait_ge(exps, 1)
                dve.tensor_scalar(top_w[:, :, 0:1], top_w[:, :, 1:2], 1.0, None, ALU.add)
                dve.drain()
                dve.reciprocal(top_w[:, :, 0:1], top_w[:, :, 0:1])
                dve.drain()
                dve.tensor_tensor(top_w[:, :, 1:2], top_w[:, :, 1:2], top_w[:, :, 0:1], ALU.mult)
                dve.wait_ge(erow_in_psum, 1)
                dve.tensor_copy(exp_row[:], p_e[0:1, 0:P])
                dve.tensor_copy(tile_row[:], p_e[0:1, P:2 * P])
                for g in range(T // GT):
                    q = resid[:, g * GT:(g + 1) * GT, :]
                    dve.tensor_tensor(q, q, be_b[:].unsqueeze(1).broadcast_to([P, GT, D]), ALU.add)

            @block.scalar
            def _(act):
                def body(u, s):
                    act.wait_ge(x_turned, u + 1)
                    wait(act, logits, u - 1)
                    act.copy(xt[s][:], p_x[s][:]).then_inc(xt_ready, 1)
                for u in range(T // 2):
                    if u % (TP // 2) == 0:
                        ph = u // (TP // 2)
                        act.wait_ge(var_ready, ph + 1)
                        act.sqrt(rs[:, ph * TP:(ph + 1) * TP], rs[:, ph * TP:(ph + 1) * TP]).then_inc(std_ready, 1)
                    body(u, u % 2)
                act.wait_ge(tops, 1)
                act.activation(top_w[:, :, 1:2], top_w[:, :, 1:2], ACT.Exp).then_inc(exps, 1)

            @block.tensor
            def _(pe):
                def turn(u, s):
                    pe.wait_ge(xl_ready, 2 * u + 2)
                    wait(pe, xt_ready, u - 1)
                    for a in range(2):
                        for k in range(2):
                            mm = pe.transpose(p_x[s][:, (2 * a + k) * P:(2 * a + k + 1) * P], xl[:, 2 * u + a, k * P:(k + 1) * P], ident[:])
                    mm.then_inc(x_turned, 1)

                def gate(u, s):
                    pe.wait_ge(xt_ready, u + 1)
                    if u % (TP // 2) == 0:
                        wait(pe, logits_taken, u // (TP // 2) - 1)
                    for a in range(2):
                        t = 2 * u + a
                        col = t % TP * NEXP
                        for k in range(2):
                            mm = pe.matmul(p_l[t // TP % 2][:, col:col + NEXP], xt[s][:, (2 * a + k) * P:(2 * a + k + 1) * P], gw[:, k, :],
                                           start=(k == 0), stop=(k == 1))
                    mm.then_inc(logits, 1)

                def rank(ph):
                    pe.wait_ge(tri_ready, 1)
                    pe.wait_ge(cnt_ready, ph + 1)
                    wait(pe, places_ready, ph - 1)
                    c2 = cnt[:].rearrange("p t e -> p (t e)")
                    pe.matmul(p_r[ph % 2][:, 0:PC], tri[:], c2, start=True, stop=True)
                    pe.matmul(p_r[ph % 2][:, PC:2 * PC], ones[:], c2, start=True, stop=True).then_inc(ranked, 1)

                pe.wait_ge(w_in, 64)
                for u in range(T // 2):
                    if u % (TP // 2) == 0 and u:
                        gate(u - 1, (u - 1) % 2)
                        rank(u // (TP // 2) - 1)
                    turn(u, u % 2)
                    if u % (TP // 2):
                        gate(u - 1, (u - 1) % 2)
                gate(T // 2 - 1, (T // 2 - 1) % 2)
                rank(PHASES - 1)
                pe.wait_ge(ecol_ready, 1)
                for k in range(2):
                    mm = pe.matmul(p_e[0:1, k * P:(k + 1) * P], ecol[:, k:k + 1], ident[:], start=True, stop=True)
                mm.then_inc(erow_in_psum, 1)

            @block.gpsimd
            def _(pool):
                pool.affine_select(out=tri[:], in_=ones[:], compare_op=ALU.is_ge, fill=0.0, base=-1,
                                   pattern=[[1, P]], channel_multiplier=-1).then_inc(tri_ready, 1)
                def bias(ph):
                    for g in range(ph * GROUPS, (ph + 1) * GROUPS):
                        a = acc[:, g * GT:(g + 1) * GT, 0:D]
                        pool.wait_ge(scaled, g + 1)
                        pool.tensor_tensor(a, a, b_gnn[:].unsqueeze(1).broadcast_to([P, GT, D]), ALU.add).then_inc(biased, 1)

                for ph in range(AHEAD):
                    bias(ph)
                for ph in range(PHASES):
                    if ph + AHEAD < PHASES:
                        bias(ph + AHEAD)
                    pool.wait_ge(places_ready, ph + 1)
                    for t in range(ph * TP, min((ph + 1) * TP, BLOCKS)):
                        n = P if t < NFULL else NREST
                        for k in range(2):
                            pool.indirect_dma_start(slot_x, bass.IndirectOffsetOnAxis(ap=places[0:n, k, t:t + 1], axis=0),
                                                    xl[0:n, t, :], None).then_inc(sent, 16)
                pool.wait_ge(sent, 2 * BLOCKS * 16)

        with ExitStack() as c:
            KF = FF // P
            HALVES = SLOT_ROWS // P
            wa = [sb(f"wa{i}", [P, 2, FF], ctx=c) for i in range(WR)]
            wb = [sb(f"wb{i}", [P, KF, D], ctx=c) for i in range(WR)]
            ba = [sb(f"ba{i}", [P, KF], ctx=c) for i in range(WR)]
            bb = [sb(f"bb{i}", [P, D], ctx=c) for i in range(WR)]
            xs = [sb(f"xs{i}", [P, HALVES, D], ctx=c) for i in range(WR)]
            xst = [sb(f"xst{i}", [P, 2, SLOT_ROWS], ctx=c) for i in range(2)]
            ht = [sb(f"ht{i}", [P, KF, SLOT_ROWS], ctx=c) for i in range(2)]
            ysb = [sb(f"ysb{i}", [P, HALVES, D], ctx=c) for i in range(2)]
            p_x = ps("e_px", [P, 2 * SLOT_ROWS], c)
            p_h = [ps(f"e_ph{i}", [P, KF * SLOT_ROWS], c) for i in range(2)]
            p_y = [ps(f"e_py{i}", [P, HALVES * D], c) for i in range(2)]
            x_in = [sem(f"e_x_in{i}", c) for i in range(WR)]
            w_in = [sem(f"e_w_in{i}", c) for i in range(WR)]
            x_turned = sem("e_x_turned", c)
            xt_ready = sem("e_xt_ready", c)
            hidden = sem("hidden", c)
            ht_ready = sem("ht_ready", c)
            y_in_psum = sem("y_in_psum", c)
            y_ready = sem("y_ready", c)
            y_out = [sem(f"y_out{i}", c) for i in range(2)]
            block = c.enter_context(nc.Block())
            w1v = w1.rearrange("e (c k) f -> k e c f", k=P)
            w2v = w2.rearrange("e (c k) f -> k e c f", k=P)

            @block.sync
            def _(sp):
                def body(t, s):
                    e = sp.value_load(exp_row[0:1, bass.ds(t, 1)], min_val=0, max_val=NEXP - 1)
                    q = sp.value_load(tile_row[0:1, bass.ds(t, 1)], min_val=0, max_val=SPARE)
                    wait(sp, x_turned, t - WR + 1)
                    sp.dma_start(xs[s][:], slot_x[bass.ts(q, SLOT_ROWS), :].rearrange("(p a) f -> p a f", a=HALVES)).then_inc(x_in[s], 16)
                    wait(sp, y_ready, t - WR + 1)
                    sp.dma_start(wa[s][:], w1v[:, bass.ds(e, 1), :, :].rearrange("k a c f -> k (a c) f")).then_inc(w_in[s], 16)
                    sp.dma_start(ba[s][:], b1_cols[bass.ds(e, 1), :, :].rearrange("a p c -> p (a c)")).then_inc(w_in[s], 16)
                    sp.dma_start(wb[s][:], w2v[:, bass.ds(e, 1), :, :].rearrange("k a c f -> k (a c) f")).then_inc(w_in[s], 16)
                    sp.dma_start(bb[s][:], b2[bass.ds(e, 1), :].broadcast_to([P, D])).then_inc(w_in[s], 16)
                ring(sp, SLOT_TILES, WR, body)

            def w_loaded(t, s):
                return (t - s) * (64 // WR) + 64

            @block.tensor
            def _(pe):
                def turn(t, s):
                    pe.wait_ge(x_in[s], (t - s) * (16 // WR) + 16)
                    wait(pe, xt_ready, t)
                    for k in range(2):
                        for a in range(HALVES):
                            mm = pe.transpose(p_x[:, k * SLOT_ROWS + a * P:k * SLOT_ROWS + (a + 1) * P],
                                              xs[s][:, a, k * P:(k + 1) * P], ident[:])
                    mm.then_inc(x_turned, 1)

                def first(t, s):
                    pe.wait_ge(w_in[s], w_loaded(t, s))
                    pe.wait_ge(xt_ready, t + 1)
                    wait(pe, ht_ready, t - 1)
                    for m in range(KF):
                        for k in range(2):
                            mm = pe.matmul(p_h[s % 2][:, m * SLOT_ROWS:(m + 1) * SLOT_ROWS], wa[s][:, k, m * P:(m + 1) * P], xst[s % 2][:, k, :],
                                           start=(k == 0), stop=(k == 1))
                    mm.then_inc(hidden, 1)

                def second(t, s):
                    pe.wait_ge(ht_ready, t + 1)
                    wait(pe, y_ready, t - 1)
                    for a in range(HALVES):
                        for k in range(KF):
                            mm = pe.matmul(p_y[s % 2][:, a * D:(a + 1) * D], ht[s % 2][:, k, a * P:(a + 1) * P], wb[s][:, k, :],
                                           start=(k == 0), stop=(k == KF - 1))
                    mm.then_inc(y_in_psum, 1)

                def body(t, s):
                    first(t, s)
                    if not (isinstance(t, int) and t == SLOT_TILES - 1):
                        turn(t + 1, (s + 1) % WR)
                    if not (isinstance(t, int) and t == 0):
                        second(t - 1, (s - 1) % WR)
                turn(0, 0)
                ring_peeled(pe, SLOT_TILES, WR, body)
                second(SLOT_TILES - 1, (SLOT_TILES - 1) % WR)

            @block.scalar
            def _(act):
                def body(t, s):
                    act.wait_ge(hidden, t + 1)
                    act.wait_ge(w_in[s], w_loaded(t, s))
                    wait(act, y_in_psum, t - 1)
                    for m in range(KF):
                        a = act.activation(ht[s % 2][:, m, :], p_h[s % 2][:, m * SLOT_ROWS:(m + 1) * SLOT_ROWS], ACT.Relu, bias=ba[s][:, m:m + 1])
                    a.then_inc(ht_ready, 1)
                ring(act, SLOT_TILES, WR, body)

            @block.vector
            def _(dve):
                def turned(t, s):
                    dve.wait_ge(x_turned, t + 1)
                    wait(dve, hidden, t - 1)
                    dve.tensor_copy(xst[s % 2][:].rearrange("p k r -> p (k r)"), p_x[:]).then_inc(xt_ready, 1)

                def body(t, s):
                    if not (isinstance(t, int) and t >= SLOT_TILES - 2):
                        turned(t + 2, (s + 2) % WR)
                    dve.wait_ge(y_in_psum, t + 1)
                    dve.wait_ge(w_in[s], w_loaded(t, s))
                    wait(dve, y_out[s % 2], (t - s % 2) * 8)
                    dve.tensor_tensor(ysb[s % 2][:], p_y[s % 2][:].rearrange("p (a f) -> p a f", a=HALVES),
                                      bb[s][:].unsqueeze(1).broadcast_to([P, HALVES, D]), ALU.add).then_inc(y_ready, 1)
                turned(0, 0)
                turned(1, 1)
                ring_peeled(dve, SLOT_TILES, WR, body)

            @block.gpsimd
            def _(pool):
                def body(t, s):
                    pool.wait_ge(y_ready, t + 1)
                    pool.dma_start(slot_y[bass.ts(t, SLOT_ROWS), :].rearrange("(p a) f -> p a f", a=HALVES), ysb[s][:]).then_inc(y_out[s], 16)
                pairs(pool, SLOT_TILES, body)
                for s in range(2):
                    pool.wait_ge(y_out[s], SLOT_TILES // 2 * 16)

        with ExitStack() as c:
            ya = [sb(f"ya{i}", [P, 2, D], ctx=c) for i in range(YR)]
            y_in = [sem(f"f_y_in{i}", c) for i in range(YR)]
            st = sb("f_st", [P, T, 6], ctx=c)
            ag = sb("f_ag", [P, T, 2], ctx=c)
            rs = sb("f_rs", [P, T], ctx=c)
            ready = sem("f_ready", c)
            ya_used = sem("ya_used", c)
            var_ready = sem("f_var_ready", c)
            std_ready = sem("f_std_ready", c)
            stored = sem("stored", c)
            block = c.enter_context(nc.Block())

            def rows(t):
                return P if t < NFULL else NREST

            groups = [list(range(t, min(t + 2, BLOCKS))) for t in range(0, BLOCKS, 2)]

            @block.gpsimd
            def _(pool):
                for t in range(BLOCKS):
                    wait(pool, ya_used, t - YR + 1)
                    for k in range(2):
                        pool.indirect_dma_start(ya[t % YR][0:rows(t), k, :], None, slot_y,
                                                bass.IndirectOffsetOnAxis(ap=y_places[0:rows(t), k, t:t + 1], axis=0)).then_inc(y_in[t % YR], 16)

            @block.scalar
            def _(act):
                for i, g in enumerate(groups):
                    act.wait_ge(var_ready, i + 1)
                    act.sqrt(rs[:, g[0]:g[-1] + 1], rs[:, g[0]:g[-1] + 1]).then_inc(std_ready, 1)

            @block.vector
            def _(dve):
                dve.memset(ag[:], 0.0)
                dve.drain()

                def step(i, new, old):
                    if old:
                        dve.wait_ge(std_ready, i)
                        dve.reciprocal(rs[:, old[0]:old[-1] + 1], rs[:, old[0]:old[-1] + 1])
                    for k in range(2):
                        for t in new:
                            n = rows(t)
                            if k == 0:
                                dve.wait_ge(y_in[t % YR], (t // YR + 1) * 32)
                            y = xl[0:n, t, :]
                            a = dve.scalar_tensor_tensor(out=y, in0=ya[t % YR][0:n, k, :], scalar=top_w[0:n, t, k:k + 1], in1=y,
                                                         op0=ALU.mult, op1=ALU.add)
                            if k:
                                a.then_inc(ya_used, 1)
                        if k == 0:
                            for t in old:
                                n = rows(t)
                                dve.scalar_tensor_tensor(out=xl[0:n, t, :], in0=xl[0:n, t, :], scalar=ag[0:n, t, 0:1], in1=g_b[0:n],
                                                         op0=ALU.subtract, op1=ALU.mult)
                        dve.drain()
                    for t in new:
                        dve.bn_stats(st[0:rows(t), t, :], xl[0:rows(t), t, :])
                    for t in old:
                        n = rows(t)
                        dve.scalar_tensor_tensor(out=xl[0:n, t, :], in0=xl[0:n, t, :], scalar=rs[0:n, t:t + 1], in1=resid[0:n, t, :],
                                                 op0=ALU.mult, op1=ALU.add).then_inc(ready, 1)
                    if new:
                        dve.drain()
                        for t in new:
                            dve.bn_aggr(ag[0:rows(t), t, :], st[0:rows(t), t, :])
                        dve.drain()
                        dve.tensor_scalar(rs[:, new[0]:new[-1] + 1], ag[:, new[0]:new[-1] + 1, 1], LN_EPS, None, ALU.add).then_inc(var_ready, 1)

                for i, g in enumerate(groups):
                    step(i, g, groups[i - 1] if i else [])
                step(len(groups), [], groups[-1])

            @block.sync
            def _(sp):
                for t in range(BLOCKS):
                    n = P if t < NFULL else NREST
                    sp.wait_ge(ready, t + 1)
                    sp.dma_start(out[t * P:t * P + n, :], xl[0:n, t, :]).then_inc(stored, 16)
                sp.wait_ge(stored, BLOCKS * 16)
        late.close()


_INS = ['x', 'src', 'dst', 'L0_gnn_W', 'L0_gnn_att_src', 'L0_gnn_att_dst', 'L0_gnn_bias', 'L0_mix_Wqkv',
        'L0_mix_bqkv', 'L0_mix_Wproj', 'L0_mix_bproj', 'L0_mix_temperature', 'L0_ffn_gate_w', 'L0_ffn_gate_b',
        'L0_ffn_w1', 'L0_ffn_b1', 'L0_ffn_w2', 'L0_ffn_b2', 'L0_ffn_gamma', 'L0_ffn_beta']
_OUTS = [((N, D), 'float32')]


def kernel(**inputs):
    import numpy as _np
    import concourse.bacc as _bacc
    from concourse import mybir as _mybir
    from concourse.bass_utils import run_bass_kernel_spmd as _run

    nc = _bacc.Bacc("TRN2", target_bir_lowering=False, num_devices=1)
    arrays, args = {}, []
    for name in _INS:
        a = _np.ascontiguousarray(inputs[name])
        arrays[f"in_{name}_dram"] = a
        args.append(nc.dram_tensor(f"in_{name}_dram", a.shape, _mybir.dt.from_np(a.dtype), kind="ExternalInput").ap())
    for i, (shape, dtype) in enumerate(_OUTS):
        args.append(nc.dram_tensor(f"out_{i}_dram", shape, _mybir.dt.from_np(_np.dtype(dtype)), kind="ExternalOutput").ap())
    gps_layer(nc, *args)
    r = _run(nc, [arrays], core_ids=[0])
    return r.results[0]["out_0_dram"]
```
